# Optimizing a Trainium2 kernel written in Bass

```python
import numpy as np
import jax
import jax.numpy as jnp

def _softmax(x, axis=-1):
    return jax.nn.softmax(x, axis=axis)

def _gelu(x):
    return jax.nn.gelu(x, approximate=True)

def _silu(x):
    return jax.nn.silu(x)

def _sigmoid(x):
    return jax.nn.sigmoid(x)

def _layernorm(x, axis=-1, eps=1e-05):
    m = jnp.mean(x, axis=axis, keepdims=True)
    v = jnp.var(x, axis=axis, keepdims=True)
    return (x - m) / jnp.sqrt(v + eps)

def _scatter_add(tgt, idx, src, axis=0):
    return tgt.at[idx].add(src)

def _segment_sum(src, seg, n):
    return jax.ops.segment_sum(src, seg, n)
kernel_name = 'mk_flamingo_gated_d4_seqx_r8_2fc57e'

def setup_inputs(seed: int=0):
    np.random.seed(seed)
    _w = jnp.asarray

    def _rec_inputs():
        import jax
        import jax.numpy as jnp
        _rk = jax.random.key(seed)
        x = -0.0002928 + 1 * jax.random.normal(jax.random.fold_in(_rk, 1), (4, 512, 128), jnp.float32)
        _lenS = 512 - jax.random.randint(jax.random.fold_in(_rk, 7), (4,), 0, max(1, 512 // 4) + 1, jnp.int32)
        _lenS2 = 154 - jax.random.randint(jax.random.fold_in(_rk, 8), (4,), 0, max(1, 154 // 4) + 1, jnp.int32)
        _ctx_1024P = jax.random.normal(jax.random.fold_in(_rk, 11), (4, 16, 128), jnp.float32)
        _ctx_1024c = jax.random.dirichlet(jax.random.fold_in(_rk, 511), 0.3 * jnp.ones((16,), jnp.float32), (4, 154))
        _ctx_1024t = jnp.einsum('bsk,bkd->bsd', _ctx_1024c, _ctx_1024P)
        _ctx_1024t = _ctx_1024t * jax.lax.rsqrt(jnp.mean(jnp.square(_ctx_1024t)) + 1e-12) * 0.953939
        ctx_1024 = -1.39393e-06 + 0.999914 * (_ctx_1024t + 0.3 * jax.random.normal(jax.random.fold_in(_rk, 611), (4, 154, 128), jnp.float32))
        fside_Bx16xSxS2_0 = -6.00028e-06 + 0.100001 * jax.random.normal(jax.random.fold_in(_rk, 12), (4, 16, 512, 154), jnp.float32)
        _validS = jnp.arange(512)[None, :] < _lenS[:, None]
        _validS2 = jnp.arange(154)[None, :] < _lenS2[:, None]
        _causal = jnp.tril(jnp.ones((512, 512), dtype=bool))
        mask_1x1xSxS2_ik0 = jnp.where(jnp.broadcast_to(_validS2[0:1, None, None, :], (1, 1, 512, 154)), 0, 1).astype(jnp.int32)
        _g = jax.random.normal(jax.random.fold_in(_rk, 9001), (2, 4), jnp.float32)
        _g = jnp.sign(_g) * jnp.maximum(jnp.abs(_g), 1.0) + (_g == 0) * 1.0
        g_xattn = _g[0]
        g_ffn = _g[1]
        return (x, ctx_1024, fside_Bx16xSxS2_0, mask_1x1xSxS2_ik0, g_xattn, g_ffn)
    x, ctx_1024, fside_Bx16xSxS2_0, mask_1x1xSxS2_ik0, g_xattn, g_ffn = _rec_inputs()

    def _L0_xattn_setup():
        import jax, jax.numpy as jnp
        import numpy as np
        import math
        H = 16
        D = 128
        FF = 512
        DK = D // H
        EPS = 1e-05

        def layer_norm(x, g, b):
            mu = jnp.mean(x, axis=-1, keepdims=True)
            var = jnp.var(x, axis=-1, keepdims=True)
            return (x - mu) * jax.lax.rsqrt(var + EPS) * g + b
        key = jax.random.key(seed)
        ks = jax.random.split(key, 16)
        B, S = (2, 256)
        s = 1.0 / math.sqrt(D)
        return {'x_q': jax.random.normal(ks[0], (B, S, D), jnp.float32), 'x_kv': jax.random.normal(ks[1], (B, S, D), jnp.float32), 'bias': jax.random.normal(ks[2], (B, H, S, S), jnp.float32) * 0.1, 'Wq': jax.random.normal(ks[3], (D, D), jnp.float32) * s, 'Wk': jax.random.normal(ks[4], (D, D), jnp.float32) * s, 'Wv': jax.random.normal(ks[5], (D, D), jnp.float32) * s, 'Wo': jax.random.normal(ks[6], (D, D), jnp.float32) * s, 'W1': jax.random.normal(ks[7], (FF, D), jnp.float32) * s, 'b1': jnp.zeros((FF,), jnp.float32), 'W2': jax.random.normal(ks[8], (D, FF), jnp.float32) * (1.0 / math.sqrt(FF)), 'b2': jnp.zeros((D,), jnp.float32), 'g1': jnp.ones((D,), jnp.float32), 'be1': jnp.zeros((D,), jnp.float32), 'g2': jnp.ones((D,), jnp.float32), 'be2': jnp.zeros((D,), jnp.float32)}
    _L0_xattn_all = _L0_xattn_setup()
    _L0_xattn_in = {k: v for k, v in _L0_xattn_all.items() if k in ('Wq', 'Wk', 'Wv', 'Wo', 'W1', 'b1', 'W2', 'b2', 'g1', 'be1', 'g2', 'be2')}
    del _L0_xattn_all

    def _L0_ffn_setup():
        import math
        import jax, jax.numpy as jnp
        import numpy as np
        TOP_K = 2
        CAP_FACTOR = 1.25
        CLAMP = 10000.0
        key = jax.random.key(seed)
        k1, k2, k3, k4, k5 = jax.random.split(key, 5)
        B, S, D, F, E = (4, 256, 128, 512, 8)
        std = 0.02
        return {'x': jax.random.normal(k1, (B, S, D), dtype=jnp.float32), 'Wr': jax.random.normal(k2, (D, E), dtype=jnp.float32) * std, 'W1': jax.random.normal(k3, (E, D, F), dtype=jnp.float32) * std, 'W3': jax.random.normal(k4, (E, D, F), dtype=jnp.float32) * std, 'W2': jax.random.normal(k5, (E, F, D), dtype=jnp.float32) * std}
    _L0_ffn_all = _L0_ffn_setup()
    _L0_ffn_in = {k: v for k, v in _L0_ffn_all.items() if k in ('Wr', 'W1', 'W3', 'W2')}
    del _L0_ffn_all

    def _L1_xattn_setup():
        import jax, jax.numpy as jnp
        import numpy as np
        B, S, D, H, DK, DV = (4, 256, 128, 16, 64, 64)
        key = jax.random.key(seed)
        ks = jax.random.split(key, 7)
        scale = 0.02
        queries = jax.random.normal(ks[0], (B, S, D), jnp.float32)
        keys_ = jax.random.normal(ks[1], (B, S, D), jnp.float32)
        values = jax.random.normal(ks[2], (B, S, D), jnp.float32)
        mask = jnp.tril(jnp.ones((S, S), jnp.int32))[None, None, :, :]
        W_Q = jax.random.normal(ks[3], (D, H * DK), jnp.float32) * scale
        W_K = jax.random.normal(ks[4], (D, H * DK), jnp.float32) * scale
        W_V = jax.random.normal(ks[5], (D, H * DV), jnp.float32) * scale
        W_O = jax.random.normal(ks[6], (H * DV, D), jnp.float32) * scale
        return {'queries': queries, 'keys': keys_, 'values': values, 'mask': mask, 'W_Q': W_Q, 'W_K': W_K, 'W_V': W_V, 'W_O': W_O}
    _L1_xattn_all = _L1_xattn_setup()
    _L1_xattn_in = {k: v for k, v in _L1_xattn_all.items() if k in ('W_Q', 'W_K', 'W_V', 'W_O')}
    del _L1_xattn_all

    def _L1_ffn_setup():
        import jax, jax.numpy as jnp
        import numpy as np
        DIM = 128
        EXPERT_DIM = 64
        N_EXPERTS = 16
        TOPK = 2
        SHARED_HIDDEN = EXPERT_DIM * TOPK
        B, T = (4, 128)

        def _moe_forward(x, router_w, router_bias, up_proj, gate_proj, down_proj, sh_gate, sh_up, sh_down):
            Bb, Tt, D = x.shape
            flat = x.reshape(Bb * Tt, D)
            N = flat.shape[0]
            logits = flat @ router_w.T
            topk_scores, topk_idx = jax.lax.top_k(logits + router_bias, TOPK)
            topk_scores = jax.nn.softmax(topk_scores, axis=-1)
            combine = jnp.zeros((N, N_EXPERTS), flat.dtype)
            combine = combine.at[jnp.arange(N)[:, None], topk_idx].add(topk_scores)
            up_all = jnp.einsum('nd,kde->nke', flat, up_proj)
            gate_all = jnp.einsum('nd,kde->nke', flat, gate_proj)
            hidden = jax.nn.silu(gate_all) * up_all
            down_all = jnp.einsum('nke,ked->nkd', hidden, down_proj)
            out = jnp.einsum('nk,nkd->nd', combine, down_all)
            sh_hidden = jax.nn.silu(flat @ sh_gate.T) * (flat @ sh_up.T)
            out = out + sh_hidden @ sh_down.T
            return out.reshape(Bb, Tt, D)
        key = jax.random.key(seed)
        ks = jax.random.split(key, 9)
        std = 0.02
        return {'x': jax.random.normal(ks[0], (B, T, DIM), jnp.float32), 'router_w': jax.random.normal(ks[1], (N_EXPERTS, DIM), jnp.float32) * std, 'router_bias': jnp.zeros((N_EXPERTS,), jnp.float32), 'up_proj': jax.random.normal(ks[2], (N_EXPERTS, DIM, EXPERT_DIM), jnp.float32) * std, 'gate_proj': jax.random.normal(ks[3], (N_EXPERTS, DIM, EXPERT_DIM), jnp.float32) * std, 'down_proj': jax.random.normal(ks[4], (N_EXPERTS, EXPERT_DIM, DIM), jnp.float32) * std, 'sh_gate': jax.random.normal(ks[5], (SHARED_HIDDEN, DIM), jnp.float32) * std, 'sh_up': jax.random.normal(ks[6], (SHARED_HIDDEN, DIM), jnp.float32) * std, 'sh_down': jax.random.normal(ks[7], (DIM, SHARED_HIDDEN), jnp.float32) * std}
    _L1_ffn_all = _L1_ffn_setup()
    _L1_ffn_in = {k: v for k, v in _L1_ffn_all.items() if k in ('router_w', 'router_bias', 'up_proj', 'gate_proj', 'down_proj', 'sh_gate', 'sh_up', 'sh_down')}
    del _L1_ffn_all

    def _L2_xattn_setup():
        import jax, jax.numpy as jnp
        import numpy as np
        B, S, D, H = (4, 256, 128, 16)
        DEPTH = D // H
        NEG = 10000000000.0

        def _split_heads(x):
            b, s, _ = x.shape
            return x.reshape(b, s, H, DEPTH).transpose(0, 2, 1, 3)
        key = jax.random.key(seed)
        ks = jax.random.split(key, 11)
        sc = 0.02
        return {'q': jax.random.normal(ks[0], (B, S, D), jnp.float32), 'v': jax.random.normal(ks[1], (B, S, D), jnp.float32), 'k': jax.random.normal(ks[2], (B, S, D), jnp.float32), 'Wq': jax.random.normal(ks[3], (D, D), jnp.float32) * sc, 'bq': jnp.zeros((D,), jnp.float32), 'Wk': jax.random.normal(ks[4], (D, D), jnp.float32) * sc, 'bk': jnp.zeros((D,), jnp.float32), 'Wv': jax.random.normal(ks[5], (D, D), jnp.float32) * sc, 'bv': jnp.zeros((D,), jnp.float32), 'Wo': jax.random.normal(ks[6], (D, D), jnp.float32) * sc, 'bo': jnp.zeros((D,), jnp.float32), 'mask': 1}
    _L2_xattn_all = _L2_xattn_setup()
    _L2_xattn_in = {k: v for k, v in _L2_xattn_all.items() if k in ('Wq', 'bq', 'Wk', 'bk', 'Wv', 'bv', 'Wo', 'bo')}
    del _L2_xattn_all

    def _L2_ffn_setup():
        import jax, jax.numpy as jnp
        import numpy as np
        TOP_K = 2
        key = jax.random.key(seed)
        k1, k2, k3, k4 = jax.random.split(key, 4)
        B, S, D, F, E = (2, 256, 128, 512, 8)
        hidden_states = jax.random.normal(k1, (B, S, D), dtype=jnp.float32)
        Wr = jax.random.normal(k2, (E, D), dtype=jnp.float32) * (1.0 / np.sqrt(D))
        W1 = jax.random.normal(k3, (E, D, F), dtype=jnp.float32) * (1.0 / np.sqrt(D))
        W2 = jax.random.normal(k4, (E, F, D), dtype=jnp.float32) * (1.0 / np.sqrt(F))
        return {'hidden_states': hidden_states, 'Wr': Wr, 'W1': W1, 'W2': W2}
    _L2_ffn_all = _L2_ffn_setup()
    _L2_ffn_in = {k: v for k, v in _L2_ffn_all.items() if k in ('Wr', 'W1', 'W2')}
    del _L2_ffn_all

    def _L3_xattn_setup():
        import jax, jax.numpy as jnp
        import numpy as np
        D_MODEL = 128
        B, S = (4, 256)
        key = jax.random.key(seed)
        ks = jax.random.split(key, 10)
        s = 1.0 / np.sqrt(D_MODEL)
        return {'k': jax.random.normal(ks[0], (B, S, D_MODEL), jnp.float32), 'v': jax.random.normal(ks[1], (B, S, D_MODEL), jnp.float32), 'q': jax.random.normal(ks[2], (B, S, D_MODEL), jnp.float32), 'Wk': jax.random.normal(ks[3], (D_MODEL, D_MODEL), jnp.float32) * s, 'Wv': jax.random.normal(ks[4], (D_MODEL, D_MODEL), jnp.float32) * s, 'bv': jnp.zeros((D_MODEL,), jnp.float32), 'Wq': jax.random.normal(ks[5], (D_MODEL, D_MODEL), jnp.float32) * s, 'bq': jnp.zeros((D_MODEL,), jnp.float32), 'Wo': jax.random.normal(ks[6], (D_MODEL, D_MODEL), jnp.float32) * s, 'bo': jnp.zeros((D_MODEL,), jnp.float32)}
    _L3_xattn_all = _L3_xattn_setup()
    _L3_xattn_in = {k: v for k, v in _L3_xattn_all.items() if k in ('Wk', 'Wv', 'bv', 'Wq', 'bq', 'Wo', 'bo')}
    del _L3_xattn_all

    def _L3_ffn_setup():
        import math
        import jax, jax.numpy as jnp
        import numpy as np
        B, S, D, H, E, F = (2, 128, 128, 16, 16, 512)
        HEAD = D // H
        MOE_TOKEN_DROPOUT = 0.2
        EPS = 1e-05

        def layer_norm(x, w, b):
            mu = x.mean(-1, keepdims=True)
            var = ((x - mu) ** 2).mean(-1, keepdims=True)
            return (x - mu) * jax.lax.rsqrt(var + EPS) * w + b
        key = jax.random.key(seed)
        ks = jax.random.split(key, 16)
        w = lambda k, shape: jax.random.normal(k, shape, jnp.float32) * 0.02
        return {'hidden_states': jax.random.normal(ks[0], (B, S, D), jnp.float32), 'ln1_w': jnp.ones((D,), jnp.float32), 'ln1_b': jnp.zeros((D,), jnp.float32), 'q_w': w(ks[1], (D, D)), 'q_b': jnp.zeros((D,), jnp.float32), 'k_w': w(ks[2], (D, D)), 'k_b': jnp.zeros((D,), jnp.float32), 'v_w': w(ks[3], (D, D)), 'v_b': jnp.zeros((D,), jnp.float32), 'o_w': w(ks[4], (D, D)), 'o_b': jnp.zeros((D,), jnp.float32), 'ln2_w': jnp.ones((D,), jnp.float32), 'ln2_b': jnp.zeros((D,), jnp.float32), 'router_w': w(ks[5], (D, E)), 'fc1_w': w(ks[6], (E, D, F)), 'fc1_b': jnp.zeros((E, F), jnp.float32), 'fc2_w': w(ks[7], (E, F, D)), 'fc2_b': jnp.zeros((E, D), jnp.float32)}
    _L3_ffn_all = _L3_ffn_setup()
    _L3_ffn_in = {k: v for k, v in _L3_ffn_all.items() if k in ('ln1_w', 'ln1_b', 'q_w', 'q_b', 'k_w', 'k_b', 'v_w', 'v_b', 'o_w', 'o_b', 'ln2_w', 'ln2_b', 'router_w', 'fc1_w', 'fc1_b', 'fc2_w', 'fc2_b')}
    del _L3_ffn_all
    return {'x': x, 'ctx_1024': ctx_1024, 'fside_Bx16xSxS2_0': fside_Bx16xSxS2_0, 'mask_1x1xSxS2_ik0': mask_1x1xSxS2_ik0, 'g_xattn': g_xattn, 'g_ffn': g_ffn, 'L0_xattn_Wq': _L0_xattn_in['Wq'], 'L0_xattn_Wk': _L0_xattn_in['Wk'], 'L0_xattn_Wv': _L0_xattn_in['Wv'], 'L0_xattn_Wo': _L0_xattn_in['Wo'], 'L0_xattn_W1': _L0_xattn_in['W1'], 'L0_xattn_b1': _L0_xattn_in['b1'], 'L0_xattn_W2': _L0_xattn_in['W2'], 'L0_xattn_b2': _L0_xattn_in['b2'], 'L0_xattn_g1': _L0_xattn_in['g1'], 'L0_xattn_be1': _L0_xattn_in['be1'], 'L0_xattn_g2': _L0_xattn_in['g2'], 'L0_xattn_be2': _L0_xattn_in['be2'], 'L0_ffn_Wr': _L0_ffn_in['Wr'], 'L0_ffn_W1': _L0_ffn_in['W1'], 'L0_ffn_W3': _L0_ffn_in['W3'], 'L0_ffn_W2': _L0_ffn_in['W2'], 'L1_xattn_W_Q': _L1_xattn_in['W_Q'], 'L1_xattn_W_K': _L1_xattn_in['W_K'], 'L1_xattn_W_V': _L1_xattn_in['W_V'], 'L1_xattn_W_O': _L1_xattn_in['W_O'], 'L1_ffn_router_w': _L1_ffn_in['router_w'], 'L1_ffn_router_bias': _L1_ffn_in['router_bias'], 'L1_ffn_up_proj': _L1_ffn_in['up_proj'], 'L1_ffn_gate_proj': _L1_ffn_in['gate_proj'], 'L1_ffn_down_proj': _L1_ffn_in['down_proj'], 'L1_ffn_sh_gate': _L1_ffn_in['sh_gate'], 'L1_ffn_sh_up': _L1_ffn_in['sh_up'], 'L1_ffn_sh_down': _L1_ffn_in['sh_down'], 'L2_xattn_Wq': _L2_xattn_in['Wq'], 'L2_xattn_bq': _L2_xattn_in['bq'], 'L2_xattn_Wk': _L2_xattn_in['Wk'], 'L2_xattn_bk': _L2_xattn_in['bk'], 'L2_xattn_Wv': _L2_xattn_in['Wv'], 'L2_xattn_bv': _L2_xattn_in['bv'], 'L2_xattn_Wo': _L2_xattn_in['Wo'], 'L2_xattn_bo': _L2_xattn_in['bo'], 'L2_ffn_Wr': _L2_ffn_in['Wr'], 'L2_ffn_W1': _L2_ffn_in['W1'], 'L2_ffn_W2': _L2_ffn_in['W2'], 'L3_xattn_Wk': _L3_xattn_in['Wk'], 'L3_xattn_Wv': _L3_xattn_in['Wv'], 'L3_xattn_bv': _L3_xattn_in['bv'], 'L3_xattn_Wq': _L3_xattn_in['Wq'], 'L3_xattn_bq': _L3_xattn_in['bq'], 'L3_xattn_Wo': _L3_xattn_in['Wo'], 'L3_xattn_bo': _L3_xattn_in['bo'], 'L3_ffn_ln1_w': _L3_ffn_in['ln1_w'], 'L3_ffn_ln1_b': _L3_ffn_in['ln1_b'], 'L3_ffn_q_w': _L3_ffn_in['q_w'], 'L3_ffn_q_b': _L3_ffn_in['q_b'], 'L3_ffn_k_w': _L3_ffn_in['k_w'], 'L3_ffn_k_b': _L3_ffn_in['k_b'], 'L3_ffn_v_w': _L3_ffn_in['v_w'], 'L3_ffn_v_b': _L3_ffn_in['v_b'], 'L3_ffn_o_w': _L3_ffn_in['o_w'], 'L3_ffn_o_b': _L3_ffn_in['o_b'], 'L3_ffn_ln2_w': _L3_ffn_in['ln2_w'], 'L3_ffn_ln2_b': _L3_ffn_in['ln2_b'], 'L3_ffn_router_w': _L3_ffn_in['router_w'], 'L3_ffn_fc1_w': _L3_ffn_in['fc1_w'], 'L3_ffn_fc1_b': _L3_ffn_in['fc1_b'], 'L3_ffn_fc2_w': _L3_ffn_in['fc2_w'], 'L3_ffn_fc2_b': _L3_ffn_in['fc2_b']}

def reference(x, ctx_1024, fside_Bx16xSxS2_0, mask_1x1xSxS2_ik0, g_xattn, g_ffn, L0_xattn_Wq, L0_xattn_Wk, L0_xattn_Wv, L0_xattn_Wo, L0_xattn_W1, L0_xattn_b1, L0_xattn_W2, L0_xattn_b2, L0_xattn_g1, L0_xattn_be1, L0_xattn_g2, L0_xattn_be2, L0_ffn_Wr, L0_ffn_W1, L0_ffn_W3, L0_ffn_W2, L1_xattn_W_Q, L1_xattn_W_K, L1_xattn_W_V, L1_xattn_W_O, L1_ffn_router_w, L1_ffn_router_bias, L1_ffn_up_proj, L1_ffn_gate_proj, L1_ffn_down_proj, L1_ffn_sh_gate, L1_ffn_sh_up, L1_ffn_sh_down, L2_xattn_Wq, L2_xattn_bq, L2_xattn_Wk, L2_xattn_bk, L2_xattn_Wv, L2_xattn_bv, L2_xattn_Wo, L2_xattn_bo, L2_ffn_Wr, L2_ffn_W1, L2_ffn_W2, L3_xattn_Wk, L3_xattn_Wv, L3_xattn_bv, L3_xattn_Wq, L3_xattn_bq, L3_xattn_Wo, L3_xattn_bo, L3_ffn_ln1_w, L3_ffn_ln1_b, L3_ffn_q_w, L3_ffn_q_b, L3_ffn_k_w, L3_ffn_k_b, L3_ffn_v_w, L3_ffn_v_b, L3_ffn_o_w, L3_ffn_o_b, L3_ffn_ln2_w, L3_ffn_ln2_b, L3_ffn_router_w, L3_ffn_fc1_w, L3_ffn_fc1_b, L3_ffn_fc2_w, L3_ffn_fc2_b):
    import jax
    import jax.numpy as jnp

    def _L0_xattn_ref(x_q, x_kv, bias, Wq, Wk, Wv, Wo, W1, b1, W2, b2, g1, be1, g2, be2):
        import jax, jax.numpy as jnp
        import numpy as np
        import math
        H = 16
        D = 128
        FF = 512
        DK = D // H
        EPS = 1e-05

        def layer_norm(x, g, b):
            mu = jnp.mean(x, axis=-1, keepdims=True)
            var = jnp.var(x, axis=-1, keepdims=True)
            return (x - mu) * jax.lax.rsqrt(var + EPS) * g + b
        B, S, _ = x_q.shape

        def split(x):
            return x.reshape(B, -1, H, DK).transpose(0, 2, 1, 3)
        q = split(x_q @ Wq.T)
        k = split(x_kv @ Wk.T)
        v = split(x_kv @ Wv.T)
        scores = jnp.einsum('bhqd,bhkd->bhqk', q, k) / math.sqrt(DK) + bias
        p = jax.nn.softmax(scores, axis=-1)
        o = jnp.einsum('bhqk,bhkd->bhqd', p, v)
        o = o.transpose(0, 2, 1, 3).reshape(B, S, D)
        x = x_q + o @ Wo.T
        h = jax.nn.gelu(layer_norm(x, g1, be1) @ W1.T + b1, approximate=False)
        x = x + h @ W2.T + b2
        return layer_norm(x, g2, be2)

    def _L0_ffn_ref(x, Wr, W1, W3, W2):
        import math
        import jax, jax.numpy as jnp
        import numpy as np
        TOP_K = 2
        CAP_FACTOR = 1.25
        CLAMP = 10000.0
        B, S, D = x.shape
        E = Wr.shape[1]
        K = TOP_K
        T = B * S
        cap = max(1, math.ceil(T * K * CAP_FACTOR / E))
        xf = x.reshape(T, D)
        logits = jnp.clip(xf @ Wr, -CLAMP, CLAMP)
        top_v, top_i = jax.lax.top_k(logits, K)
        m = jnp.max(top_v, axis=-1, keepdims=True)
        expv = jnp.exp(top_v - m)
        top_p = expv / (jnp.sum(expv, axis=-1, keepdims=True) + 1e-12)
        Sp = T * K
        experts = top_i.reshape(Sp)
        weights = top_p.reshape(Sp)
        tokens = jnp.repeat(jnp.arange(T), K)
        oh = experts[:, None] == jnp.arange(E)[None, :]
        pos = jnp.sum(jnp.cumsum(oh.astype(jnp.int32), axis=0) * oh, axis=-1) - 1
        kept = pos < cap
        pos_safe = jnp.where(kept, pos, cap)
        xe = jnp.zeros((E, cap + 1, D), x.dtype).at[experts, pos_safe].set(xf[tokens])[:, :cap]
        h = jax.nn.silu(jnp.einsum('ecd,edf->ecf', xe, W1)) * jnp.einsum('ecd,edf->ecf', xe, W3)
        ye = jnp.einsum('ecf,efd->ecd', h, W2)
        yp = ye[experts, jnp.minimum(pos_safe, cap - 1)]
        wk = weights * kept.astype(weights.dtype)
        out = jnp.zeros((T, D), x.dtype).at[tokens].add(wk[:, None] * yp)
        return out.reshape(B, S, D)

    def _L1_xattn_ref(queries, keys, values, mask, W_Q, W_K, W_V, W_O):
        import jax, jax.numpy as jnp
        import numpy as np
        B, S, D, H, DK, DV = (4, 256, 128, 16, 64, 64)
        b, skv, _ = keys.shape
        sq = queries.shape[1]
        scaling = 1.0 / DK ** 0.5
        Q = (queries @ W_Q).reshape(b, sq, H, DK)
        K = (keys @ W_K).reshape(b, skv, H, DK)
        V = (values @ W_V).reshape(b, skv, H, DV)
        scores = jnp.einsum('bqhd,bkhd->bhqk', Q, K)
        scores = jnp.where(mask == 0, -jnp.inf, scores)
        probs = jax.nn.softmax(scores * scaling, axis=-1)
        attn = jnp.einsum('bhqk,bkhd->bqhd', probs, V).reshape(b, sq, H * DV)
        return attn @ W_O

    def _L1_ffn_ref(x, router_w, router_bias, up_proj, gate_proj, down_proj, sh_gate, sh_up, sh_down):
        import jax, jax.numpy as jnp
        import numpy as np
        DIM = 128
        EXPERT_DIM = 64
        N_EXPERTS = 16
        TOPK = 2
        SHARED_HIDDEN = EXPERT_DIM * TOPK
        B, T = (4, 128)

        def _moe_forward(x, router_w, router_bias, up_proj, gate_proj, down_proj, sh_gate, sh_up, sh_down):
            Bb, Tt, D = x.shape
            flat = x.reshape(Bb * Tt, D)
            N = flat.shape[0]
            logits = flat @ router_w.T
            topk_scores, topk_idx = jax.lax.top_k(logits + router_bias, TOPK)
            topk_scores = jax.nn.softmax(topk_scores, axis=-1)
            combine = jnp.zeros((N, N_EXPERTS), flat.dtype)
            combine = combine.at[jnp.arange(N)[:, None], topk_idx].add(topk_scores)
            up_all = jnp.einsum('nd,kde->nke', flat, up_proj)
            gate_all = jnp.einsum('nd,kde->nke', flat, gate_proj)
            hidden = jax.nn.silu(gate_all) * up_all
            down_all = jnp.einsum('nke,ked->nkd', hidden, down_proj)
            out = jnp.einsum('nk,nkd->nd', combine, down_all)
            sh_hidden = jax.nn.silu(flat @ sh_gate.T) * (flat @ sh_up.T)
            out = out + sh_hidden @ sh_down.T
            return out.reshape(Bb, Tt, D)
        return _moe_forward(x, router_w, router_bias, up_proj, gate_proj, down_proj, sh_gate, sh_up, sh_down)

    def _L2_xattn_ref(q, v, k, Wq, bq, Wk, bk, Wv, bv, Wo, bo, mask):
        import jax, jax.numpy as jnp
        import numpy as np
        B, S, D, H = (4, 256, 128, 16)
        DEPTH = D // H
        NEG = 10000000000.0

        def _split_heads(x):
            b, s, _ = x.shape
            return x.reshape(b, s, H, DEPTH).transpose(0, 2, 1, 3)
        qh = _split_heads(q @ Wq + bq)
        kh = _split_heads(k @ Wk + bk)
        vh = _split_heads(v @ Wv + bv)
        scale = 1.0 / jnp.sqrt(jnp.asarray(DEPTH, jnp.float32))
        logits = jnp.einsum('bhqd,bhkd->bhqk', qh, kh) * scale
        if mask:
            nd, ns = (logits.shape[-2], logits.shape[-1])
            i = jnp.arange(nd)[:, None]
            j = jnp.arange(ns)[None, :]
            b = (i >= j - ns + nd).astype(logits.dtype)
            logits = logits * b - NEG * (1.0 - b)
        attn = jax.nn.softmax(logits, axis=-1)
        out = jnp.einsum('bhqk,bhkd->bhqd', attn, vh)
        out = out.transpose(0, 2, 1, 3).reshape(q.shape[0], -1, D)
        return out @ Wo + bo

    def _L2_ffn_ref(hidden_states, Wr, W1, W2):
        import jax, jax.numpy as jnp
        import numpy as np
        TOP_K = 2
        B, S, D = hidden_states.shape
        E = Wr.shape[0]
        x = hidden_states.reshape(-1, D)
        T = x.shape[0]
        router_logits = x @ Wr.T
        routing_weights = jax.nn.softmax(router_logits, axis=-1)
        top_w, top_idx = jax.lax.top_k(routing_weights, TOP_K)
        top_w = top_w / jnp.sum(top_w, axis=-1, keepdims=True)
        comb = jnp.zeros((T, E), dtype=x.dtype).at[jnp.arange(T)[:, None], top_idx].add(top_w)
        h = jax.nn.silu(jnp.einsum('td,edf->tef', x, W1))
        y = jnp.einsum('tef,efd->ted', h, W2)
        out = jnp.einsum('te,ted->td', comb, y)
        return out.reshape(B, S, D)

    def _L3_xattn_ref(k, v, q, Wk, Wv, bv, Wq, bq, Wo, bo):
        import jax, jax.numpy as jnp
        import numpy as np
        D_MODEL = 128
        B, S = (4, 256)
        kp = jnp.einsum('bsd,ed->bse', k, Wk)
        vp = jnp.einsum('bsd,ed->bse', v, Wv) + bv
        qp = jnp.einsum('bsd,ed->bse', q, Wq) + bq
        scale = 1.0 / jnp.sqrt(jnp.float32(kp.shape[-1]))
        scores = jnp.einsum('bqd,bkd->bqk', qp, kp) * scale
        probs = jax.nn.softmax(scores, axis=-1)
        ctx = jnp.einsum('bqk,bkd->bqd', probs, vp)
        return jnp.einsum('bqd,ed->bqe', ctx, Wo) + bo

    def _L3_ffn_ref(hidden_states, ln1_w, ln1_b, q_w, q_b, k_w, k_b, v_w, v_b, o_w, o_b, ln2_w, ln2_b, router_w, fc1_w, fc1_b, fc2_w, fc2_b):
        import math
        import jax, jax.numpy as jnp
        import numpy as np
        B, S, D, H, E, F = (2, 128, 128, 16, 16, 512)
        HEAD = D // H
        MOE_TOKEN_DROPOUT = 0.2
        EPS = 1e-05

        def layer_norm(x, w, b):
            mu = x.mean(-1, keepdims=True)
            var = ((x - mu) ** 2).mean(-1, keepdims=True)
            return (x - mu) * jax.lax.rsqrt(var + EPS) * w + b
        b, s, _ = hidden_states.shape
        T = b * s
        neg = jnp.finfo(jnp.float32).min
        resid = hidden_states
        x = layer_norm(hidden_states, ln1_w, ln1_b)
        q = (x @ q_w + q_b) / math.sqrt(HEAD)
        k = x @ k_w + k_b
        v = x @ v_w + v_b
        split = lambda t: t.reshape(b, s, H, HEAD).transpose(0, 2, 1, 3)
        q, k, v = (split(q), split(k), split(v))
        scores = jnp.einsum('bhqd,bhkd->bhqk', q, k)
        causal = jnp.tril(jnp.ones((s, s), bool))
        scores = jnp.where(causal, scores, neg)
        attn = jax.nn.softmax(scores, axis=-1)
        ctx = jnp.einsum('bhqk,bhkd->bhqd', attn, v)
        ctx = ctx.transpose(0, 2, 1, 3).reshape(b, s, D)
        hidden = resid + (ctx @ o_w + o_b)
        resid = hidden
        xt = layer_norm(hidden, ln2_w, ln2_b).reshape(T, D)
        logits = xt @ router_w
        probs = jax.nn.softmax(logits, axis=-1)
        top1 = jnp.argmax(probs, axis=-1)
        m1 = jax.nn.one_hot(top1, E, dtype=jnp.float32)
        logits_no1 = jnp.where(m1 > 0, -jnp.inf, logits)
        top2 = jnp.argmax(logits_no1, axis=-1)
        m2 = jax.nn.one_hot(top2, E, dtype=jnp.float32)
        loc1 = jnp.cumsum(m1, axis=0) - 1.0
        loc2 = jnp.cumsum(m2, axis=0) - 1.0 + m1.sum(axis=0, keepdims=True)
        C = 2 * math.ceil(T / E)
        m1 = m1 * (loc1 < C)
        m2 = m2 * (loc2 < C)
        g1 = (probs * m1).sum(-1)
        g2 = (probs * m2).sum(-1)
        denom = jnp.maximum(g1 + g2, jnp.finfo(jnp.float32).eps)
        g1, g2 = (g1 / denom, g2 / denom)
        slot1 = (loc1 * m1).sum(-1).astype(jnp.int32)
        slot2 = (loc2 * m2).sum(-1).astype(jnp.int32)
        d1 = m1[:, :, None] * jax.nn.one_hot(slot1, C, dtype=jnp.float32)[:, None, :]
        d2 = m2[:, :, None] * jax.nn.one_hot(slot2, C, dtype=jnp.float32)[:, None, :]
        dispatch = d1 + d2
        combine = g1[:, None, None] * d1 + g2[:, None, None] * d2
        xin = jnp.einsum('tec,td->ecd', dispatch, xt)
        h = jnp.einsum('ecd,edf->ecf', xin, fc1_w) + fc1_b[:, None, :]
        h = jax.nn.gelu(h, approximate=False)
        eout = jnp.einsum('ecf,efd->ecd', h, fc2_w) + fc2_b[:, None, :]
        eout = eout * (1.0 - MOE_TOKEN_DROPOUT)
        moe_out = jnp.einsum('tec,ecd->td', combine, eout).reshape(b, s, D)
        return resid + moe_out
    x = x + jnp.tanh(g_xattn[0]) * _L0_xattn_ref(_layernorm(x, axis=-1), ctx_1024, fside_Bx16xSxS2_0, L0_xattn_Wq, L0_xattn_Wk, L0_xattn_Wv, L0_xattn_Wo, L0_xattn_W1, L0_xattn_b1, L0_xattn_W2, L0_xattn_b2, L0_xattn_g1, L0_xattn_be1, L0_xattn_g2, L0_xattn_be2)
    x = x + jnp.tanh(g_ffn[0]) * _L0_ffn_ref(_layernorm(x, axis=-1), L0_ffn_Wr, L0_ffn_W1, L0_ffn_W3, L0_ffn_W2)
    x = x + jnp.tanh(g_xattn[1]) * _L1_xattn_ref(_layernorm(x, axis=-1), ctx_1024, ctx_1024, mask_1x1xSxS2_ik0, L1_xattn_W_Q, L1_xattn_W_K, L1_xattn_W_V, L1_xattn_W_O)
    x = x + jnp.tanh(g_ffn[1]) * _L1_ffn_ref(_layernorm(x, axis=-1), L1_ffn_router_w, L1_ffn_router_bias, L1_ffn_up_proj, L1_ffn_gate_proj, L1_ffn_down_proj, L1_ffn_sh_gate, L1_ffn_sh_up, L1_ffn_sh_down)
    x = x + jnp.tanh(g_xattn[2]) * _L2_xattn_ref(_layernorm(x, axis=-1), ctx_1024, ctx_1024, L2_xattn_Wq, L2_xattn_bq, L2_xattn_Wk, L2_xattn_bk, L2_xattn_Wv, L2_xattn_bv, L2_xattn_Wo, L2_xattn_bo, 1)
    x = x + jnp.tanh(g_ffn[2]) * _L2_ffn_ref(_layernorm(x, axis=-1), L2_ffn_Wr, L2_ffn_W1, L2_ffn_W2)
    x = x + jnp.tanh(g_xattn[3]) * _L3_xattn_ref(ctx_1024, ctx_1024, _layernorm(x, axis=-1), L3_xattn_Wk, L3_xattn_Wv, L3_xattn_bv, L3_xattn_Wq, L3_xattn_bq, L3_xattn_Wo, L3_xattn_bo)
    x = x + jnp.tanh(g_ffn[3]) * _L3_ffn_ref(_layernorm(x, axis=-1), L3_ffn_ln1_w, L3_ffn_ln1_b, L3_ffn_q_w, L3_ffn_q_b, L3_ffn_k_w, L3_ffn_k_b, L3_ffn_v_w, L3_ffn_v_b, L3_ffn_o_w, L3_ffn_o_b, L3_ffn_ln2_w, L3_ffn_ln2_b, L3_ffn_router_w, L3_ffn_fc1_w, L3_ffn_fc1_b, L3_ffn_fc2_w, L3_ffn_fc2_b)
    return x

_drawn_inputs = setup_inputs


def setup_inputs(seed=0):
    import zlib

    import numpy as np

    out = dict(_drawn_inputs(seed))
    spreads = {'L0_xattn_b1': (0.0, 0.1),
     'L0_xattn_b2': (0.0, 0.1),
     'L0_xattn_g1': (1.0, 0.2),
     'L0_xattn_be1': (0.0, 0.279),
     'L0_xattn_g2': (1.0, 0.2),
     'L0_xattn_be2': (0.0, 0.1),
     'L1_ffn_router_bias': (0.0, 0.8),
     'L2_xattn_bq': (0.0, 2.0),
     'L2_xattn_bk': (0.0, 2.0),
     'L2_xattn_bv': (0.0, 0.458),
     'L2_xattn_bo': (0.0, 0.1),
     'L3_xattn_bv': (0.0, 0.1),
     'L3_xattn_bq': (0.0, 0.602),
     'L3_xattn_bo': (0.0, 0.1),
     'L3_ffn_ln1_w': (1.0, 0.6),
     'L3_ffn_ln1_b': (0.0, 0.8),
     'L3_ffn_q_b': (0.0, 0.8),
     'L3_ffn_k_b': (0.0, 2.0),
     'L3_ffn_v_b': (0.0, 0.8),
     'L3_ffn_o_b': (0.0, 0.1),
     'L3_ffn_ln2_w': (1.0, 0.6),
     'L3_ffn_ln2_b': (0.0, 0.693),
     'L3_ffn_fc1_b': (0.0, 0.8),
     'L3_ffn_fc2_b': (0.0, 0.381)}
    factors = {'fside_Bx16xSxS2_0': 6.169,
     'g_ffn': 32.336,
     'L0_ffn_Wr': 5.637,
     'L0_ffn_W1': 5.714,
     'L0_ffn_W3': 5.587,
     'L0_ffn_W2': 5.564,
     'L1_xattn_W_Q': 8.0,
     'L1_xattn_W_K': 8.0,
     'L1_ffn_router_w': 8.0,
     'L1_ffn_up_proj': 8.0,
     'L1_ffn_gate_proj': 8.0,
     'L1_ffn_down_proj': 8.0,
     'L1_ffn_sh_gate': 7.104,
     'L1_ffn_sh_up': 7.119,
     'L1_ffn_sh_down': 8.0,
     'L2_xattn_Wq': 8.0,
     'L2_xattn_Wk': 8.0,
     'L2_xattn_Wv': 3.288,
     'L3_ffn_q_w': 8.0,
     'L3_ffn_k_w': 8.0,
     'L3_ffn_v_w': 7.729,
     'L3_ffn_o_w': 5.264,
     'L3_ffn_fc1_w': 5.007,
     'L3_ffn_fc2_w': 4.519}
    for name, (base, spread) in spreads.items():
        noise = np.random.default_rng([zlib.crc32(name.encode()), seed]).standard_normal(out[name].shape)
        drawn = base * np.exp(spread * noise) if base else spread * noise
        out[name] = jnp.asarray(drawn.astype(out[name].dtype))
    for name, factor in factors.items():
        out[name] = (out[name] * factor).astype(out[name].dtype)
    return out
```

```python
from contextlib import ExitStack, contextmanager

import numpy as np
import concourse.bass as bass
from concourse import mybir

ALU = mybir.AluOpType
ACT = mybir.ActivationFunctionType
F32 = mybir.dt.float32
I32 = mybir.dt.int32
AX_X = mybir.AxisListType.X

P = 128
B, S, D = 4, 512, 128
NT = B * S // P
TB = S // P
S2 = 154
KM_, KR = 128, S2 - 128
H = 16
HG = 4
RR = HG * KR
GH = 3
NG = -(-H // GH)
EPS = 1e-5
LOW = -3.0e38
MASKED = -1.0e30
NOWHERE = 1.0e6
CAP0 = 640
CAP3 = 256

CONST = {}


def constants():
    p = np.arange(P)[:, None]
    f = np.arange(P)[None, :]
    parts = {
        "ident": (p == f) * 1.0,
        "ones": np.ones((P, P)),
        "earlier": (p < f) * 1.0,
        "first": (p == 0) * np.ones((1, P)),
        "head8": (p // 8 == np.arange(16)[None]) * (1 / np.sqrt(8.0)),
        "head64": (p // 64 == np.arange(2)[None]) * 0.125,
        "rest": (p // KR == np.arange(HG)[None]) * 1.0,
        "slot8": np.broadcast_to(float(CAP0) * np.arange(8)[None], (P, 8)),
        "slot16": np.broadcast_to(float(CAP3) * np.arange(16)[None], (P, 16)),
        "rank8": np.broadcast_to(8.0 - np.arange(8)[None], (P, 8)),
        "rank16": np.broadcast_to(16.0 - np.arange(16)[None], (P, 16)),
    }
    for i in range(TB):
        q = i * P + p
        parts[f"causal{i}"] = np.where(q >= np.arange(S2)[None] + S - S2, 0.0, MASKED)
    parts["tril"] = np.where(p >= f, 0.0, MASKED)
    parts["triu"] = np.where(f >= p, 0.0, MASKED)
    at, cols = 0, []
    for name, a in parts.items():
        CONST[name] = (at, a.shape[1])
        at += a.shape[1]
        cols.append(a.astype(np.float32))
    return np.ascontiguousarray(np.concatenate(cols, 1))


CONSTS = constants()

ROWS = ["L0_xattn_g2", "L0_xattn_be2", "L0_xattn_b2", "L2_xattn_bv", "L2_xattn_bo", "L3_xattn_bv", "L3_xattn_bo",
        "L3_ffn_v_b", "L3_ffn_o_b"]
COLS = ["L0_xattn_g1", "L0_xattn_be1", "L2_xattn_bq", "L2_xattn_bk", "L3_xattn_bq", "L3_ffn_q_b", "L3_ffn_k_b",
        "L3_ffn_ln1_w", "L3_ffn_ln1_b", "L3_ffn_ln2_w", "L3_ffn_ln2_b"]


class Tally:

    def __init__(self, per, i=0):
        self.per, self.i, self.k = per, i, 0

    def take(self):
        n = self.i * self.per + self.k
        self.k += 1
        return n

    def end(self):
        assert self.k == self.per, (self.k, self.per)


class Own:

    def __init__(self, eng, sem, base=0):
        self.eng, self.sem, self.base, self.i, self.per, self.k = eng, sem, base, 0, 0, 0

    def done(self, ins):
        ins.then_inc(self.sem, 1)
        self.k += 1

    def wait(self):
        self.eng.wait_ge(self.sem, self.i * self.per + (self.base + self.k))

    def loop(self, i, per):
        self.base, self.k, self.i, self.per = self.base + self.k, 0, i, per

    def end(self, count):
        assert self.k == self.per, (self.k, self.per)
        self.base, self.i, self.k, self.per = self.base + count * self.per, 0, 0, 0


class Model:

    def __init__(self):
        self.last_sems, self.now_sems = [], []


@contextmanager
def stage(nc, m, name):
    m.now_sems = []

    def sem(s):
        m.now_sems.append(nc.alloc_semaphore(f"{name}_{s}"))
        return m.now_sems[-1]

    yield sem
    for s in m.last_sems:
        nc.release_semaphore(s)
    m.last_sems = m.now_sems


def clear_last(m, sp):
    for s in m.last_sems:
        sp.sem_clear(s)


def ln_stats_vector(nc, dve, own, stats, tmp, src, var_ready, std_ready, std_count=1):
    with dve.Fori(0, NT) as t:
        own.loop(t, 1)
        own.done(nc.vector.bn_stats(stats[:, bass.ds(t, 1), :], src[:, bass.ds(t, 1), :]))
        own.end(NT)
    own.wait()
    mean_e, m2_e, mean_o, m2_o = (stats[:, :, k] for k in (1, 2, 4, 5))
    own.done(nc.vector.tensor_tensor(tmp[:, 2], mean_e, mean_o, ALU.subtract))
    own.done(nc.vector.tensor_tensor(tmp[:, 3], mean_e, mean_o, ALU.add))
    own.done(nc.vector.tensor_tensor(tmp[:, 4], m2_e, m2_o, ALU.add))
    own.wait()
    own.done(nc.vector.tensor_scalar(tmp[:, 0], tmp[:, 3], 0.5, None, ALU.mult))
    own.done(nc.vector.tensor_scalar(tmp[:, 5], tmp[:, 4], 1.0 / D, EPS, ALU.mult, ALU.add))
    own.done(nc.vector.tensor_tensor(tmp[:, 6], tmp[:, 2], tmp[:, 2], ALU.mult))
    own.wait()
    nc.vector.scalar_tensor_tensor(tmp[:, 7], tmp[:, 6], 0.25, tmp[:, 5], ALU.mult, ALU.add).then_inc(var_ready, 1)
    dve.wait_ge(std_ready, std_count)
    own.done(nc.vector.reciprocal(tmp[:, 1], tmp[:, 8]))
    own.wait()


def attention(nc, m, c):
    nm, dv, tiles, mode = c["name"], c["dv"], c["tiles"], c["mode"]
    W = dv + 1
    n = len(tiles)
    KB = H * dv // P
    OB = 1 if dv == 8 else HG
    OH = H // OB
    NM = 1 + -(-KB // GH) + 2 * (-(-KB // 4)) + n * -(-KB // 4)
    NTT = NG + n * (HG + 1)
    with ExitStack() as ctx:
        sb = lambda s, shape: ctx.enter_context(nc.sbuf_tensor(f"{nm}_{s}", shape, F32))
        ps = lambda s, shape: ctx.enter_context(nc.psum_tensor(f"{nm}_{s}", shape, F32))
        sem = ctx.enter_context(stage(nc, m, nm))
        stats, ln = sb("stats", [P, NT, 6]), sb("ln", [P, 9, NT])
        xn, xnT = sb("xn", [P, TB, D]), sb("xnT", [P, TB * P])
        KT, KM = sb("KT", [P, KB, S2]), sb("KM", [P, H, S2])
        G = sb("G", [P, H, S2])
        NZ = TB if mode == "bias" else 2
        Z = sb("Z", [P, NZ, H, S2])
        Zr = sb("Zr", [P, 2, HG, RR])
        mask = sb("mask", [P, TB, S2]) if mode == "mask" else None
        mx = sb("mx", [P, 2, H])
        E, Er = sb("E", [P, 2, H, P]), sb("Er", [RR, 2, HG, P])
        V, Vr = sb("V", [P, H, W]), sb("Vr", [RR, HG, HG * W])
        On, rin, OT = sb("On", [P, H, dv]), sb("rin", [P, H, 1]), sb("OT", [P, KB, P])
        ctm, ctr = sb("ctm", [P, S2]), sb("ctr", [P, HG, KR])
        pad = sb("pad", [P, n * NG])
        ys = sb("ys", [P, D]) if mode == "causal" else None
        bqr = sb("bqr", [P, P]) if mode == "causal" else None
        if mode == "mask":
            maski = ctx.enter_context(nc.sbuf_tensor(f"{nm}_maski", [P, TB, S2], I32))
        psS, psT, psO = ps("psS", [P, 2, 512]), ps("psT", [P, 2, 512]), ps("psO", [P, 2, 512])
        psM, psY = ps("psM", [P, 512]), ps("psY", [P, 512])
        own_v = sem("own_v")
        var_ready, std_ready = sem("var_ready"), sem("std_ready")
        loaded, bias_in = sem("loaded"), [sem(f"bias_in{i}") for i in range(TB if mode == "bias" else 0)]
        xn_ready, km_ready = sem("xn_ready"), sem("km_ready")
        vr_ready = sem("vr_ready")
        s_full, s_free, t_full, t_free = sem("s_full"), sem("s_free"), sem("t_full"), sem("t_free")
        o_full, o_free, m_full, m_free = sem("o_full"), sem("o_free"), sem("m_full"), sem("m_free")
        y_full, y_free = sem("y_full"), sem("y_free")
        ctr_ready, z_ready = sem("ctr_ready"), sem("z_ready")
        block = ctx.enter_context(nc.Block())
        NY = n + (mode == "causal")
        nOT = -(-KB // 4)
        ctx_b = m.ctxT

        @block.sync
        def _(sp):
            clear_last(m, sp)
            if mode == "mask":
                sp.dma_start(maski[:], m.mask.rearrange("(i p) k -> p i k", p=P)).then_inc(loaded, 16)
            if mode == "bias":
                for i in range(TB):
                    sp.dma_start(Z[:, i], m.bias[0, :, i * P:(i + 1) * P].rearrange("h p k -> p h k")).then_inc(bias_in[i], 16)
                with sp.Fori(0, B - 1) as b:
                    for i in range(TB):
                        sp.wait_ge(t_full, b * NTT + (NG + (i + 1) * (HG + 1)))
                        sp.dma_start(Z[:, i], m.bias[bass.ds(b + 1, 1), :, i * P:(i + 1) * P].rearrange(
                            "o h p k -> p (o h) k")).then_inc(bias_in[i], 16)

        @block.scalar
        def _(act):
            act.wait_ge(var_ready, 1)
            nc.scalar.activation(ln[:, 8], ln[:, 7], ACT.Sqrt).then_inc(std_ready, 1)
            with act.Fori(0, B) as b:
                mt, tt, av = Tally(NM, b), Tally(NTT, b), Tally(n * OB, b)

                def from_m(copies):
                    act.wait_ge(m_full, mt.take() + 1)
                    for k, (dst, src) in enumerate(copies):
                        last = nc.scalar.copy(dst, src)
                    last.then_inc(m_free, 1)

                from_m([(xnT[:], psM[:])])
                for j in range(0, KB, GH):
                    w = min(GH, KB - j)
                    act.wait_ge(m_full, mt.take() + 1)
                    if mode == "causal":
                        last = nc.scalar.activation(KT[:, 0], psM[:, 0:S2], ACT.Identity, bias=m.col("L2_xattn_bk"))
                    else:
                        last = nc.scalar.copy(KT[:, j:j + w], psM[:, 0:w * S2].rearrange("p (j k) -> p j k", k=S2))
                    last.then_inc(m_free, 1)
                for j in range(nOT):
                    hh = min(H, 512 // dv)
                    from_m([(V[:, hh * j:hh * (j + 1), 0:dv],
                             psM[:, 0:hh * dv].rearrange("p (h d) -> p h d", d=dv))])
                for j in range(nOT):
                    mt.take()
                for g in range(NG):
                    w = min(GH, H - GH * g)
                    act.wait_ge(t_full, tt.take() + 1)
                    nc.scalar.copy(G[:, GH * g:GH * g + w],
                                   psT[:, g % 2, 0:w * S2].rearrange("p (h k) -> p h k", k=S2)).then_inc(t_free, 1)
                for k in range(n + 2):
                    if k >= 2:
                        for j in range(nOT):
                            w = min(4, KB)
                            from_m([(OT[:, 4 * j:4 * j + w], psM[:, 0:w * P].rearrange("p (j q) -> p j q", q=P))])
                    if k < n:
                        for g in range(HG + 1):
                            if g == 0 and k >= 2:
                                act.wait_ge(o_full, b * (n * OB) + (k - 1) * OB)
                            x = tt.take()
                            act.wait_ge(t_full, x + 1)
                            bank = (NG + k * (HG + 1) + g) % 2
                            if g < HG:
                                nc.scalar.activation(E[:, k % 2, HG * g:HG * g + HG],
                                                     psT[:, bank].rearrange("p (h q) -> p h q", q=P),
                                                     ACT.Exp).then_inc(t_free, 1)
                            else:
                                nc.scalar.activation(Er[:, k % 2], psT[0:RR, bank].rearrange("p (h q) -> p h q", q=P),
                                                     ACT.Exp).then_inc(t_free, 1)
                mt.end(), tt.end()

        @block.gpsimd
        def _(pool):
            with pool.Fori(0, B) as b:
                for k in range(n):
                    for g in range(HG):
                        need = -(-(HG * g + HG) // GH)
                        pool.wait_ge(s_free, b * (n * NG) + (k * NG + need + 2))
                        h = slice(HG * g, HG * g + HG)
                        zz = Z[:, k % NZ, h, 0:KM_]
                        nc.gpsimd.tensor_tensor(zz, zz, mx[:, k % 2, h].unsqueeze(2).broadcast_to([P, HG, KM_]),
                                                ALU.subtract).then_inc(z_ready, 1)
                        nc.gpsimd.tensor_tensor(Zr[:, k % 2, g].rearrange("p (h k) -> p h k", k=KR), Z[:, k % NZ, h, KM_:S2],
                                                mx[:, k % 2, h].unsqueeze(2).broadcast_to([P, HG, KR]),
                                                ALU.subtract).then_inc(z_ready, 1)

        @block.tensor
        def _(pe):
            pe.sem_inc(m_free, 1)
            pe.sem_inc(y_free, 1)
            pe.sem_inc(s_free, 2)
            pe.sem_inc(t_free, 2)
            pe.sem_inc(o_free, 2)
            for s, v in c["weights"]:
                pe.wait_ge(s, v)
            with pe.Fori(0, B) as b:
                mt, tt, st, ot, yt = Tally(NM, b), Tally(NTT, b), Tally(n * NG, b), Tally(n * OB, b), Tally(NY, b)
                pe.wait_ge(m_free, mt.take() + 1)
                for i in range(TB):
                    pe.wait_ge(xn_ready, b * TB + (i + 1))
                    last = pe.transpose(psM[:, i * P:(i + 1) * P], xn[:, i], m.ident)
                last.then_inc(m_full, 1)
                pe.wait_ge(ctr_ready, b + 1)
                for j in range(0, KB, GH):
                    w = min(GH, KB - j)
                    pe.wait_ge(m_free, mt.take() + 1)
                    for jj in range(w):
                        last = pe.matmul(psM[:, jj * S2:(jj + 1) * S2], c["wk"][:, (j + jj) * P:(j + jj + 1) * P],
                                         ctm[:], start=(jj == 0), stop=(jj == w - 1),
                                         skip_group_check=True)
                    last.then_inc(m_full, 1)
                for j in range(nOT):
                    pe.wait_ge(m_free, mt.take() + 1)
                    w = min(512, H * dv)
                    last = pe.matmul(psM[:, 0:w], ctm[:, 0:KM_], c["wv"][:, j * w:(j + 1) * w], start=True,
                                     stop=mode != "causal")
                    if mode == "causal":
                        last = pe.matmul(psM[:, 0:w], m.ones[0:1, :], m.row("L2_xattn_bv"), start=False, stop=True)
                    last.then_inc(m_full, 1)
                for j in range(nOT):
                    pe.wait_ge(m_free, mt.take() + 1)
                    w = min(512, H * dv)
                    last = pe.matmul(psM[0:RR, 0:w], ctr[:].rearrange("p h k -> p (h k)"), c["wv"][:, j * w:(j + 1) * w],
                                     start=True, stop=mode != "causal")
                    if mode == "causal":
                        last = pe.matmul(psM[0:RR, 0:w], m.ones[0:1, 0:RR], m.row("L2_xattn_bv"), start=False, stop=True)
                    last.then_inc(m_full, 1)
                pe.wait_ge(km_ready, b + 1)
                for g in range(NG):
                    w = min(GH, H - GH * g)
                    pe.wait_ge(t_free, tt.take() + 1)
                    for hh in range(w) if KB > 1 else range(1):
                        h = GH * g + hh
                        if KB > 1:
                            last = pe.matmul(psT[:, g % 2, hh * S2:(hh + 1) * S2], c["wq"][:, h // 2], KM[:, h],
                                             start=(hh == 0), stop=(hh == w - 1), skip_group_check=True)
                        else:
                            last = pe.matmul(psT[:, g % 2, 0:w * S2], c["wq"],
                                             KM[:, h:h + w].rearrange("p h k -> p (h k)"), start=True, stop=True)
                    last.then_inc(t_full, 1)

                def scores(k):
                    for g in range(NG):
                        w = min(GH, H - GH * g)
                        hs = slice(GH * g, GH * g + w)
                        if k == 0 and g == 0:
                            pe.wait_ge(t_free, b * NTT + (NG + 2))
                        pe.wait_ge(s_free, st.take() + 1)
                        q = slice(tiles[k] * P, tiles[k] * P + P)
                        last = pe.matmul(psS[:, g % 2, 0:w * S2], xnT[:, q],
                                         G[:, hs].rearrange("p h k -> p (h k)"), start=True, stop=mode != "causal")
                        if mode == "causal":
                            last = pe.matmul(psS[:, g % 2, 0:w * S2], bqr[:],
                                             KM[:, hs].rearrange("p h k -> p (h k)"), start=False, stop=True)
                        last.then_inc(s_full, 1)

                scores(0)
                for k in range(n + 2):
                    if k >= 2:
                        pe.wait_ge(o_free, b * (n * OB) + ((k - 1) * OB + 2))
                        for j in range(nOT):
                            pe.wait_ge(m_free, mt.take() + 1)
                            for jj in range(min(4, KB)):
                                x = On[:].rearrange("p h d -> p (h d)")[:, (4 * j + jj) * P:(4 * j + jj + 1) * P]
                                last = pe.transpose(psM[:, jj * P:(jj + 1) * P], x, m.ident)
                            last.then_inc(m_full, 1)
                    if k + 1 < n:
                        scores(k + 1)
                    if k >= 2:
                        pe.wait_ge(m_free, b * NM + (mt.k + 1))
                        pe.wait_ge(y_free, yt.take() + 1)
                        for j in range(KB):
                            last = pe.matmul(psY[:, 0:D], OT[:, j], c["wo"][:, j], start=(j == 0),
                                             stop=(j == KB - 1 and mode != "causal"))
                        if mode == "causal":
                            last = pe.matmul(psY[:, 0:D], m.ones[0:1, :], m.row("L2_xattn_bo"), start=False, stop=True)
                        last.then_inc(y_full, 1)
                    if k < n:
                        for g in range(HG + 1):
                            pe.wait_ge(z_ready, b * (2 * n * HG) + 2 * (k * HG + min(g + 1, HG)))
                            pe.wait_ge(t_free, tt.take() + 1)
                            bank = (NG + k * (HG + 1) + g) % 2
                            for j in range(HG):
                                if g < HG:
                                    last = pe.transpose(psT[:, bank, j * P:(j + 1) * P],
                                                        Z[:, k % NZ, HG * g + j, 0:KM_], m.ident)
                                else:
                                    last = pe.transpose(psT[0:RR, bank, j * P:(j + 1) * P],
                                                        Zr[:, k % 2, j], m.ident)
                            last.then_inc(t_full, 1)
                    if 1 <= k <= n:
                        kk = k - 1
                        if kk == 0:
                            pe.wait_ge(vr_ready, b + 1)
                        pe.wait_ge(t_free, b * NTT + (NG + (kk + 1) * (HG + 1) + 2))
                        for o in range(OB):
                            u = ot.take()
                            pe.wait_ge(o_free, u + 1)
                            bank = (kk * OB + o) % 2
                            out = psO[:, bank, 0:OH * W].rearrange("p (h d) -> p h d", d=W)
                            for h0 in range(0, OH, HG):
                                for j in range(HG):
                                    hl = h0 + j
                                    h = o * OH + hl
                                    pe.matmul(out[:, hl], E[:, kk % 2, h], V[:, h], start=(hl == 0), stop=False,
                                              skip_group_check=True)
                                g = (o * OH + h0) // HG
                                last = pe.matmul(psO[:, bank, h0 * W:(h0 + HG) * W], Er[:, kk % 2, g], Vr[:, g],
                                                 start=False, stop=(h0 + HG == OH), skip_group_check=True)
                            last.then_inc(o_full, 1)
                if mode == "causal":
                    pe.wait_ge(y_free, yt.take() + 1)
                    pe.matmul(psY[:, 0:D], m.first, ys[:], start=True, stop=True).then_inc(y_full, 1)
                mt.end(), tt.end(), st.end(), ot.end(), yt.end()

        @block.vector
        def _(dve):
            own = Own(dve, own_v)
            if mode == "mask":
                dve.wait_ge(loaded, 16)
                own.done(nc.vector.tensor_copy(mask[:], maski[:]))
                own.wait()
                own.done(nc.vector.tensor_scalar(mask[:], mask[:], 0.0, MASKED, ALU.is_equal, ALU.mult))
            if mode == "causal":
                own.done(nc.vector.tensor_copy(bqr[:], m.col("L2_xattn_bq").broadcast_to([P, P])))
            own.done(nc.vector.memset(V[:, :, dv:W], 1.0))
            ln_stats_vector(nc, dve, own, stats, ln, m.X, var_ready, std_ready)
            with dve.Fori(0, B) as b:
                own.loop(b, n * OB + (mode == "causal"))
                st, ot, yt = Tally(n * NG, b), Tally(n * OB, b), Tally(NY, b)
                dve.wait_ge(y_free, b * NY + 1)
                nc.vector.tensor_copy(ctm[:], ctx_b[:, bass.ds(b, 1), :].rearrange("p o k -> p (o k)"))
                nc.vector.tensor_copy(ctr[:], ctx_b[:, bass.ds(b, 1), KM_:S2].broadcast_to([P, HG, KR])
                                      ).then_inc(ctr_ready, 1)
                for i in range(TB):
                    t = b * TB + i
                    nc.vector.tensor_scalar(xn[:, i], m.X[:, bass.ds(t, 1), :].rearrange("p o d -> p (o d)"),
                                            ln[:, 0, bass.ds(t, 1)], ln[:, 1, bass.ds(t, 1)], ALU.subtract, ALU.mult
                                            ).then_inc(xn_ready, 1)
                mdone = b * NM + (2 + 1 + -(-KB // GH) - 1)
                dve.wait_ge(m_free, mdone)
                if KB == 1:
                    nc.vector.tensor_tensor(KM[:], KT[:].broadcast_to([P, H, S2]),
                                            m.head8.unsqueeze(2).broadcast_to([P, H, S2]), ALU.mult).then_inc(km_ready, 1)
                else:
                    kmv = KM[:].rearrange("p (j a) k -> p j a k", a=2)
                    nc.vector.tensor_scalar(kmv[:, :, 0], KT[:], m.head64[:, 0:1], None, ALU.mult)
                    nc.vector.tensor_scalar(kmv[:, :, 1], KT[:], m.head64[:, 1:2], None, ALU.mult).then_inc(km_ready, 1)
                mrest = 1 + -(-KB // GH) + nOT
                for j in range(nOT):
                    dve.wait_ge(m_full, b * NM + (mrest + j + 1))
                    gs = HG // nOT
                    vv = Vr[:, j * gs:(j + 1) * gs].rearrange("p g (h d) -> p (g h) d", d=W)[:, :, 0:dv]
                    src = psM[0:RR, 0:gs * HG * dv].rearrange("p (h d) -> p h d", d=dv)
                    for g in range(gs):
                        last = nc.vector.tensor_tensor(
                            vv[:, g * HG:(g + 1) * HG], src[:, g * HG:(g + 1) * HG],
                            m.rest[0:RR].unsqueeze(2).broadcast_to([RR, HG, dv]), ALU.mult)
                    last.then_inc(m_free, 1)
                nc.vector.tensor_copy(Vr[:].rearrange("p g (h d) -> p g h d", d=W)[:, :, :, dv],
                                      m.rest[0:RR].unsqueeze(1).broadcast_to([RR, HG, HG])).then_inc(vr_ready, 1)

                def maxima(k):
                    for g in range(NG):
                        w = min(GH, H - GH * g)
                        if g == 0 and mode == "bias":
                            dve.wait_ge(bias_in[k], b * 16 + 16)
                        if g == 0 and NZ == 2 and k >= 2:
                            dve.wait_ge(t_full, b * NTT + (NG + (k - 1) * (HG + 1)))
                        dve.wait_ge(s_full, st.take() + 1)
                        nc.vector.memset(pad[:, k * NG + g:k * NG + g + 1], 0.0)
                        for hh in range(w):
                            h = GH * g + hh
                            add = Z[:, k, h] if mode == "bias" else mask[:, k] if mode == "mask" else m.causal[tiles[k]]
                            last = nc.vector.tensor_tensor_reduce(
                                Z[:, k % NZ, h], psS[:, g % 2, hh * S2:(hh + 1) * S2], add, 1.0, LOW, ALU.add, ALU.max,
                                mx[:, k % 2, h:h + 1])
                        last.then_inc(s_free, 1)

                maxima(0)
                for k in range(n + 2):
                    if k + 1 < n:
                        maxima(k + 1)
                    if k >= 2:
                        i = tiles[k - 2]
                        t = b * TB + i
                        dve.wait_ge(y_full, yt.take() + 1)
                        if mode == "causal" and k == 2:
                            own.done(nc.vector.tensor_copy(ys[:], psY[:, 0:D]))
                            own.wait()
                        x = m.X[:, bass.ds(t, 1), :].rearrange("p o d -> p (o d)")
                        if mode == "bias":
                            x1 = m.X1[:, bass.ds(t, 1), :].rearrange("p o d -> p (o d)")
                            nc.vector.tensor_tensor(x1, psY[:, 0:D], xn[:, i], ALU.add).then_inc(y_free, 1)
                        else:
                            nc.vector.scalar_tensor_tensor(x, psY[:, 0:D], m.gate(c["gate"]), x, ALU.mult, ALU.add
                                                           ).then_inc(y_free, 1)
                    if 1 <= k <= n:
                        for o in range(OB):
                            dve.wait_ge(o_full, ot.take() + 1)
                            bank = ((k - 1) * OB + o) % 2
                            out = psO[:, bank, 0:OH * W].rearrange("p (h d) -> p h d", d=W)
                            hs = slice(o * OH, (o + 1) * OH)
                            own.done(nc.vector.reciprocal(rin[:, hs], out[:, :, dv:W]))
                            own.wait()
                            last = nc.vector.tensor_tensor(On[:, hs], out[:, :, 0:dv],
                                                           rin[:, hs].broadcast_to([P, OH, dv]), ALU.mult)
                            last.then_inc(o_free, 1)
                if mode == "causal":
                    dve.wait_ge(y_full, yt.take() + 1)
                    for i in range(2):
                        x = m.X[:, bass.ds(b * TB + i, 1), :].rearrange("p o d -> p (o d)")
                        last = nc.vector.scalar_tensor_tensor(x, psY[:, 0:D], m.gate(c["gate"]), x, ALU.mult, ALU.add)
                    last.then_inc(y_free, 1)
                own.end(B)
                st.end(), ot.end(), yt.end()


def norm_transpose(nc, m, name, src, dst, w=None, b=None, router=None, turn=True):
    with ExitStack() as ctx:
        sb = lambda s, shape: ctx.enter_context(nc.sbuf_tensor(f"{name}_{s}", shape, F32))
        ps = lambda s, shape: ctx.enter_context(nc.psum_tensor(f"{name}_{s}", shape, F32))
        sem = ctx.enter_context(stage(nc, m, name))
        stats, ln = sb("stats", [P, NT, 6]), sb("ln", [P, 9, NT])
        psT = ps("psT", [P, NT // TB, 512])
        own_v, var_ready, std_ready = sem("own_v"), sem("var_ready"), sem("std_ready")
        x_ready, t_full, xt_ready = sem("x_ready"), sem("t_full"), sem("xt_ready")
        if router:
            r = Router(nc, sb, ps, sem, m, router)
        block = ctx.enter_context(nc.Block())

        @block.sync
        def _(sp):
            clear_last(m, sp)

        @block.scalar
        def _(act):
            act.wait_ge(var_ready, 1)
            nc.scalar.activation(ln[:, 8], ln[:, 7], ACT.Sqrt).then_inc(std_ready, 1)
            for c in range(NT // TB if turn else 0):
                act.wait_ge(t_full, c + 1)
                dst_t = m.XT[:, c * 512:(c + 1) * 512]
                if w is None:
                    nc.scalar.copy(dst_t, psT[:, c]).then_inc(xt_ready, 1)
                else:
                    nc.scalar.activation(dst_t, psT[:, c], ACT.Identity, bias=b, scale=w).then_inc(xt_ready, 1)
            if router:
                r.scalar(act)

        @block.tensor
        def _(pe):
            for t in range(NT if turn else 0):
                pe.wait_ge(x_ready, t + 1)
                last = pe.transpose(psT[:, t // TB, (t % TB) * P:(t % TB + 1) * P], dst[:, t], m.ident)
                if t % TB == TB - 1:
                    last.then_inc(t_full, 1)
            if router:
                r.tensor(pe, xt_ready)

        @block.vector
        def _(dve):
            own = Own(dve, own_v)
            ln_stats_vector(nc, dve, own, stats, ln, src, var_ready, std_ready)
            with dve.Fori(0, NT) as t:
                nc.vector.tensor_scalar(dst[:, bass.ds(t, 1), :], src[:, bass.ds(t, 1), :], ln[:, 0, bass.ds(t, 1)],
                                        ln[:, 1, bass.ds(t, 1)], ALU.subtract, ALU.mult).then_inc(x_ready, 1)
            if router:
                r.vector(dve, own)


class Router:

    def __init__(self, nc, sb, ps, sem, m, c):
        self.nc, self.m, self.c = nc, m, c
        E = c["E"]
        self.psL = ps("psL", [P, NT, E])
        self.psC = ps("psC", [P, 2, 512])
        self.L, self.eq, self.rank = sb("logits", [P, NT, E]), sb("eq", [P, NT, E]), sb("rank", [P, NT, E])
        self.hot = sb("hot", [P, 2, NT, E])
        self.v = sb("rv", [P, 12, NT])
        self.pos, self.run = sb("pos", [P, 2, NT, E]), sb("run", [P, 2, NT, E])
        self.l_ready, self.diff_ready, self.exp_ready = sem("l_ready"), sem("diff_ready"), sem("exp_ready")
        self.hot_ready, self.c_ready = sem("hot_ready"), sem("c_ready")

    def tensor(self, pe, xt_ready):
        c, m = self.c, self.m
        for t in range(NT):
            pe.wait_ge(xt_ready, t // TB + 1)
            last = pe.matmul(self.psL[:, t], m.XT[:, t * P:(t + 1) * P], c["w"], start=(t == 0), stop=(t == NT - 1),
                             skip_group_check=True)
        last.then_inc(self.l_ready, 1)
        if c["kind"] in ("L0", "L3"):
            pe.wait_ge(self.hot_ready, 1)
            n = NT * c["E"]
            for k in range(1 if c["kind"] == "L0" else 2):
                hot = self.hot[:, k].rearrange("p t e -> p (t e)")
                pe.matmul(self.psC[:, k, 0:n], m.const["earlier"], hot, start=True, stop=True, skip_group_check=True)
                last = pe.matmul(self.psC[:, k, 256:256 + n], m.ones, hot, start=False, stop=True, skip_group_check=True)
            last.then_inc(self.c_ready, 1)

    def scalar(self, act):
        nc, v = self.nc, self.v
        act.wait_ge(self.diff_ready, 1)
        last = nc.scalar.activation(v[:, 3], v[:, 2], ACT.Exp)
        if self.c["kind"] == "L3":
            last = nc.scalar.activation(self.rank[:], self.eq[:], ACT.Exp)
        last.then_inc(self.exp_ready, 1)

    def vector(self, dve, own):
        nc, c, v, m = self.nc, self.c, self.v, self.m
        E, kind, L, eq, rank, hot = c["E"], c["kind"], self.L, self.eq, self.rank, self.hot
        wide = lambda a: a.unsqueeze(2).broadcast_to([P, NT, E])
        order = m.const["rank%d" % E].unsqueeze(1).broadcast_to([P, NT, E])

        def step(ins):
            own.done(ins)
            own.wait()

        dve.wait_ge(self.l_ready, 1)
        if kind == "L0":
            step(nc.vector.tensor_scalar(L[:], self.psL[:], -1e4, 1e4, ALU.max, ALU.min))
        elif kind == "L1":
            step(nc.vector.tensor_tensor(L[:], self.psL[:], m.router_bias[:].unsqueeze(1).broadcast_to([P, NT, E]), ALU.add))
        else:
            step(nc.vector.tensor_copy(L[:], self.psL[:]))
        for k in range(2):
            step(nc.vector.tensor_reduce(v[:, k], L[:], AX_X, ALU.max))
            step(nc.vector.tensor_tensor(eq[:], L[:], wide(v[:, k]), ALU.is_equal))
            step(nc.vector.tensor_tensor(rank[:], eq[:], order, ALU.mult))
            step(nc.vector.tensor_reduce(v[:, 4], rank[:], AX_X, ALU.max))
            step(nc.vector.tensor_tensor(hot[:, k], rank[:], wide(v[:, 4]), ALU.is_equal))
            if k == 0:
                if kind == "L3":
                    step(nc.vector.tensor_tensor(self.run[:, 1], L[:], wide(v[:, 0]), ALU.subtract))
                step(nc.vector.scalar_tensor_tensor(L[:], hot[:, 0], LOW, L[:], ALU.mult, ALU.add))
        if kind == "L0":
            own.done(nc.vector.tensor_tensor(self.pos[:, 1], hot[:, 0], hot[:, 1], ALU.add))
            own.wait()
            own.done(nc.vector.tensor_copy(self.run[:, 1], hot[:, 0]))
            own.wait()
            nc.vector.tensor_copy(hot[:, 0], self.pos[:, 1]).then_inc(self.hot_ready, 1)
        elif kind == "L3":
            own.done(nc.vector.tensor_copy(eq[:], self.run[:, 1]))
            own.wait()
            dve.wait_ge(own.sem, own.base + own.k)
            nc.vector.memset(v[:, 11], 0.0).then_inc(self.hot_ready, 1)
        own.done(nc.vector.tensor_tensor(v[:, 2], v[:, 1], v[:, 0], ALU.subtract))
        own.wait()
        nc.vector.memset(v[:, 10], 0.0).then_inc(self.diff_ready, 1)
        dve.wait_ge(self.exp_ready, 1)
        if kind != "L3":
            step(nc.vector.tensor_scalar(v[:, 5], v[:, 3], 1.0, 1e-12 if kind == "L0" else 0.0, ALU.add, ALU.add))
            step(nc.vector.reciprocal(v[:, 6], v[:, 5]))
            step(nc.vector.tensor_tensor(v[:, 7], v[:, 3], v[:, 6], ALU.mult))
        if kind in ("L0", "L3"):
            self.positions(dve, own, step)
        if kind in ("L0", "L3"):
            cap = CAP0 if kind == "L0" else CAP3
            if kind == "L3":
                step(nc.vector.tensor_reduce(v[:, 5], rank[:], AX_X, ALU.add))
                step(nc.vector.reciprocal(v[:, 6], v[:, 5]))
                step(nc.vector.tensor_tensor(v[:, 7], v[:, 3], v[:, 6], ALU.mult))
            for k in range(2):
                pos = self.pos[:, 0 if kind == "L0" else k]
                chosen = self.run[:, 1] if kind == "L0" and k == 0 else hot[:, k]
                step(nc.vector.tensor_scalar(rank[:], pos, float(cap), NOWHERE, ALU.is_ge, ALU.mult))
                step(nc.vector.tensor_tensor(rank[:], rank[:], pos, ALU.add))
                step(nc.vector.tensor_tensor(rank[:], rank[:], m.const["slot%d" % E].unsqueeze(1).broadcast_to([P, NT, E]),
                                             ALU.add))
                step(nc.vector.tensor_tensor(rank[:], rank[:], chosen, ALU.mult))
                step(nc.vector.tensor_reduce(v[:, 8], rank[:], AX_X, ALU.add))
                step(nc.vector.tensor_copy(m.slot_to[:, k], v[:, 8]))
                step(nc.vector.tensor_scalar(v[:, 9], v[:, 8], float(E * cap - 1), None, ALU.min))
                step(nc.vector.tensor_copy(m.slot_from[:, k], v[:, 9]))
                step(nc.vector.tensor_scalar(v[:, 9], v[:, 8], NOWHERE, None, ALU.is_lt))
                step(nc.vector.tensor_tensor(v[:, 6 + k], v[:, 6 + k], v[:, 9], ALU.mult))
            if kind == "L3":
                step(nc.vector.tensor_tensor(v[:, 8], v[:, 6], v[:, 7], ALU.add))
                step(nc.vector.tensor_scalar(v[:, 8], v[:, 8], float(np.finfo(np.float32).eps), None, ALU.max))
                step(nc.vector.reciprocal(v[:, 9], v[:, 8]))
                for k in range(2):
                    step(nc.vector.tensor_tensor(v[:, 6 + k], v[:, 6 + k], v[:, 9], ALU.mult))
                step(nc.vector.tensor_scalar(v[:, 6:8], v[:, 6:8], 1.0 - 0.2, None, ALU.mult))
            step(nc.vector.tensor_scalar(m.slot_share[:], v[:, 6:8], m.gate(c["gate"]), None, ALU.mult))
            return
        step(nc.vector.tensor_tensor(eq[:], hot[:, 0], wide(v[:, 6]), ALU.mult))
        step(nc.vector.tensor_tensor(rank[:], hot[:, 1], wide(v[:, 7]), ALU.mult))
        step(nc.vector.tensor_tensor(eq[:], eq[:], rank[:], ALU.add))
        step(nc.vector.tensor_scalar(c["comb"], eq[:], m.gate(c["gate"]), None, ALU.mult))

    def positions(self, dve, own, step):
        nc, E = self.nc, self.c["E"]
        pos, run, n = self.pos, self.run, NT * E
        dve.wait_ge(self.c_ready, 1)
        ks = 1 if self.c["kind"] == "L0" else 2
        for k in range(ks):
            sums = self.psC[:, k, 256:256 + n].rearrange("p (t e) -> p t e", e=E)
            inside = self.psC[:, k, 0:n].rearrange("p (t e) -> p t e", e=E)
            r = run[:, 0]
            step(nc.vector.tensor_copy(r, sums))
            for t in range(1, NT):
                step(nc.vector.tensor_tensor(r[:, t], r[:, t], r[:, t - 1], ALU.add))
            if k == 0 and ks == 2:
                step(nc.vector.tensor_copy(run[:, 1, 0], r[:, NT - 1]))
            step(nc.vector.tensor_tensor(r, r, sums, ALU.subtract))
            step(nc.vector.tensor_tensor(pos[:, k], r, inside, ALU.add))
            if k == 1:
                step(nc.vector.tensor_tensor(pos[:, 1], pos[:, 1], run[:, 1, 0].unsqueeze(1).broadcast_to([P, NT, E]),
                                             ALU.add))


def experts(nc, m, name, c):
    EB, split, J = c["w1"].shape[0], c.get("split", 1), c["w1"].shape[2] // P
    C = NT // TB
    U = min(2, EB)
    glu = "w3" in c
    acc = c["dst"]
    with ExitStack() as ctx:
        sb = lambda s, shape: ctx.enter_context(nc.sbuf_tensor(f"{name}_{s}", shape, F32))
        ps = lambda s, shape: ctx.enter_context(nc.psum_tensor(f"{name}_{s}", shape, F32))
        sem = ctx.enter_context(stage(nc, m, name))
        w1, w2 = sb("w1", [P, U, J * P]), sb("w2", [P, U, J, D])
        b1 = sb("b1", [P, U, J]) if "b1" in c else None
        w3 = sb("w3", [P, U, J * P]) if glu else None
        h = sb("h", [P, 2, J, 512])
        psA = ps("psA", [P, 2, 512])
        psB = ps("psB", [P, 2, 512]) if glu else None
        psY = ps("psY", [P, 2 * split, 512])
        w_in = [sem(f"w_in{u}") for u in range(U)]
        a_full, a_free, b_full, b_free = sem("a_full"), sem("a_free"), sem("b_full"), sem("b_free")
        y_full, y_free, part = sem("y_full"), sem("y_free"), sem("part")
        block = ctx.enter_context(nc.Block())
        nw = 2 + glu + (b1 is not None)
        N = U * C * J

        def load(sp, e, u):
            sp.dma_start(w1[:, u], e(c["w1"])).then_inc(w_in[u], 16)
            if glu:
                sp.dma_start(w3[:, u], e(c["w3"])).then_inc(w_in[u], 16)
            if b1 is not None:
                sp.dma_start(b1[:, u], e(c["b1"])).then_inc(w_in[u], 16)
            sp.dma_start(w2[:, u], e(c["w2"])).then_inc(w_in[u], 16)

        @block.sync
        def _(sp):
            clear_last(m, sp)
            for u in range(U):
                load(sp, lambda a: a[u], u)
            if EB > U:
                with sp.Fori(0, EB // U - 1) as i:
                    for u in range(U):
                        sp.wait_ge(y_full, i * (U * C) + ((u + 1) * C + 2))
                        load(sp, lambda a: a[bass.ds(i * U + (U + u), 1)].rearrange(
                            "o p f -> p (o f)" if len(a.shape) == 3 else "o p j f -> p (o j) f"), u)

        @block.scalar
        def _(act):
            with act.Fori(0, EB // U) as i:
                a = Tally(N, i)
                for u in range(U):
                    for cc in range(C):
                        s = (u * C + cc) % 2
                        for j in range(J):
                            if j == 0:
                                act.wait_ge(y_full, i * (U * C) + (u * C + cc + 1))
                            act.wait_ge(a_full, a.take() + 1)
                            bias = 0.0
                            if "b1" in c:
                                bias = b1[:, u, j:j + 1]
                            nc.scalar.activation(h[:, s, j], psA[:, j % 2] if J > 1 else psA[:, s], c["act"], bias=bias
                                                 ).then_inc(a_free, 1)
                a.end()

        @block.tensor
        def _(pe):
            pe.sem_inc(a_free, 2)
            pe.sem_inc(b_free, 2)
            pe.sem_inc(y_free, 2)
            pe.sem_inc(y_full, 2)
            with pe.Fori(0, EB // U) as i:
                a = Tally(N, i)

                def hidden(k):
                    u, cc = divmod(k, C)
                    if cc == 0:
                        pe.wait_ge(w_in[u], i * (16 * nw) + 16 * nw)
                    x = m.XT[:, cc * 512:(cc + 1) * 512]
                    for j in range(J):
                        n = a.take()
                        bank = j % 2 if J > 1 else k % 2
                        pe.wait_ge(a_free, n + 1)
                        last = pe.matmul(psA[:, bank], w1[:, u, j * P:(j + 1) * P], x, start=True, stop=True)
                        if glu:
                            pe.wait_ge(b_free, n + 1)
                            last.then_inc(a_full, 1)
                            last = pe.matmul(psB[:, bank], w3[:, u, j * P:(j + 1) * P], x, start=True, stop=True)
                            last.then_inc(b_full, 1)
                        else:
                            last.then_inc(a_full, 1)

                def outputs(k):
                    u, cc = divmod(k, C)
                    pe.wait_ge(b_free if glu else a_free, i * N + ((k + 1) * J + 2))
                    pe.wait_ge(y_free, i * (U * C) + (k + 1))
                    for q in range(split):
                        r = slice(q * (P // split), (q + 1) * (P // split))
                        for t in range(TB):
                            for j in range(J):
                                last = pe.matmul(psY[:, (k % 2) * split + q, t * P:(t + 1) * P], h[r, k % 2, j, t * P:(t + 1) * P],
                                                 w2[r, u, j], start=(t == 0 and j == 0),
                                                 stop=(t == TB - 1 and j == J - 1 and "b2" not in c), skip_group_check=True)
                            if "b2" in c:
                                last = pe.matmul(psY[:, (k % 2) * split + q, t * P:(t + 1) * P], m.ones[0:1, :],
                                                 c["b2"](i, U, u), start=False, stop=(t == TB - 1), skip_group_check=True)
                    last.then_inc(y_full, 1)

                hidden(0)
                for k in range(U * C):
                    if k + 1 < U * C:
                        hidden(k + 1)
                    outputs(k)
                a.end()

        @block.vector
        def _(dve):
            with dve.Fori(0, EB // U) as i:
                n = Tally(N, i)

                def gate(k):
                    for j in range(J):
                        x = n.take()
                        bank = j % 2 if J > 1 else k % 2
                        dve.wait_ge(a_free, x + 3)
                        dve.wait_ge(b_full, x + 1)
                        nc.vector.tensor_tensor(h[:, k % 2, j], h[:, k % 2, j], psB[:, bank], ALU.mult).then_inc(b_free, 1)

                if glu:
                    gate(0)
                for k in range(U * C):
                    u, cc = divmod(k, C)
                    if glu and k + 1 < U * C:
                        gate(k + 1)
                    dve.wait_ge(y_full, i * (U * C) + (k + 3))
                    for q in range(split):
                        for t in range(TB):
                            x = acc[:, cc * TB + t]
                            if q == 0 and t == 0:
                                dve.wait_ge(y_free, i * (U * C) + (k + 2))
                            elif q > 0 and t == 0:
                                dve.wait_ge(part, i * (U * C * (split - 1)) + (k * (split - 1) + q))
                            last = nc.vector.scalar_tensor_tensor(x, psY[:, (k % 2) * split + q, t * P:(t + 1) * P],
                                                                  c["share"](i, U, u, q, cc * TB + t), x, ALU.mult, ALU.add)
                        if q < split - 1:
                            last.then_inc(part, 1)
                    last.then_inc(y_free, 1)
                if glu:
                    n.end()



def routed_experts(nc, m, name, c):
    EB, J, U, chunks = c["w1"].shape[0], c["w1"].shape[2] // P, c["U"], c["chunks"]
    T, CH = sum(chunks), len(chunks)
    NMAX = max(chunks) * P
    UC = U * CH
    assert UC % 2 == 0 and EB % U == 0
    TOT = EB * CH
    NS = EB * T * P
    glu = "w3" in c
    b1, b2 = "b1" in c, "b2" in c
    units = [(u, sum(chunks[:q]), chunks[q]) for u in range(U) for q in range(CH)]
    with ExitStack() as ctx:
        sb = lambda s, shape: ctx.enter_context(nc.sbuf_tensor(f"{name}_{s}", shape, F32))
        ps = lambda s, shape: ctx.enter_context(nc.psum_tensor(f"{name}_{s}", shape, F32))
        sem = ctx.enter_context(stage(nc, m, name))
        w1, w2 = sb("w1", [P, U, J * P]), sb("w2", [P, U, J, D])
        w3 = sb("w3", [P, U, J * P]) if glu else None
        b1s = sb("b1", [P, U, J]) if b1 else None
        b2s = sb("b2", [P, U, D]) if b2 else None
        xs, xsT = sb("xs", [P, U, T, D]), sb("xsT", [P, 2, NMAX])
        h, ys = sb("h", [P, 2, J, NMAX]), sb("ys", [P, 2, NMAX // P, D])
        psT, psA, psY = ps("psT", [P, 2, 512]), ps("psA", [P, 2, 512]), ps("psY", [P, 2, 512])
        psB = ps("psB", [P, 2, 512]) if glu else None
        w_in, x_in = [sem(f"w_in{u}") for u in range(U)], [sem(f"x_in{u}") for u in range(U)]
        stored = [sem("stored0"), sem("stored1")]
        scattered, gathered, before = m.scattered, m.gathered, c["before"]
        t_full, t_free = sem("t_full"), sem("t_free")
        a_full, a_free = sem("a_full"), sem("a_free")
        b_full, b_free = (sem("b_full"), sem("b_free")) if glu else (a_full, a_free)
        y_full, y_free, summed = sem("y_full"), sem("y_free"), sem("summed")
        block = ctx.enter_context(nc.Block())
        nw = 2 + glu + b1 + b2
        N = UC * J
        slots_in = m.slots_in[0:NS].rearrange("(e t p) d -> e p t d", p=P, t=T)
        slots_out = m.slots_out[0:NS].rearrange("(e t p) d -> e p t d", p=P, t=T)

        @block.sync
        def _(sp):
            clear_last(m, sp)
            sp.sem_inc(stored[0], 16)
            sp.sem_inc(stored[1], 16)

            def load_w(e, u):
                sp.dma_start(w1[:, u], e(c["w1"])).then_inc(w_in[u], 16)
                if glu:
                    sp.dma_start(w3[:, u], e(c["w3"])).then_inc(w_in[u], 16)
                if b1:
                    sp.dma_start(b1s[:, u], e(c["b1"])).then_inc(w_in[u], 16)
                if b2:
                    sp.dma_start(b2s[:, u], e(c["b2"]).broadcast_to([P, D])).then_inc(w_in[u], 16)
                sp.dma_start(w2[:, u], e(c["w2"])).then_inc(w_in[u], 16)

            for u in range(U):
                load_w(lambda a: a[u], u)
            sp.wait_ge(scattered, (before + 1) * 16 * 2 * NT)
            for u in range(U):
                sp.dma_start(xs[:, u], slots_in[u]).then_inc(x_in[u], 16)
            def store(k, i, i0=0):
                u, first, tiles = units[k]
                sp.wait_ge(y_free, (i0 + i) * UC + (k + 3))
                e = slots_out[bass.ds(i * U + u, 1)] if i0 == 0 else slots_out[i0 * U + u:i0 * U + u + 1]
                sp.dma_start(e.rearrange("o p t d -> p (o t) d")[:, first:first + tiles], ys[:, k % 2, 0:tiles]
                             ).then_inc(stored[k % 2], 16)

            rounds = EB // U
            with sp.Fori(0, rounds - 1) as i:
                for u in range(U):
                    at = lambda a: a[bass.ds(i * U + (U + u), 1)].rearrange(
                        "o p f -> p (o f)" if len(a.shape) == 3 else "o p j f -> p (o j) f")
                    sp.wait_ge(t_full, i * UC + (u + 1) * CH)
                    sp.dma_start(xs[:, u], at(slots_in)).then_inc(x_in[u], 16)
                    for q in range(CH):
                        store(u * CH + q, i)
                    load_w(at, u)
            for k in range(UC):
                store(k, 0, rounds - 1)

        @block.scalar
        def _(act):
            with act.Fori(0, EB // U) as i:
                a = Tally(N, i)

                def turned(k):
                    tiles = units[k][2]
                    act.wait_ge(t_full, i * UC + (k + 1))
                    act.wait_ge(b_full, i * N + (k + 1) * J)
                    src, dst = psT[:, k % 2, 0:tiles * P], xsT[:, k % 2, 0:tiles * P]
                    if c.get("scale") is None:
                        nc.scalar.copy(dst, src).then_inc(t_free, 1)
                    else:
                        nc.scalar.activation(dst, src, ACT.Identity, bias=c["bias"], scale=c["scale"]).then_inc(t_free, 1)

                turned(0)
                turned(1)
                for k, (u, _, tiles) in enumerate(units):
                    for j in range(J):
                        if j == 0:
                            act.wait_ge(y_full, i * UC + (k + 1))
                        act.wait_ge(a_full, a.take() + (2 * J + 1))
                        nc.scalar.activation(h[:, k % 2, j, 0:tiles * P], psA[:, j % 2, 0:tiles * P], c["act"],
                                             bias=b1s[:, u, j:j + 1] if b1 else 0.0).then_inc(a_free, 1)
                    if k + 2 < UC:
                        turned(k + 2)
                a.end()

        @block.tensor
        def _(pe):
            pe.sem_inc(t_free, 2)
            pe.sem_inc(a_free, 2)
            pe.sem_inc(a_full, 2 * J)
            if glu:
                pe.sem_inc(b_free, 2)
                pe.sem_inc(b_full, 2 * J)
            pe.sem_inc(y_free, 2)
            pe.sem_inc(y_full, 2)
            with pe.Fori(0, EB // U) as i:
                a = Tally(N, i)

                def turn(k):
                    u, first, tiles = units[k]
                    if first == 0:
                        pe.wait_ge(x_in[u], i * 16 + 16)
                    pe.wait_ge(t_free, i * UC + (k + 1))
                    for t in range(tiles):
                        last = pe.transpose(psT[:, k % 2, t * P:(t + 1) * P], xs[:, u, first + t], m.ident)
                    last.then_inc(t_full, 1)

                def hidden(k):
                    u, first, tiles = units[k]
                    w = tiles * P
                    if first == 0:
                        pe.wait_ge(w_in[u], i * (16 * nw) + 16 * nw)
                    pe.wait_ge(t_free, i * UC + (k + 3))
                    x = xsT[:, k % 2, 0:w]
                    for j in range(J):
                        n = a.take()
                        pe.wait_ge(a_free, n + 1)
                        pe.matmul(psA[:, j % 2, 0:w], w1[:, u, j * P:(j + 1) * P], x, start=True, stop=True).then_inc(a_full, 1)
                        if glu:
                            pe.wait_ge(b_free, n + 1)
                            pe.matmul(psB[:, j % 2, 0:w], w3[:, u, j * P:(j + 1) * P], x, start=True, stop=True).then_inc(b_full, 1)

                def outputs(k):
                    u, first, tiles = units[k]
                    pe.wait_ge(b_free, i * N + ((k + 1) * J + 2))
                    pe.wait_ge(y_free, i * UC + (k + 1))
                    for t in range(tiles):
                        for j in range(J):
                            last = pe.matmul(psY[:, k % 2, t * P:(t + 1) * P], h[:, k % 2, j, t * P:(t + 1) * P], w2[:, u, j],
                                             start=(t == 0 and j == 0), stop=(t == tiles - 1 and j == J - 1),
                                             skip_group_check=True)
                    last.then_inc(y_full, 1)

                turn(0)
                turn(1)
                hidden(0)
                for k in range(UC):
                    if k + 2 < UC:
                        turn(k + 2)
                    if k + 1 < UC:
                        hidden(k + 1)
                    outputs(k)
                a.end()

        @block.vector
        def _(dve):
            with dve.Fori(0, EB // U) as i:
                n = Tally(N, i)

                def gate(k):
                    w = units[k][2] * P
                    for j in range(J):
                        x = n.take()
                        dve.wait_ge(a_free, x + 3)
                        dve.wait_ge(b_full, x + (2 * J + 1))
                        nc.vector.tensor_tensor(h[:, k % 2, j, 0:w], h[:, k % 2, j, 0:w], psB[:, j % 2, 0:w], ALU.mult
                                                ).then_inc(b_free, 1)

                if glu:
                    gate(0)
                for k, (u, _, tiles) in enumerate(units):
                    if glu and k + 1 < UC:
                        gate(k + 1)
                    dve.wait_ge(y_full, i * UC + (k + 3))
                    dve.wait_ge(stored[k % 2], i * (8 * UC) + (16 * (k // 2) + 16))
                    src = psY[:, k % 2, 0:tiles * P].rearrange("p (t d) -> p t d", d=D)
                    if b2:
                        nc.vector.tensor_tensor(ys[:, k % 2, 0:tiles], src, b2s[:, u:u + 1].broadcast_to([P, tiles, D]), ALU.add
                                                ).then_inc(y_free, 1)
                    else:
                        nc.vector.tensor_copy(ys[:, k % 2, 0:tiles], src).then_inc(y_free, 1)
                if glu:
                    n.end()
            for g in range(TB):
                dve.wait_ge(gathered[g], (before + 1) * 16 * 2 * TB)
                for k, back in enumerate((m.XN, m.XT3)):
                    if k:
                        dve.wait_ge(summed, 2 * g + 1)
                    for t in range(g * TB, (g + 1) * TB):
                        last = nc.vector.scalar_tensor_tensor(m.X[:, t], back[:, t], m.slot_share[:, k, t:t + 1], m.X[:, t],
                                                              ALU.mult, ALU.add)
                    last.then_inc(summed, 1)

        @block.gpsimd
        def _(pool):
            pool.wait_ge(m.zeroed, 16 * 2)
            for k in range(2):
                for t in range(NT):
                    pool.indirect_dma_start(m.slots_in[0:NS], bass.IndirectOffsetOnAxis(ap=m.slot_to[:, k, t:t + 1], axis=0),
                                            c["rows"][:, t], None, bounds_check=NS - 1, oob_is_err=False
                                            ).then_inc(scattered, 16)
            for s in stored:
                pool.wait_ge(s, 16 * (TOT // 2 + 1))
            for t in range(NT):
                for k, back in enumerate((m.XN, m.XT3)):
                    pool.indirect_dma_start(back[:, t], None, m.slots_out[0:NS],
                                            bass.IndirectOffsetOnAxis(ap=m.slot_from[:, k, t:t + 1], axis=0),
                                            bounds_check=NS - 1, oob_is_err=False).then_inc(gathered[t // TB], 16)


def add_layer(nc, m, name, src, gate, w=None, b=None):
    with ExitStack() as ctx:
        own_v = ctx.enter_context(stage(nc, m, name))("own")
        block = ctx.enter_context(nc.Block())

        @block.sync
        def _(sp):
            clear_last(m, sp)

        @block.vector
        def _(dve):
            own = Own(dve, own_v)
            if w is not None:
                own.done(nc.vector.tensor_tensor(src[:], src[:], w.unsqueeze(1).broadcast_to([P, NT, D]), ALU.mult))
                own.wait()
                own.done(nc.vector.tensor_tensor(src[:], src[:], b.unsqueeze(1).broadcast_to([P, NT, D]), ALU.add))
                own.wait()
            nc.vector.scalar_tensor_tensor(m.X[:], src[:], m.gate(gate), m.X[:], ALU.mult, ALU.add)


def single_head(nc, m):
    nm, w = "L3x", m.w
    SC = 1.0 / float(np.sqrt(np.float32(D)))
    with ExitStack() as ctx:
        sb = lambda s, shape: ctx.enter_context(nc.sbuf_tensor(f"{nm}_{s}", shape, F32))
        ps = lambda s, shape: ctx.enter_context(nc.psum_tensor(f"{nm}_{s}", shape, F32))
        sem = ctx.enter_context(stage(nc, m, nm))
        stats, ln = sb("stats", [P, NT, 6]), sb("ln", [P, 9, NT])
        xn, xnT, ctm = sb("xn", [P, TB, D]), sb("xnT", [P, 512]), sb("ctm", [P, S2])
        KT, G, V, Vr = sb("KT", [P, S2]), sb("G", [P, S2]), sb("V", [P, D]), sb("Vr", [KR, D])
        bqr, nmx, rs, rin = sb("bqr", [P, P]), sb("nmx", [P, TB]), sb("rs", [P, TB]), sb("rin", [P, TB])
        nms = sb("nms", [P, TB])
        pr = sb("pr", [P, TB, S2])
        PT, PTr, OT = sb("PT", [P, 512]), sb("PTr", [KR, 512]), sb("OT", [P, 512])
        psX, psK, psS = ps("psX", [P, 512]), ps("psK", [P, 512]), ps("psS", [P, 2, 512])
        psP, psPr, psO, psY = ps("psP", [P, 512]), ps("psPr", [P, 512]), ps("psO", [P, 512]), ps("psY", [P, 512])
        own_v, var_ready, std_ready = sem("own_v"), sem("var_ready"), sem("std_ready")
        xn_ready, x_full, xt_done, k_full, k_done = sem("xn_ready"), sem("x_full"), sem("xt_done"), sem("k_full"), sem("k_done")
        s_full, m_ready, e_ready, p_ready = sem("s_full"), sem("m_ready"), sem("e_ready"), sem("p_ready")
        p_full, pt_done, o_full, ot_done, y_full, y_done = (
            sem("p_full"), sem("pt_done"), sem("o_full"), sem("ot_done"), sem("y_full"), sem("y_done"))
        block = ctx.enter_context(nc.Block())

        @block.sync
        def _(sp):
            clear_last(m, sp)

        @block.scalar
        def _(act):
            act.wait_ge(var_ready, 1)
            nc.scalar.activation(ln[:, 8], ln[:, 7], ACT.Sqrt).then_inc(std_ready, 1)
            with act.Fori(0, B) as b:
                act.wait_ge(x_full, b + 1)
                nc.scalar.copy(xnT[:], psX[:]).then_inc(xt_done, 1)
                act.wait_ge(k_full, b * 2 + 1)
                nc.scalar.copy(KT[:], psK[:, 0:S2]).then_inc(k_done, 1)
                nc.scalar.copy(V[:], psK[:, 160:160 + D]).then_inc(k_done, 1)
                nc.scalar.copy(Vr[:], psK[0:KR, 288:288 + D]).then_inc(k_done, 1)
                act.wait_ge(k_full, b * 2 + 2)
                nc.scalar.copy(G[:], psK[:, 0:S2]).then_inc(k_done, 1)
                act.wait_ge(m_ready, b + 1)
                for t in range(TB):
                    nc.scalar.activation(pr[:, t], psS[:, t // 2, (t % 2) * S2:(t % 2 + 1) * S2], ACT.Exp, scale=SC,
                                         bias=nms[:, t:t + 1], accum_out=rs[:, t:t + 1]).then_inc(e_ready, 1)
                act.wait_ge(p_full, b + 1)
                nc.scalar.copy(PT[:], psP[:]).then_inc(pt_done, 1)
                nc.scalar.copy(PTr[:], psPr[0:KR]).then_inc(pt_done, 1)
                act.wait_ge(o_full, b + 1)
                nc.scalar.copy(OT[:], psO[:]).then_inc(ot_done, 1)

        @block.tensor
        def _(pe):
            with pe.Fori(0, B) as b:
                pe.wait_ge(xn_ready, b + 1)
                for t in range(TB):
                    last = pe.transpose(psX[:, t * P:(t + 1) * P], xn[:, t], m.ident)
                last.then_inc(x_full, 1)
                pe.matmul(psK[:, 0:S2], w["L3_xattn_Wk"][:], ctm[:], start=True, stop=True, skip_group_check=True)
                pe.matmul(psK[:, 160:160 + D], ctm[:, 0:KM_], w["L3_xattn_Wv"][:], start=False, stop=False, skip_group_check=True)
                pe.matmul(psK[:, 160:160 + D], m.ones[0:1, :], m.row("L3_xattn_bv"), start=False, stop=True, skip_group_check=True)
                pe.matmul(psK[0:KR, 288:288 + D], ctm[:, KM_:S2], w["L3_xattn_Wv"][:], start=False, stop=False, skip_group_check=True)
                pe.matmul(psK[0:KR, 288:288 + D], m.ones[0:1, 0:KR], m.row("L3_xattn_bv"), start=False, stop=True,
                          skip_group_check=True).then_inc(k_full, 1)
                pe.wait_ge(k_done, b * 4 + 3)
                pe.matmul(psK[:, 0:S2], w["L3_xattn_Wq"][:], KT[:], start=True, stop=True).then_inc(k_full, 1)
                pe.wait_ge(k_done, b * 4 + 4)
                pe.wait_ge(xt_done, b + 1)
                for t in range(TB):
                    o = psS[:, t // 2, (t % 2) * S2:(t % 2 + 1) * S2]
                    pe.matmul(o, xnT[:, t * P:(t + 1) * P], G[:], start=(t % 2 == 0), stop=False, skip_group_check=True)
                    pe.matmul(o, bqr[:], KT[:], start=False, stop=True, skip_group_check=True).then_inc(s_full, 1)
                pe.wait_ge(p_ready, b + 1)
                for t in range(TB):
                    pe.transpose(psP[:, t * P:(t + 1) * P], pr[:, t, 0:KM_], m.ident)
                for t in range(TB):
                    last = pe.transpose(psPr[0:KR, t * P:(t + 1) * P], pr[:, t, KM_:S2], m.ident)
                last.then_inc(p_full, 1)
                pe.wait_ge(pt_done, b * 2 + 2)
                pe.matmul(psO[:], V[:], PT[:], start=True, stop=False)
                pe.matmul(psO[:], Vr[:], PTr[:], start=False, stop=True).then_inc(o_full, 1)
                pe.wait_ge(ot_done, b + 1)
                for t in range(TB):
                    o = psY[:, t * P:(t + 1) * P]
                    pe.matmul(o, OT[:, t * P:(t + 1) * P], w["L3_xattn_Wo"][:], start=(t == 0), stop=False, skip_group_check=True)
                    last = pe.matmul(o, m.ones[0:1, :], m.row("L3_xattn_bo"), start=False, stop=(t == TB - 1), skip_group_check=True)
                last.then_inc(y_full, 1)

        @block.vector
        def _(dve):
            own = Own(dve, own_v)
            own.done(nc.vector.tensor_copy(bqr[:], m.col("L3_xattn_bq").broadcast_to([P, P])))
            ln_stats_vector(nc, dve, own, stats, ln, m.X, var_ready, std_ready)
            with dve.Fori(0, B) as b:
                own.loop(b, 7)
                for t in range(TB):
                    tt = b * TB + t
                    own.done(nc.vector.tensor_scalar(xn[:, t], m.X[:, bass.ds(tt, 1), :].rearrange("p o d -> p (o d)"),
                                                     ln[:, 0, bass.ds(tt, 1)], ln[:, 1, bass.ds(tt, 1)], ALU.subtract, ALU.mult))
                own.wait()
                nc.vector.tensor_copy(ctm[:], m.ctxT[:, bass.ds(b, 1), :].rearrange("p o k -> p (o k)")).then_inc(xn_ready, 1)
                dve.wait_ge(s_full, b * TB + TB)
                own.done(nc.vector.tensor_reduce(nmx[:].rearrange("p (a t) -> p a t", a=2),
                                                 psS[:, :, 0:2 * S2].rearrange("p a (t k) -> p a t k", k=S2), AX_X, ALU.max))
                own.wait()
                nc.vector.tensor_scalar(nms[:], nmx[:], -SC, None, ALU.mult).then_inc(m_ready, 1)
                dve.wait_ge(e_ready, b * TB + TB)
                own.done(nc.vector.reciprocal(rin[:], rs[:]))
                own.wait()
                own.done(nc.vector.tensor_tensor(pr[:], pr[:], rin[:].unsqueeze(2).broadcast_to([P, TB, S2]), ALU.mult))
                own.wait()
                nc.vector.memset(stats[:, 0, 0:1], 0.0).then_inc(p_ready, 1)
                dve.wait_ge(y_full, b + 1)
                x = m.X[:, bass.ds(b * TB, TB), :].rearrange("p t d -> p (t d)")
                nc.vector.scalar_tensor_tensor(x, psY[:], m.gate(3), x, ALU.mult, ALU.add).then_inc(y_done, 1)
                dve.wait_ge(y_done, b + 1)
                own.end(B)


def self_attention(nc, m, d):
    nm, w = "L3s", m.w
    BF = mybir.dt.bfloat16
    DH = D // H
    TR = 9 * DH
    SC = 1.0 / float(np.sqrt(8.0))
    parts_d = nc.dram_tensor("qk_parts", (2, 3, P, NT * P), BF).ap()
    max_d = nc.dram_tensor("max_parts", (B, 3, H, S), BF).ap()
    with ExitStack() as ctx0:
        V = ctx0.enter_context(nc.sbuf_tensor(f"{nm}_V", [P, NT, H, DH + 1], F32))
        with ExitStack() as ctx:
            sb = lambda s, shape, dt=F32: ctx.enter_context(nc.sbuf_tensor(f"{nm}_{s}", shape, dt))
            sem = ctx.enter_context(stage(nc, m, nm))
            C = NT // TB
            ps = ctx.enter_context(nc.psum_tensor(f"{nm}_psP", [P, 2, 512], F32))
            psV = ctx.enter_context(nc.psum_tensor(f"{nm}_psV", [P, 2, 512], F32))
            parts = sb("parts", [P, 2, 3, NT * P], BF)
            full, rest = sb("full", [P, 2, 512]), sb("rest", [P, 2, 512])
            qb = sb("qb", [P, 1])
            qb_ready, p_full, f_ready, hi_ready = sem("qb_ready"), sem("p_full"), sem("f_ready"), sem("hi_ready")
            r_ready, mid_ready, lo_ready = sem("r_ready"), sem("mid_ready"), sem("lo_ready")
            v_full, v_done, stored = sem("v_full"), sem("v_done"), sem("stored")
            block = ctx.enter_context(nc.Block())

            @block.tensor
            def _(pe):
                for k in range(2):
                    for c in range(C):
                        n = k * C + c
                        if n >= 2:
                            pe.wait_ge(f_ready, n - 1)
                        pe.matmul(ps[:, n % 2], w["L3_ffn_q_w" if k == 0 else "L3_ffn_k_w"][:], m.XT[:, c * 512:(c + 1) * 512],
                                  start=True, stop=True).then_inc(p_full, 1)
                for c in range(C):
                    if c >= 2:
                        pe.wait_ge(v_done, c - 1)
                    for t in range(TB):
                        o = psV[:, c % 2, t * P:(t + 1) * P]
                        tt = c * TB + t
                        pe.matmul(o, m.XT[:, tt * P:(tt + 1) * P], w["L3_ffn_v_w"][:], start=(t == 0), stop=False, skip_group_check=True)
                        last = pe.matmul(o, m.ones[0:1, :], m.row("L3_ffn_v_b"), start=False, stop=(t == TB - 1), skip_group_check=True)
                    last.then_inc(v_full, 1)

            @block.scalar
            def _(act):
                act.wait_ge(qb_ready, 1)
                for k in range(2):
                    for c in range(C):
                        n = k * C + c
                        cs = slice(c * 512, (c + 1) * 512)
                        act.wait_ge(p_full, n + 1)
                        if n >= 2:
                            act.wait_ge(r_ready, n - 1)
                        if k == 0:
                            nc.scalar.activation(full[:, n % 2], ps[:, n % 2], ACT.Identity, scale=SC, bias=qb[:]).then_inc(f_ready, 1)
                        else:
                            nc.scalar.activation(full[:, n % 2], ps[:, n % 2], ACT.Identity, bias=m.col("L3_ffn_k_b")).then_inc(f_ready, 1)
                        act.wait_ge(f_ready, n + 1)
                        nc.scalar.copy(parts[:, k, 0, cs], full[:, n % 2]).then_inc(hi_ready, 1)
                        act.wait_ge(r_ready, n + 1)
                        nc.scalar.copy(parts[:, k, 1, cs], rest[:, n % 2]).then_inc(mid_ready, 1)
                for c in range(C):
                    act.wait_ge(v_full, c + 1)
                    nc.scalar.copy(V[:, c * TB:(c + 1) * TB, :, 0:DH],
                                   psV[:, c % 2].rearrange("p (t h d) -> p t h d", h=H, d=DH)).then_inc(v_done, 1)

            @block.vector
            def _(dve):
                nc.vector.tensor_scalar(qb[:], m.col("L3_ffn_q_b"), SC, None, ALU.mult).then_inc(qb_ready, 1)
                nc.vector.memset(V[:, :, :, DH:DH + 1], 1.0)
                for k in range(2):
                    for c in range(C):
                        n = k * C + c
                        cs = slice(c * 512, (c + 1) * 512)
                        dve.wait_ge(hi_ready, n + 1)
                        if n >= 2:
                            dve.wait_ge(lo_ready, n - 1)
                        nc.vector.tensor_tensor(rest[:, n % 2], full[:, n % 2], parts[:, k, 0, cs], ALU.subtract).then_inc(r_ready, 1)
                        dve.wait_ge(mid_ready, n + 1)
                        nc.vector.tensor_tensor(parts[:, k, 2, cs], rest[:, n % 2], parts[:, k, 1, cs], ALU.subtract).then_inc(lo_ready, 1)

            @block.sync
            def _(sp):
                clear_last(m, sp)
                for k in range(2):
                    sp.wait_ge(lo_ready, (k + 1) * C)
                    sp.dma_start(parts_d[k].rearrange("s p t -> p s t"), parts[:, k]).then_inc(stored, 16)
                sp.wait_ge(stored, 32)

        with ExitStack() as ctx:
            sb = lambda s, shape, dt=F32: ctx.enter_context(nc.sbuf_tensor(f"{nm}_{s}", shape, dt))
            ps = lambda s, shape: ctx.enter_context(nc.psum_tensor(f"{nm}_{s}", shape, F32))
            sem = ctx.enter_context(stage(nc, m, nm))
            QS, KS = sb("QS", [TR + 3, 2, H, S], BF), sb("KS", [TR + 3, 2, H, S], BF)
            identb, trilb, triub = sb("identb", [P, P], BF), sb("trilb", [P, P], BF), sb("triub", [P, P], BF)
            onesb = sb("onesb", [3, H, S], BF)
            mx, mr = sb("mx", [P, TB, H]), sb("mr", [P, 2, TB, H])
            mparts = sb("mparts", [P, TB, 3, H], BF)
            MT = sb("MT", [3 * H, S], BF)
            E = sb("E", [P, 2, TB, S])
            On, rin, OT = sb("On", [P, TB, H, DH]), sb("rin", [P, TB, 1]), sb("OT", [P, S])
            psS, psT, psO, psM = ps("psS", [P, 2, 512]), ps("psT", [P, 3, 512]), ps("psO", [P, 2, 512]), ps("psM", [P, 512])
            own_v, const_ready = sem("own_v2"), sem("const_ready")
            ones_in, stack_in, max_out, max_in = sem("ones_in"), [sem(f"stack_in{u}") for u in range(2)], sem("max_out"), sem("max_in")
            s_full, s_free, t_full, t_free = sem("s_full"), sem("s_free"), sem("t_full"), sem("t_free")
            o_full, o_free, m_full, m_free = sem("o_full"), sem("o_free"), sem("m_full"), sem("m_free")
            mp_ready, on_done = sem("mp_ready"), sem("on_done")
            block = ctx.enter_context(nc.Block())
            SG = [[3], [2, 0], [1]]
            TG = [[0], [1, 3], [2]]
            ND = 18 * 16

            def place(group, width):
                at, out = 0, []
                for t in group:
                    out.append((t, at, width(t)))
                    at += width(t)
                return out

            def over_heads(eng, step):
                step(0, 0)
                with eng.Fori(0, (H - 2) // 2) as i:
                    step(i * 2 + 1, 1)
                    step(i * 2 + 2, 0)
                step(H - 1, 1)

            @block.sync
            def _(sp):
                clear_last(m, sp)
                def stacks(b):
                    u, cols = b % 2, slice(b * S, (b + 1) * S)
                    for i in range(3):
                        for j in range(3):
                            rows = slice((3 * i + j) * DH, (3 * i + j + 1) * DH)
                            for k, st, part in ((0, QS, i), (1, KS, j)):
                                sp.dma_start(st[rows, u], parts_d[k, part].rearrange("(h d) t -> d h t", d=DH)[:, :, cols]
                                             ).then_inc(stack_in[u], 16)

                stacks(0)
                stacks(1)
                sp.wait_ge(const_ready, 1)
                for u in range(2):
                    sp.dma_start(KS[TR:TR + 3, u], onesb[:]).then_inc(ones_in, 16)
                for b in range(B):
                    sp.wait_ge(m_free, 1 + (1 if b == 0 else 1 + 3 * b - 2))
                    sp.dma_start(max_d[b].rearrange("s h t -> (s h) t"), MT[:]).then_inc(max_out, 16)
                    sp.wait_ge(max_out, 16 * (b + 1))
                    sp.dma_start(QS[TR:TR + 3, b % 2], max_d[b]).then_inc(max_in, 16)
                    if 1 <= b and b + 1 < B:
                        sp.wait_ge(t_full, 3 * H * b)
                        stacks(b + 1)

            @block.tensor
            def _(pe):
                pe.sem_inc(s_free, 2)
                pe.sem_inc(t_free, 3)
                pe.sem_inc(o_free, 2)
                pe.sem_inc(m_free, 1)
                pe.wait_ge(const_ready, 1)

                def scores(b, h, par):
                    g, u = h + b * H, b % 2
                    for k, group in enumerate(SG):
                        pe.wait_ge(s_free, g * 3 + (k + 1))
                        bank = (3 * par + k) % 2
                        tiles = place(group, lambda t: (t + 1) * P)
                        for n, (t, at, wd) in enumerate(tiles):
                            pe.matmul(psS[:, bank, at:at + wd], QS[0:TR, u, hd(h), t * P:(t + 1) * P], KS[0:TR, u, hd(h), 0:wd],
                                      start=(n == 0), stop=False, skip_group_check=True)
                            last = pe.matmul(psS[:, bank, at + wd - P:at + wd], identb[:], trilb[:], start=False,
                                             stop=(n == len(tiles) - 1), skip_group_check=True)
                        last.then_inc(s_full, 1)

                def shifted(b, h, par):
                    g, u = h + b * H, b % 2
                    for k, group in enumerate(TG):
                        pe.wait_ge(t_free, g * 3 + (k + 1))
                        tiles = place(group, lambda t: (TB - t) * P)
                        for n, (t, at, wd) in enumerate(tiles):
                            pe.matmul(psT[:, k, at:at + wd], KS[0:TR + 3, u, hd(h), t * P:(t + 1) * P], QS[0:TR + 3, u, hd(h), t * P:S],
                                      start=(n == 0), stop=False, skip_group_check=True)
                            last = pe.matmul(psT[:, k, at:at + P], identb[:], triub[:], start=False,
                                             stop=(n == len(tiles) - 1), skip_group_check=True)
                        last.then_inc(t_full, 1)

                def values(b, h, par):
                    g = h + b * H
                    pe.wait_ge(t_free, g * 3 + 6)
                    pe.wait_ge(o_free, g + 1)
                    for i in range(TB):
                        for j in range(i + 1):
                            last = pe.matmul(psO[:, par, i * (DH + 1):(i + 1) * (DH + 1)], E[:, par, j, i * P:(i + 1) * P],
                                             V[:, b * TB + j, hd(h)].rearrange("p o d -> p (o d)") if not isinstance(h, int) else V[:, b * TB + j, h],
                                             start=(i == 0 and j == 0), stop=(i == TB - 1 and j == i), skip_group_check=True)
                    last.then_inc(o_full, 1)

                uses = [0]

                def bank():
                    uses[0] += 1
                    pe.wait_ge(m_free, uses[0])

                def turn_maxima(b):
                    pe.wait_ge(mp_ready, b + 1)
                    bank()
                    for t in range(TB):
                        last = pe.transpose(psM[0:3 * H].bitcast(BF)[:, t * P:(t + 1) * P], mparts[:, t].rearrange("p s h -> p (s h)"), identb[:])
                    last.then_inc(m_full, 1)

                pe.wait_ge(stack_in[0], ND)
                over_heads(pe, lambda h, par: scores(0, h, par))
                turn_maxima(0)
                pe.wait_ge(ones_in, 32)
                for b in range(B):
                    nxt = b + 1 < B
                    if nxt:
                        pe.wait_ge(stack_in[(b + 1) % 2], ND * ((b + 1) // 2 + 1))
                    pe.wait_ge(max_in, 16 * (b + 1))

                    def step(h, par):
                        if nxt:
                            scores(b + 1, h, par)
                        shifted(b, h, par)
                        if not (isinstance(h, int) and h == 0):
                            values(b, h - 1 if isinstance(h, int) else h + (-1), 1 - par)

                    over_heads(pe, step)
                    values(b, H - 1, 1)
                    if nxt:
                        turn_maxima(b + 1)
                    pe.wait_ge(o_free, (b + 1) * H + 2)
                    bank()
                    for t in range(TB):
                        last = pe.transpose(psM[:, t * P:(t + 1) * P], On[:, t].rearrange("p h d -> p (h d)"), m.ident)
                    last.then_inc(m_full, 1)
                    bank()
                    for t in range(TB):
                        o = psM[:, t * P:(t + 1) * P]
                        pe.matmul(o, OT[:, t * P:(t + 1) * P], w["L3_ffn_o_w"][:], start=(t == 0), stop=False, skip_group_check=True)
                        last = pe.matmul(o, m.ones[0:1, :], m.row("L3_ffn_o_b"), start=False, stop=(t == TB - 1), skip_group_check=True)
                    last.then_inc(m_full, 1)

            @block.scalar
            def _(act):
                uses = [0]

                def bank():
                    uses[0] += 1
                    act.wait_ge(m_full, uses[0])

                def turn_maxima(b):
                    bank()
                    if b >= 1:
                        act.wait_ge(max_out, 16 * b)
                    nc.scalar.copy(MT[:], psM[0:3 * H].bitcast(BF)[:, 0:S]).then_inc(m_free, 1)

                turn_maxima(0)
                for b in range(B):
                    def step(h, par):
                        g = h + b * H
                        act.wait_ge(o_free, g + 1)
                        for k, group in enumerate(TG):
                            act.wait_ge(t_full, g * 3 + (k + 1))
                            tiles = place(group, lambda t: (TB - t) * P)
                            for t, at, wd in tiles:
                                last = nc.scalar.activation(E[:, par, t, t * P:S], psT[:, k, at:at + wd], ACT.Exp)
                            last.then_inc(t_free, 1)

                    over_heads(act, step)
                    if b + 1 < B:
                        turn_maxima(b + 1)
                    bank()
                    nc.scalar.copy(OT[:], psM[:]).then_inc(m_free, 1)
                    uses[0] += 1

            @block.vector
            def _(dve):
                own = Own(dve, own_v)
                own.done(nc.vector.memset(onesb[:], 1.0))
                own.done(nc.vector.tensor_copy(identb[:], m.ident))
                own.done(nc.vector.tensor_copy(trilb[:], m.const["tril"]))
                own.wait()
                nc.vector.tensor_copy(triub[:], m.const["triu"]).then_inc(const_ready, 1)

                def maxima(b, h, par):
                    g = h + b * H
                    for k, group in enumerate(SG):
                        dve.wait_ge(s_full, g * 3 + (k + 1))
                        for t, at, wd in place(group, lambda t: (t + 1) * P):
                            last = nc.vector.tensor_reduce(mx[:, t, hd(h)], psS[:, (3 * par + k) % 2, at:at + wd], AX_X, ALU.max)
                        last.then_inc(s_free, 1)

                def cut_maxima(b):
                    dve.wait_ge(s_free, (b + 1) * H * 3 + 2)
                    if b >= 1:
                        dve.wait_ge(m_full, 1 if b == 1 else 3 * (b - 1))
                    own.done(nc.vector.tensor_scalar(mr[:, 0], mx[:], -1.0, None, ALU.mult))
                    own.wait()
                    own.done(nc.vector.tensor_copy(mparts[:, :, 0], mr[:, 0]))
                    own.wait()
                    own.done(nc.vector.tensor_tensor(mr[:, 1], mr[:, 0], mparts[:, :, 0], ALU.subtract))
                    own.wait()
                    own.done(nc.vector.tensor_copy(mparts[:, :, 1], mr[:, 1]))
                    own.wait()
                    nc.vector.tensor_tensor(mparts[:, :, 2], mr[:, 1], mparts[:, :, 1], ALU.subtract).then_inc(mp_ready, 1)
                    dve.wait_ge(mp_ready, b + 1)

                def divide(b, h, par):
                    g = h + b * H
                    out = psO[:, par, 0:TB * (DH + 1)].rearrange("p (t d) -> p t d", d=DH + 1)
                    dve.wait_ge(o_full, g + 1)
                    dve.wait_ge(o_free, g + 2)
                    nc.vector.reciprocal(rin[:], out[:, :, DH:DH + 1]).then_inc(on_done, 1)
                    dve.wait_ge(on_done, g + 1)
                    o = On[:, :, hd(h), :].rearrange("p t o d -> p t (o d)") if not isinstance(h, int) else On[:, :, h, :]
                    nc.vector.tensor_tensor(o, out[:, :, 0:DH], rin[:].broadcast_to([P, TB, DH]), ALU.mult).then_inc(o_free, 1)

                over_heads(dve, lambda h, par: maxima(0, h, par))
                cut_maxima(0)
                for b in range(B):
                    def step(h, par):
                        if b + 1 < B:
                            maxima(b + 1, h, par)
                        if not (isinstance(h, int) and h == 0):
                            divide(b, h - 1 if isinstance(h, int) else h + (-1), 1 - par)

                    over_heads(dve, step)
                    divide(b, H - 1, 1)
                    if b + 1 < B:
                        cut_maxima(b + 1)
                    dve.wait_ge(m_full, 3 * (b + 1) + (1 if b + 1 < B else 0))
                    x = m.XN[:, b * TB:(b + 1) * TB].rearrange("p t d -> p (t d)")
                    nc.vector.tensor_tensor(x, x, psM[:], ALU.add).then_inc(m_free, 1)


def hd(h):
    return slice(h, h + 1) if isinstance(h, int) else bass.ds(h, 1)


def stage_list(nc, m, d, upto):
    w = m.w

    def share(E, split):
        return lambda i, U, u, q, t: m.comb[:, t, bass.ds(i * (U * split) + (u * split + q), 1)]

    attention(nc, m, dict(name="L0", dv=8, tiles=range(TB), mode="bias", gate=0, weights=[],
                          wq=w["L0_xattn_Wq"][:], wk=w["L0_xattn_Wk"][:], wv=w["L0_xattn_Wv"][:],
                          wo=w["L0_xattn_Wo"][:].unsqueeze(1)))
    norm_transpose(nc, m, "L0n1", m.X1, m.XN, m.col("L0_xattn_g1"), m.col("L0_xattn_be1"))
    experts(nc, m, "L0h", dict(w1=d["L0_xattn_W1"].unsqueeze(0), w2=d["L0_xattn_W2"].unsqueeze(0), act=ACT.Gelu,
                               b1=d["L0_xattn_b1"].unsqueeze(0), b2=lambda i, U, u: m.row("L0_xattn_b2"),
                               dst=m.X1, share=lambda *a: m.ones[:, 0:1]))
    norm_transpose(nc, m, "L0n2", m.X1, m.XN, turn=False)
    add_layer(nc, m, "L0a", m.XN, 0, m.wide("L0_xattn_g2"), m.wide("L0_xattn_be2"))
    if upto == 0: return
    norm_transpose(nc, m, "L0r", m.X, m.XN, router=dict(E=8, kind="L0", w=w["L0_ffn_Wr"][:], gate=4, comb=m.comb[:, :, 0:8]))
    m.slots_in, m.slots_out = m.slots0, nc.dram_tensor("results0", (8 * CAP0, D), F32).ap()
    routed_experts(nc, m, "L0f", dict(w1=d["L0_ffn_W1"], w3=d["L0_ffn_W3"], w2=d["L0_ffn_W2"], act=ACT.Silu, rows=m.XN,
                                      U=2, chunks=[3, 2], before=0))
    if upto == 1: return
    attention(nc, m, dict(name="L1", dv=64, tiles=range(TB), mode="mask", gate=1, weights=[],
                          wq=w["L1_xattn_W_Q"][:], wk=w["L1_xattn_W_K"][:], wv=w["L1_xattn_W_V"][:],
                          wo=w["L1_xattn_W_O"][:]))
    if upto == 2: return
    norm_transpose(nc, m, "L1r", m.X, m.XN, router=dict(E=16, kind="L1", w=w["L1_ffn_router_w"][:], gate=5, comb=m.comb[:]))
    experts(nc, m, "L1s", dict(w1=d["L1_ffn_sh_gate"], w3=d["L1_ffn_sh_up"], w2=d["L1_ffn_sh_down"], act=ACT.Silu,
                               dst=m.X, share=lambda *a: m.gate(5)))
    experts(nc, m, "L1f", dict(w1=d["L1_ffn_gate_proj"], w3=d["L1_ffn_up_proj"], w2=d["L1_ffn_down_proj"], act=ACT.Silu,
                               dst=m.X, share=share(16, 2), split=2))
    if upto == 3: return
    attention(nc, m, dict(name="L2", dv=8, tiles=[2, 3], mode="causal", gate=2, weights=[],
                          wq=w["L2_xattn_Wq"][:], wk=w["L2_xattn_Wk"][:], wv=w["L2_xattn_Wv"][:],
                          wo=w["L2_xattn_Wo"][:].unsqueeze(1)))
    if upto == 4: return
    norm_transpose(nc, m, "L2r", m.X, m.XN, router=dict(E=8, kind="L2", w=w["L2_ffn_Wr"][:], gate=6, comb=m.comb[:, :, 0:8]))
    experts(nc, m, "L2f", dict(w1=d["L2_ffn_W1"], w2=d["L2_ffn_W2"], act=ACT.Silu, dst=m.X, share=share(8, 1)))
    if upto == 5: return
    single_head(nc, m)
    if upto == 6: return
    norm_transpose(nc, m, "L3n0", m.X, m.XN, turn=False)
    norm_transpose(nc, m, "L3n1", m.XN, m.X1, m.col("L3_ffn_ln1_w"), m.col("L3_ffn_ln1_b"))
    self_attention(nc, m, d)
    norm_transpose(nc, m, "L3r", m.XN, m.X1, m.col("L3_ffn_ln2_w"), m.col("L3_ffn_ln2_b"),
                   router=dict(E=16, kind="L3", w=w["L3_ffn_router_w"][:], gate=7, comb=m.comb[:]))
    add_layer(nc, m, "L3a", m.XN, 7)
    m.slots_in, m.slots_out = m.slots3, nc.dram_tensor("results3", (16 * CAP3, D), F32).ap()
    routed_experts(nc, m, "L3f", dict(w1=d["L3_ffn_fc1_w"], w2=d["L3_ffn_fc2_w"], b1=d["L3_ffn_fc1_b"], b2=d["L3_ffn_fc2_b"],
                                      act=ACT.Gelu, rows=m.X1, scale=m.col("L3_ffn_ln2_w"), bias=m.col("L3_ffn_ln2_b"),
                                      U=4, chunks=[2], before=1))


def _t(a):
    return a.T


INPUTS = {
    "x": lambda a: a.reshape(NT, P, D),
    "ctx_1024": lambda a: a.transpose(2, 0, 1),
    "fside_Bx16xSxS2_0": lambda a: a,
    "mask_1x1xSxS2_ik0": lambda a: a.reshape(S, S2),
    "g_xattn": lambda a: a.reshape(1, 4),
    "g_ffn": lambda a: a.reshape(1, 4),
    "L0_xattn_Wq": lambda a: a, "L0_xattn_Wk": _t, "L0_xattn_Wv": _t, "L0_xattn_Wo": _t,
    "L0_xattn_W1": _t, "L0_xattn_b1": lambda a: a.reshape(4, P).T, "L0_xattn_W2": lambda a: a.T.reshape(4, P, D).transpose(1, 0, 2),
    "L0_ffn_Wr": lambda a: a, "L0_ffn_W1": lambda a: a, "L0_ffn_W3": lambda a: a,
    "L0_ffn_W2": lambda a: a.reshape(8, 4, P, D).transpose(0, 2, 1, 3),
    "L1_xattn_W_Q": lambda a: a.T.reshape(8, P, D).transpose(1, 0, 2), "L1_xattn_W_K": lambda a: a,
    "L1_xattn_W_V": lambda a: a, "L1_xattn_W_O": lambda a: a.reshape(8, P, D).transpose(1, 0, 2),
    "L1_ffn_router_w": _t,
    "L1_ffn_router_bias": lambda a: a.reshape(1, 16),
    "L1_ffn_up_proj": lambda a: a.reshape(8, 2, D, 64).transpose(0, 2, 1, 3).reshape(8, D, P),
    "L1_ffn_gate_proj": lambda a: a.reshape(8, 2, D, 64).transpose(0, 2, 1, 3).reshape(8, D, P),
    "L1_ffn_down_proj": lambda a: a.reshape(8, P, 1, D),
    "L1_ffn_sh_gate": lambda a: a.T.reshape(1, D, P), "L1_ffn_sh_up": lambda a: a.T.reshape(1, D, P),
    "L1_ffn_sh_down": lambda a: a.T.reshape(1, P, 1, D),
    "L2_xattn_Wq": _t, "L2_xattn_Wk": lambda a: a, "L2_xattn_Wv": lambda a: a, "L2_xattn_Wo": lambda a: a,
    "L2_ffn_Wr": _t, "L2_ffn_W1": lambda a: a, "L2_ffn_W2": lambda a: a.reshape(8, 4, P, D).transpose(0, 2, 1, 3),
    "L3_xattn_Wk": _t, "L3_xattn_Wv": _t, "L3_xattn_Wq": lambda a: a, "L3_xattn_Wo": _t,
    "L3_ffn_q_w": lambda a: a, "L3_ffn_k_w": lambda a: a, "L3_ffn_v_w": lambda a: a, "L3_ffn_o_w": lambda a: a,
    "L3_ffn_router_w": lambda a: a, "L3_ffn_fc1_w": lambda a: a,
    "L3_ffn_fc1_b": lambda a: a.reshape(16, 4, P).transpose(0, 2, 1),
    "L3_ffn_fc2_w": lambda a: a.reshape(16, 4, P, D).transpose(0, 2, 1, 3),
    "L3_ffn_fc2_b": lambda a: a.reshape(16, 1, D),
}
KEPT = ["L0_xattn_Wk", "L0_xattn_Wv", "L0_xattn_Wq", "L0_xattn_Wo", 
        "L0_ffn_Wr", "L1_xattn_W_Q", "L1_xattn_W_K", "L1_xattn_W_V", "L1_xattn_W_O", "L1_ffn_router_w",
        "L2_xattn_Wq", "L2_xattn_Wk", "L2_xattn_Wv", "L2_xattn_Wo", "L2_ffn_Wr",
        "L3_xattn_Wk", "L3_xattn_Wv", "L3_xattn_Wq", "L3_xattn_Wo",
        "L3_ffn_q_w", "L3_ffn_k_w", "L3_ffn_v_w", "L3_ffn_o_w", "L3_ffn_router_w"]


def setup(nc, ctx, m, d):
    sb = lambda s, shape: ctx.enter_context(nc.sbuf_tensor(s, shape, F32))
    m.X, m.XN, m.X1, m.XT = (sb(s, [P, NT, D]) for s in ("X", "XN", "X1", "XT"))
    m.XT3 = m.XT
    m.XT = m.XT[:].rearrange("p t d -> p (t d)")
    const = sb("const", list(CONSTS.shape))
    m.const = {}
    for name, (at, w) in CONST.items():
        m.const[name] = const[:, at:at + w]
    m.ident, m.ones, m.first, m.rest = (m.const[k] for k in ("ident", "ones", "first", "rest"))
    m.head8, m.head64 = m.const["head8"], m.const["head64"]
    m.causal = [m.const["causal%d" % i] for i in range(TB)]
    rows, cols = sb("rows", [P, len(ROWS), D]), sb("cols", [P, len(COLS)])
    m.row = lambda s: rows[0:1, ROWS.index(s), :]
    m.wide = lambda s: rows[:, ROWS.index(s), :]
    m.col = lambda s: cols[:, COLS.index(s):COLS.index(s) + 1]
    gates = sb("gates", [P, 8])
    m.gate = lambda k: gates[:, k:k + 1]
    m.ctxT = sb("ctxT", [P, B, S2])
    m.comb = sb("comb", [P, NT, 16])
    m.slot_share = sb("slot_share", [P, 2, NT])
    m.slot_to, m.slot_from = (ctx.enter_context(nc.sbuf_tensor(s, [P, 2, NT], I32)) for s in ("slot_to", "slot_from"))
    m.slots0, m.slots3 = nc.dram_tensor("slots0", (8 * CAP0, D), F32).ap(), nc.dram_tensor("slots3", (16 * CAP3, D), F32).ap()
    m.scattered = ctx.enter_context(nc.semaphore("scattered"))
    m.gathered = [ctx.enter_context(nc.semaphore(f"gathered{g}")) for g in range(TB)]
    m.zeroed = ctx.enter_context(nc.semaphore("zeroed"))
    zeros, zeros_ready = sb("zeros", [P, 512]), ctx.enter_context(nc.semaphore("zeros_ready"))
    m.w = {}
    for k in KEPT:
        shape = list(d[k].shape)
        m.w[k] = sb("w_" + k, shape)
    rb = sb("router_bias", [P, 16])
    m.router_bias = rb
    loaded, gates_in = ctx.enter_context(nc.semaphore("loaded")), ctx.enter_context(nc.semaphore("gates_in"))
    tanh_done = ctx.enter_context(nc.semaphore("tanh_done"))
    with nc.Block() as block:
        @block.sync
        def _(sp):
            clear_last(m, sp)
            n = 0
            for dst, src in [(const[:], d["consts"]), (cols[:], d["cols"]), (m.ctxT[:], d["ctx_1024"]),
                             (m.X[:], d["x"].rearrange("t p d -> p t d"))]:
                sp.dma_start(dst, src).then_inc(loaded, 16)
                n += 16
            sp.dma_start(rows[:], d["rows"].unsqueeze(0).broadcast_to([P, len(ROWS), D])).then_inc(loaded, 16)
            sp.dma_start(rb[:], d["L1_ffn_router_bias"].broadcast_to([P, 16])).then_inc(loaded, 16)
            n += 32
            for k in KEPT:
                sp.dma_start(m.w[k][:], d[k]).then_inc(loaded, 16)
                n += 16
            sp.wait_ge(loaded, n)

        @block.vector
        def _(dve):
            nc.vector.memset(zeros[:], 0.0).then_inc(zeros_ready, 1)

        @block.gpsimd
        def _(pool):
            pool.wait_ge(zeros_ready, 1)
            for table in (m.slots0, m.slots3):
                r = table.shape[0] * D // P // 512
                pool.dma_start(table.rearrange("(p r) d -> p (r d)", p=P).rearrange("p (r f) -> p r f", f=512),
                               zeros[:].unsqueeze(1).broadcast_to([P, r, 512])).then_inc(m.zeroed, 16)

        @block.scalar
        def _(act):
            act.dma_start(gates[:, 0:4], d["g_xattn"].broadcast_to([P, 4])).then_inc(gates_in, 16)
            act.dma_start(gates[:, 4:8], d["g_ffn"].broadcast_to([P, 4])).then_inc(gates_in, 16)
            act.wait_ge(gates_in, 32)
            nc.scalar.activation(gates[:], gates[:], ACT.Tanh).then_inc(tanh_done, 1)
            act.wait_ge(tanh_done, 1)


def program(nc, d, out, upto=99):
    m = Model()
    m.mask, m.bias = d["mask_1x1xSxS2_ik0"], d["fside_Bx16xSxS2_0"]
    with ExitStack() as ctx:
        setup(nc, ctx, m, d)
        stage_list(nc, m, d, upto)
        res = m.X
        stored = ctx.enter_context(nc.semaphore("stored"))
        with nc.Block() as block:
            @block.sync
            def _(sp):
                sp.dma_start(out.rearrange("t p d -> p t d"), res[:]).then_inc(stored, 16)
                sp.wait_ge(stored, 16)


def kernel(**inputs):
    import concourse.bacc as bacc
    from concourse.bass_utils import run_bass_kernel_spmd

    nc = bacc.Bacc("TRN2", target_bir_lowering=False, num_devices=1)
    arrays, d = {}, {}
    laid = {k: np.ascontiguousarray(f(np.asarray(inputs[k]))) for k, f in INPUTS.items()}
    laid["rows"] = np.stack([np.asarray(inputs[k]) for k in ROWS])
    laid["cols"] = np.ascontiguousarray(np.stack([np.asarray(inputs[k]) for k in COLS], 1))
    laid["consts"] = CONSTS
    for k, a in laid.items():
        arrays["in_" + k] = a
        d[k] = nc.dram_tensor("in_" + k, a.shape, mybir.dt.from_np(a.dtype), kind="ExternalInput").ap()
    out = nc.dram_tensor("out", (NT, P, D), F32, kind="ExternalOutput").ap()
    program(nc, d, out)
    r = run_bass_kernel_spmd(nc, [arrays], core_ids=[0])
    return r.results[0]["out"].reshape(B, S, D)
```

```python
from contextlib import ExitStack, contextmanager

import numpy as np
import concourse.bass as bass
from concourse import mybir

ALU = mybir.AluOpType
ACT = mybir.ActivationFunctionType
F32 = mybir.dt.float32
I32 = mybir.dt.int32
AX_X = mybir.AxisListType.X

P = 128
B, S, D = 4, 512, 128
NT = B * S // P
TB = S // P
S2 = 154
KM_, KR = 128, S2 - 128
H = 16
HG = 4
RR = HG * KR
GH = 3
NG = -(-H // GH)
EPS = 1e-5
LOW = -3.0e38
MASKED = -1.0e30
NOWHERE = 1.0e6
CAP0 = 640
CAP3 = 256

CONST = {}


def constants():
    p = np.arange(P)[:, None]
    f = np.arange(P)[None, :]
    parts = {
        "ident": (p == f) * 1.0,
        "ones": np.ones((P, P)),
        "earlier": (p < f) * 1.0,
        "first": (p == 0) * np.ones((1, P)),
        "head8": (p // 8 == np.arange(16)[None]) * (1 / np.sqrt(8.0)),
        "head64": (p // 64 == np.arange(2)[None]) * 0.125,
        "rest": (p // KR == np.arange(HG)[None]) * 1.0,
        "slot8": np.broadcast_to(float(CAP0) * np.arange(8)[None], (P, 8)),
        "slot16": np.broadcast_to(float(CAP3) * np.arange(16)[None], (P, 16)),
        "rank8": np.broadcast_to(8.0 - np.arange(8)[None], (P, 8)),
        "rank16": np.broadcast_to(16.0 - np.arange(16)[None], (P, 16)),
    }
    for i in range(TB):
        q = i * P + p
        parts[f"causal{i}"] = np.where(q >= np.arange(S2)[None] + S - S2, 0.0, MASKED)
    parts["tril"] = np.where(p >= f, 0.0, MASKED)
    parts["triu"] = np.where(f >= p, 0.0, MASKED)
    at, cols = 0, []
    for name, a in parts.items():
        CONST[name] = (at, a.shape[1])
        at += a.shape[1]
        cols.append(a.astype(np.float32))
    return np.ascontiguousarray(np.concatenate(cols, 1))


CONSTS = constants()

ROWS = ["L0_xattn_g2", "L0_xattn_be2", "L0_xattn_b2", "L2_xattn_bv", "L2_xattn_bo", "L3_xattn_bv", "L3_xattn_bo",
        "L3_ffn_v_b", "L3_ffn_o_b"]
COLS = ["L0_xattn_g1", "L0_xattn_be1", "L2_xattn_bq", "L2_xattn_bk", "L3_xattn_bq", "L3_ffn_q_b", "L3_ffn_k_b",
        "L3_ffn_ln1_w", "L3_ffn_ln1_b", "L3_ffn_ln2_w", "L3_ffn_ln2_b"]


class Tally:

    def __init__(self, per, i=0):
        self.per, self.i, self.k = per, i, 0

    def take(self):
        n = self.i * self.per + self.k
        self.k += 1
        return n

    def end(self):
        assert self.k == self.per, (self.k, self.per)


class Own:

    def __init__(self, eng, sem, base=0):
        self.eng, self.sem, self.base, self.i, self.per, self.k = eng, sem, base, 0, 0, 0

    def done(self, ins):
        ins.then_inc(self.sem, 1)
        self.k += 1

    def wait(self):
        self.eng.wait_ge(self.sem, self.i * self.per + (self.base + self.k))

    def loop(self, i, per):
        self.base, self.k, self.i, self.per = self.base + self.k, 0, i, per

    def end(self, count):
        assert self.k == self.per, (self.k, self.per)
        self.base, self.i, self.k, self.per = self.base + count * self.per, 0, 0, 0


class Model:

    def __init__(self):
        self.last_sems, self.now_sems = [], []


@contextmanager
def stage(nc, m, name):
    m.now_sems = []

    def sem(s):
        m.now_sems.append(nc.alloc_semaphore(f"{name}_{s}"))
        return m.now_sems[-1]

    yield sem
    for s in m.last_sems:
        nc.release_semaphore(s)
    m.last_sems = m.now_sems


def clear_last(m, sp):
    for s in m.last_sems:
        sp.sem_clear(s)


def ln_stats_vector(nc, dve, own, stats, tmp, src, var_ready, std_ready, std_count=1):
    with dve.Fori(0, NT) as t:
        own.loop(t, 1)
        own.done(nc.vector.bn_stats(stats[:, bass.ds(t, 1), :], src[:, bass.ds(t, 1), :]))
        own.end(NT)
    own.wait()
    mean_e, m2_e, mean_o, m2_o = (stats[:, :, k] for k in (1, 2, 4, 5))
    own.done(nc.vector.tensor_tensor(tmp[:, 2], mean_e, mean_o, ALU.subtract))
    own.done(nc.vector.tensor_tensor(tmp[:, 3], mean_e, mean_o, ALU.add))
    own.done(nc.vector.tensor_tensor(tmp[:, 4], m2_e, m2_o, ALU.add))
    own.wait()
    own.done(nc.vector.tensor_scalar(tmp[:, 0], tmp[:, 3], 0.5, None, ALU.mult))
    own.done(nc.vector.tensor_scalar(tmp[:, 5], tmp[:, 4], 1.0 / D, EPS, ALU.mult, ALU.add))
    own.done(nc.vector.tensor_tensor(tmp[:, 6], tmp[:, 2], tmp[:, 2], ALU.mult))
    own.wait()
    nc.vector.scalar_tensor_tensor(tmp[:, 7], tmp[:, 6], 0.25, tmp[:, 5], ALU.mult, ALU.add).then_inc(var_ready, 1)
    dve.wait_ge(std_ready, std_count)
    own.done(nc.vector.reciprocal(tmp[:, 1], tmp[:, 8]))
    own.wait()


def attention(nc, m, c):
    nm, dv, tiles, mode = c["name"], c["dv"], c["tiles"], c["mode"]
    W = dv + 1
    n = len(tiles)
    KB = H * dv // P
    OB = 1 if dv == 8 else HG
    OH = H // OB
    NM = 1 + -(-KB // GH) + 2 * (-(-KB // 4)) + n * -(-KB // 4)
    NTT = NG + n * (HG + 1)
    with ExitStack() as ctx:
        sb = lambda s, shape: ctx.enter_context(nc.sbuf_tensor(f"{nm}_{s}", shape, F32))
        ps = lambda s, shape: ctx.enter_context(nc.psum_tensor(f"{nm}_{s}", shape, F32))
        sem = ctx.enter_context(stage(nc, m, nm))
        stats, ln = sb("stats", [P, NT, 6]), sb("ln", [P, 9, NT])
        xn, xnT = sb("xn", [P, TB, D]), sb("xnT", [P, TB * P])
        KT, KM = sb("KT", [P, KB, S2]), sb("KM", [P, H, S2])
        G = sb("G", [P, H, S2])
        NZ = TB if mode == "bias" else 2
        Z = sb("Z", [P, NZ, H, S2])
        Zr = sb("Zr", [P, 2, HG, RR])
        mask = sb("mask", [P, TB, S2]) if mode == "mask" else None
        mx = sb("mx", [P, 2, H])
        E, Er = sb("E", [P, 2, H, P]), sb("Er", [RR, 2, HG, P])
        V, Vr = sb("V", [P, H, W]), sb("Vr", [RR, HG, HG * W])
        On, rin, OT = sb("On", [P, H, dv]), sb("rin", [P, H, 1]), sb("OT", [P, KB, P])
        ctm, ctr = sb("ctm", [P, S2]), sb("ctr", [P, HG, KR])
        pad = sb("pad", [P, n * NG])
        ys = sb("ys", [P, D]) if mode == "causal" else None
        bqr = sb("bqr", [P, P]) if mode == "causal" else None
        if mode == "mask":
            maski = ctx.enter_context(nc.sbuf_tensor(f"{nm}_maski", [P, TB, S2], I32))
        psS, psT, psO = ps("psS", [P, 2, 512]), ps("psT", [P, 2, 512]), ps("psO", [P, 2, 512])
        psM, psY = ps("psM", [P, 512]), ps("psY", [P, 512])
        own_v = sem("own_v")
        var_ready, std_ready = sem("var_ready"), sem("std_ready")
        loaded, bias_in = sem("loaded"), [sem(f"bias_in{i}") for i in range(TB if mode == "bias" else 0)]
        xn_ready, km_ready = sem("xn_ready"), sem("km_ready")
        vr_ready = sem("vr_ready")
        s_full, s_free, t_full, t_free = sem("s_full"), sem("s_free"), sem("t_full"), sem("t_free")
        o_full, o_free, m_full, m_free = sem("o_full"), sem("o_free"), sem("m_full"), sem("m_free")
        y_full, y_free = sem("y_full"), sem("y_free")
        ctr_ready, z_ready = sem("ctr_ready"), sem("z_ready")
        block = ctx.enter_context(nc.Block())
        NY = n + (mode == "causal")
        nOT = -(-KB // 4)
        ctx_b = m.ctxT

        @block.sync
        def _(sp):
            clear_last(m, sp)
            if mode == "mask":
                sp.dma_start(maski[:], m.mask.rearrange("(i p) k -> p i k", p=P)).then_inc(loaded, 16)
            if mode == "bias":
                for i in range(TB):
                    sp.dma_start(Z[:, i], m.bias[0, :, i * P:(i + 1) * P].rearrange("h p k -> p h k")).then_inc(bias_in[i], 16)
                with sp.Fori(0, B - 1) as b:
                    for i in range(TB):
                        sp.wait_ge(t_full, b * NTT + (NG + (i + 1) * (HG + 1)))
                        sp.dma_start(Z[:, i], m.bias[bass.ds(b + 1, 1), :, i * P:(i + 1) * P].rearrange(
                            "o h p k -> p (o h) k")).then_inc(bias_in[i], 16)

        @block.scalar
        def _(act):
            act.wait_ge(var_ready, 1)
            nc.scalar.activation(ln[:, 8], ln[:, 7], ACT.Sqrt).then_inc(std_ready, 1)
            with act.Fori(0, B) as b:
                mt, tt, av = Tally(NM, b), Tally(NTT, b), Tally(n * OB, b)

                def from_m(copies):
                    act.wait_ge(m_full, mt.take() + 1)
                    for k, (dst, src) in enumerate(copies):
                        last = nc.scalar.copy(dst, src)
                    last.then_inc(m_free, 1)

                from_m([(xnT[:], psM[:])])
                for j in range(0, KB, GH):
                    w = min(GH, KB - j)
                    act.wait_ge(m_full, mt.take() + 1)
                    if mode == "causal":
                        last = nc.scalar.activation(KT[:, 0], psM[:, 0:S2], ACT.Identity, bias=m.col("L2_xattn_bk"))
                    else:
                        last = nc.scalar.copy(KT[:, j:j + w], psM[:, 0:w * S2].rearrange("p (j k) -> p j k", k=S2))
                    last.then_inc(m_free, 1)
                for j in range(nOT):
                    hh = min(H, 512 // dv)
                    from_m([(V[:, hh * j:hh * (j + 1), 0:dv],
                             psM[:, 0:hh * dv].rearrange("p (h d) -> p h d", d=dv))])
                for j in range(nOT):
                    mt.take()
                for g in range(NG):
                    w = min(GH, H - GH * g)
                    act.wait_ge(t_full, tt.take() + 1)
                    nc.scalar.copy(G[:, GH * g:GH * g + w],
                                   psT[:, g % 2, 0:w * S2].rearrange("p (h k) -> p h k", k=S2)).then_inc(t_free, 1)
                for k in range(n + 2):
                    if k >= 2:
                        for j in range(nOT):
                            w = min(4, KB)
                            from_m([(OT[:, 4 * j:4 * j + w], psM[:, 0:w * P].rearrange("p (j q) -> p j q", q=P))])
                    if k < n:
                        for g in range(HG + 1):
                            if g == 0 and k >= 2:
                                act.wait_ge(o_full, b * (n * OB) + (k - 1) * OB)
                            x = tt.take()
                            act.wait_ge(t_full, x + 1)
                            bank = (NG + k * (HG + 1) + g) % 2
                            if g < HG:
                                nc.scalar.activation(E[:, k % 2, HG * g:HG * g + HG],
                                                     psT[:, bank].rearrange("p (h q) -> p h q", q=P),
                                                     ACT.Exp).then_inc(t_free, 1)
                            else:
                                nc.scalar.activation(Er[:, k % 2], psT[0:RR, bank].rearrange("p (h q) -> p h q", q=P),
                                                     ACT.Exp).then_inc(t_free, 1)
                mt.end(), tt.end()

        @block.gpsimd
        def _(pool):
            with pool.Fori(0, B) as b:
                for k in range(n):
                    for g in range(HG):
                        need = -(-(HG * g + HG) // GH)
                        pool.wait_ge(s_free, b * (n * NG) + (k * NG + need + 2))
                        h = slice(HG * g, HG * g + HG)
                        zz = Z[:, k % NZ, h, 0:KM_]
                        nc.gpsimd.tensor_tensor(zz, zz, mx[:, k % 2, h].unsqueeze(2).broadcast_to([P, HG, KM_]),
                                                ALU.subtract).then_inc(z_ready, 1)
                        nc.gpsimd.tensor_tensor(Zr[:, k % 2, g].rearrange("p (h k) -> p h k", k=KR), Z[:, k % NZ, h, KM_:S2],
                                                mx[:, k % 2, h].unsqueeze(2).broadcast_to([P, HG, KR]),
                                                ALU.subtract).then_inc(z_ready, 1)

        @block.tensor
        def _(pe):
            pe.sem_inc(m_free, 1)
            pe.sem_inc(y_free, 1)
            pe.sem_inc(s_free, 2)
            pe.sem_inc(t_free, 2)
            pe.sem_inc(o_free, 2)
            for s, v in c["weights"]:
                pe.wait_ge(s, v)
            with pe.Fori(0, B) as b:
                mt, tt, st, ot, yt = Tally(NM, b), Tally(NTT, b), Tally(n * NG, b), Tally(n * OB, b), Tally(NY, b)
                pe.wait_ge(m_free, mt.take() + 1)
                for i in range(TB):
                    pe.wait_ge(xn_ready, b * TB + (i + 1))
                    last = pe.transpose(psM[:, i * P:(i + 1) * P], xn[:, i], m.ident)
                last.then_inc(m_full, 1)
                pe.wait_ge(ctr_ready, b + 1)
                for j in range(0, KB, GH):
                    w = min(GH, KB - j)
                    pe.wait_ge(m_free, mt.take() + 1)
                    for jj in range(w):
                        last = pe.matmul(psM[:, jj * S2:(jj + 1) * S2], c["wk"][:, (j + jj) * P:(j + jj + 1) * P],
                                         ctm[:], start=(jj == 0), stop=(jj == w - 1),
                                         skip_group_check=True)
                    last.then_inc(m_full, 1)
                for j in range(nOT):
                    pe.wait_ge(m_free, mt.take() + 1)
                    w = min(512, H * dv)
                    last = pe.matmul(psM[:, 0:w], ctm[:, 0:KM_], c["wv"][:, j * w:(j + 1) * w], start=True,
                                     stop=mode != "causal")
                    if mode == "causal":
                        last = pe.matmul(psM[:, 0:w], m.ones[0:1, :], m.row("L2_xattn_bv"), start=False, stop=True)
                    last.then_inc(m_full, 1)
                for j in range(nOT):
                    pe.wait_ge(m_free, mt.take() + 1)
                    w = min(512, H * dv)
                    last = pe.matmul(psM[0:RR, 0:w], ctr[:].rearrange("p h k -> p (h k)"), c["wv"][:, j * w:(j + 1) * w],
                                     start=True, stop=mode != "causal")
                    if mode == "causal":
                        last = pe.matmul(psM[0:RR, 0:w], m.ones[0:1, 0:RR], m.row("L2_xattn_bv"), start=False, stop=True)
                    last.then_inc(m_full, 1)
                pe.wait_ge(km_ready, b + 1)
                for g in range(NG):
                    w = min(GH, H - GH * g)
                    pe.wait_ge(t_free, tt.take() + 1)
                    for hh in range(w) if KB > 1 else range(1):
                        h = GH * g + hh
                        if KB > 1:
                            last = pe.matmul(psT[:, g % 2, hh * S2:(hh + 1) * S2], c["wq"][:, h // 2], KM[:, h],
                                             start=(hh == 0), stop=(hh == w - 1), skip_group_check=True)
                        else:
                            last = pe.matmul(psT[:, g % 2, 0:w * S2], c["wq"],
                                             KM[:, h:h + w].rearrange("p h k -> p (h k)"), start=True, stop=True)
                    last.then_inc(t_full, 1)

                def scores(k):
                    for g in range(NG):
                        w = min(GH, H - GH * g)
                        hs = slice(GH * g, GH * g + w)
                        if k == 0 and g == 0:
                            pe.wait_ge(t_free, b * NTT + (NG + 2))
                        pe.wait_ge(s_free, st.take() + 1)
                        q = slice(tiles[k] * P, tiles[k] * P + P)
                        last = pe.matmul(psS[:, g % 2, 0:w * S2], xnT[:, q],
                                         G[:, hs].rearrange("p h k -> p (h k)"), start=True, stop=mode != "causal")
                        if mode == "causal":
                            last = pe.matmul(psS[:, g % 2, 0:w * S2], bqr[:],
                                             KM[:, hs].rearrange("p h k -> p (h k)"), start=False, stop=True)
                        last.then_inc(s_full, 1)

                scores(0)
                for k in range(n + 2):
                    if k >= 2:
                        pe.wait_ge(o_free, b * (n * OB) + ((k - 1) * OB + 2))
                        for j in range(nOT):
                            pe.wait_ge(m_free, mt.take() + 1)
                            for jj in range(min(4, KB)):
                                x = On[:].rearrange("p h d -> p (h d)")[:, (4 * j + jj) * P:(4 * j + jj + 1) * P]
                                last = pe.transpose(psM[:, jj * P:(jj + 1) * P], x, m.ident)
                            last.then_inc(m_full, 1)
                    if k + 1 < n:
                        scores(k + 1)
                    if k >= 2:
                        pe.wait_ge(m_free, b * NM + (mt.k + 1))
                        pe.wait_ge(y_free, yt.take() + 1)
                        for j in range(KB):
                            last = pe.matmul(psY[:, 0:D], OT[:, j], c["wo"][:, j], start=(j == 0),
                                             stop=(j == KB - 1 and mode != "causal"))
                        if mode == "causal":
                            last = pe.matmul(psY[:, 0:D], m.ones[0:1, :], m.row("L2_xattn_bo"), start=False, stop=True)
                        last.then_inc(y_full, 1)
                    if k < n:
                        for g in range(HG + 1):
                            pe.wait_ge(z_ready, b * (2 * n * HG) + 2 * (k * HG + min(g + 1, HG)))
                            pe.wait_ge(t_free, tt.take() + 1)
                            bank = (NG + k * (HG + 1) + g) % 2
                            for j in range(HG):
                                if g < HG:
                                    last = pe.transpose(psT[:, bank, j * P:(j + 1) * P],
                                                        Z[:, k % NZ, HG * g + j, 0:KM_], m.ident)
                                else:
                                    last = pe.transpose(psT[0:RR, bank, j * P:(j + 1) * P],
                                                        Zr[:, k % 2, j], m.ident)
                            last.then_inc(t_full, 1)
                    if 1 <= k <= n:
                        kk = k - 1
                        if kk == 0:
                            pe.wait_ge(vr_ready, b + 1)
                        pe.wait_ge(t_free, b * NTT + (NG + (kk + 1) * (HG + 1) + 2))
                        for o in range(OB):
                            u = ot.take()
                            pe.wait_ge(o_free, u + 1)
                            bank = (kk * OB + o) % 2
                            out = psO[:, bank, 0:OH * W].rearrange("p (h d) -> p h d", d=W)
                            for h0 in range(0, OH, HG):
                                for j in range(HG):
                                    hl = h0 + j
                                    h = o * OH + hl
                                    pe.matmul(out[:, hl], E[:, kk % 2, h], V[:, h], start=(hl == 0), stop=False,
                                              skip_group_check=True)
                                g = (o * OH + h0) // HG
                                last = pe.matmul(psO[:, bank, h0 * W:(h0 + HG) * W], Er[:, kk % 2, g], Vr[:, g],
                                                 start=False, stop=(h0 + HG == OH), skip_group_check=True)
                            last.then_inc(o_full, 1)
                if mode == "causal":
                    pe.wait_ge(y_free, yt.take() + 1)
                    pe.matmul(psY[:, 0:D], m.first, ys[:], start=True, stop=True).then_inc(y_full, 1)
                mt.end(), tt.end(), st.end(), ot.end(), yt.end()

        @block.vector
        def _(dve):
            own = Own(dve, own_v)
            if mode == "mask":
                dve.wait_ge(loaded, 16)
                own.done(nc.vector.tensor_copy(mask[:], maski[:]))
                own.wait()
                own.done(nc.vector.tensor_scalar(mask[:], mask[:], 0.0, MASKED, ALU.is_equal, ALU.mult))
            if mode == "causal":
                own.done(nc.vector.tensor_copy(bqr[:], m.col("L2_xattn_bq").broadcast_to([P, P])))
            own.done(nc.vector.memset(V[:, :, dv:W], 1.0))
            ln_stats_vector(nc, dve, own, stats, ln, m.X, var_ready, std_ready)
            with dve.Fori(0, B) as b:
                own.loop(b, n * OB + (mode == "causal"))
                st, ot, yt = Tally(n * NG, b), Tally(n * OB, b), Tally(NY, b)
                dve.wait_ge(y_free, b * NY + 1)
                nc.vector.tensor_copy(ctm[:], ctx_b[:, bass.ds(b, 1), :].rearrange("p o k -> p (o k)"))
                nc.vector.tensor_copy(ctr[:], ctx_b[:, bass.ds(b, 1), KM_:S2].broadcast_to([P, HG, KR])
                                      ).then_inc(ctr_ready, 1)
                for i in range(TB):
                    t = b * TB + i
                    nc.vector.tensor_scalar(xn[:, i], m.X[:, bass.ds(t, 1), :].rearrange("p o d -> p (o d)"),
                                            ln[:, 0, bass.ds(t, 1)], ln[:, 1, bass.ds(t, 1)], ALU.subtract, ALU.mult
                                            ).then_inc(xn_ready, 1)
                mdone = b * NM + (2 + 1 + -(-KB // GH) - 1)
                dve.wait_ge(m_free, mdone)
                if KB == 1:
                    nc.vector.tensor_tensor(KM[:], KT[:].broadcast_to([P, H, S2]),
                                            m.head8.unsqueeze(2).broadcast_to([P, H, S2]), ALU.mult).then_inc(km_ready, 1)
                else:
                    kmv = KM[:].rearrange("p (j a) k -> p j a k", a=2)
                    nc.vector.tensor_scalar(kmv[:, :, 0], KT[:], m.head64[:, 0:1], None, ALU.mult)
                    nc.vector.tensor_scalar(kmv[:, :, 1], KT[:], m.head64[:, 1:2], None, ALU.mult).then_inc(km_ready, 1)
                mrest = 1 + -(-KB // GH) + nOT
                for j in range(nOT):
                    dve.wait_ge(m_full, b * NM + (mrest + j + 1))
                    gs = HG // nOT
                    vv = Vr[:, j * gs:(j + 1) * gs].rearrange("p g (h d) -> p (g h) d", d=W)[:, :, 0:dv]
                    src = psM[0:RR, 0:gs * HG * dv].rearrange("p (h d) -> p h d", d=dv)
                    for g in range(gs):
                        last = nc.vector.tensor_tensor(
                            vv[:, g * HG:(g + 1) * HG], src[:, g * HG:(g + 1) * HG],
                            m.rest[0:RR].unsqueeze(2).broadcast_to([RR, HG, dv]), ALU.mult)
                    last.then_inc(m_free, 1)
                nc.vector.tensor_copy(Vr[:].rearrange("p g (h d) -> p g h d", d=W)[:, :, :, dv],
                                      m.rest[0:RR].unsqueeze(1).broadcast_to([RR, HG, HG])).then_inc(vr_ready, 1)

                def maxima(k):
                    for g in range(NG):
                        w = min(GH, H - GH * g)
                        if g == 0 and mode == "bias":
                            dve.wait_ge(bias_in[k], b * 16 + 16)
                        if g == 0 and NZ == 2 and k >= 2:
                            dve.wait_ge(t_full, b * NTT + (NG + (k - 1) * (HG + 1)))
                        dve.wait_ge(s_full, st.take() + 1)
                        nc.vector.memset(pad[:, k * NG + g:k * NG + g + 1], 0.0)
                        for hh in range(w):
                            h = GH * g + hh
                            add = Z[:, k, h] if mode == "bias" else mask[:, k] if mode == "mask" else m.causal[tiles[k]]
                            last = nc.vector.tensor_tensor_reduce(
                                Z[:, k % NZ, h], psS[:, g % 2, hh * S2:(hh + 1) * S2], add, 1.0, LOW, ALU.add, ALU.max,
                                mx[:, k % 2, h:h + 1])
                        last.then_inc(s_free, 1)

                maxima(0)
                for k in range(n + 2):
                    if k + 1 < n:
                        maxima(k + 1)
                    if k >= 2:
                        i = tiles[k - 2]
                        t = b * TB + i
                        dve.wait_ge(y_full, yt.take() + 1)
                        if mode == "causal" and k == 2:
                            own.done(nc.vector.tensor_copy(ys[:], psY[:, 0:D]))
                            own.wait()
                        x = m.X[:, bass.ds(t, 1), :].rearrange("p o d -> p (o d)")
                        if mode == "bias":
                            x1 = m.X1[:, bass.ds(t, 1), :].rearrange("p o d -> p (o d)")
                            nc.vector.tensor_tensor(x1, psY[:, 0:D], xn[:, i], ALU.add).then_inc(y_free, 1)
                        else:
                            nc.vector.scalar_tensor_tensor(x, psY[:, 0:D], m.gate(c["gate"]), x, ALU.mult, ALU.add
                                                           ).then_inc(y_free, 1)
                    if 1 <= k <= n:
                        for o in range(OB):
                            dve.wait_ge(o_full, ot.take() + 1)
                            bank = ((k - 1) * OB + o) % 2
                            out = psO[:, bank, 0:OH * W].rearrange("p (h d) -> p h d", d=W)
                            hs = slice(o * OH, (o + 1) * OH)
                            own.done(nc.vector.reciprocal(rin[:, hs], out[:, :, dv:W]))
                            own.wait()
                            last = nc.vector.tensor_tensor(On[:, hs], out[:, :, 0:dv],
                                                           rin[:, hs].broadcast_to([P, OH, dv]), ALU.mult)
                            last.then_inc(o_free, 1)
                if mode == "causal":
                    dve.wait_ge(y_full, yt.take() + 1)
                    for i in range(2):
                        x = m.X[:, bass.ds(b * TB + i, 1), :].rearrange("p o d -> p (o d)")
                        last = nc.vector.scalar_tensor_tensor(x, psY[:, 0:D], m.gate(c["gate"]), x, ALU.mult, ALU.add)
                    last.then_inc(y_free, 1)
                own.end(B)
                st.end(), ot.end(), yt.end()


def norm_transpose(nc, m, name, src, dst, w=None, b=None, router=None, turn=True):
    with ExitStack() as ctx:
        sb = lambda s, shape: ctx.enter_context(nc.sbuf_tensor(f"{name}_{s}", shape, F32))
        ps = lambda s, shape: ctx.enter_context(nc.psum_tensor(f"{name}_{s}", shape, F32))
        sem = ctx.enter_context(stage(nc, m, name))
        stats, ln = sb("stats", [P, NT, 6]), sb("ln", [P, 9, NT])
        psT = ps("psT", [P, NT // TB, 512])
        own_v, var_ready, std_ready = sem("own_v"), sem("var_ready"), sem("std_ready")
        x_ready, t_full, xt_ready = sem("x_ready"), sem("t_full"), sem("xt_ready")
        if router:
            r = Router(nc, sb, ps, sem, m, router)
        block = ctx.enter_context(nc.Block())

        @block.sync
        def _(sp):
            clear_last(m, sp)

        @block.scalar
        def _(act):
            act.wait_ge(var_ready, 1)
            nc.scalar.activation(ln[:, 8], ln[:, 7], ACT.Sqrt).then_inc(std_ready, 1)
            for c in range(NT // TB if turn else 0):
                act.wait_ge(t_full, c + 1)
                dst_t = m.XT[:, c * 512:(c + 1) * 512]
                if w is None:
                    nc.scalar.copy(dst_t, psT[:, c]).then_inc(xt_ready, 1)
                else:
                    nc.scalar.activation(dst_t, psT[:, c], ACT.Identity, bias=b, scale=w).then_inc(xt_ready, 1)
            if router:
                r.scalar(act)

        @block.tensor
        def _(pe):
            for t in range(NT if turn else 0):
                pe.wait_ge(x_ready, t + 1)
                last = pe.transpose(psT[:, t // TB, (t % TB) * P:(t % TB + 1) * P], dst[:, t], m.ident)
                if t % TB == TB - 1:
                    last.then_inc(t_full, 1)
            if router:
                r.tensor(pe, xt_ready)

        @block.vector
        def _(dve):
            own = Own(dve, own_v)
            ln_stats_vector(nc, dve, own, stats, ln, src, var_ready, std_ready)
            with dve.Fori(0, NT) as t:
                nc.vector.tensor_scalar(dst[:, bass.ds(t, 1), :], src[:, bass.ds(t, 1), :], ln[:, 0, bass.ds(t, 1)],
                                        ln[:, 1, bass.ds(t, 1)], ALU.subtract, ALU.mult).then_inc(x_ready, 1)
            if router:
                r.vector(dve, own)


class Router:

    def __init__(self, nc, sb, ps, sem, m, c):
        self.nc, self.m, self.c = nc, m, c
        E = c["E"]
        self.psL = ps("psL", [P, NT, E])
        self.psC = ps("psC", [P, 2, 512])
        self.L, self.eq, self.rank = sb("logits", [P, NT, E]), sb("eq", [P, NT, E]), sb("rank", [P, NT, E])
        self.hot = sb("hot", [P, 2, NT, E])
        self.v = sb("rv", [P, 12, NT])
        self.pos, self.run = sb("pos", [P, 2, NT, E]), sb("run", [P, 2, NT, E])
        self.l_ready, self.diff_ready, self.exp_ready = sem("l_ready"), sem("diff_ready"), sem("exp_ready")
        self.hot_ready, self.c_ready = sem("hot_ready"), sem("c_ready")

    def tensor(self, pe, xt_ready):
        c, m = self.c, self.m
        for t in range(NT):
            pe.wait_ge(xt_ready, t // TB + 1)
            last = pe.matmul(self.psL[:, t], m.XT[:, t * P:(t + 1) * P], c["w"], start=(t == 0), stop=(t == NT - 1),
                             skip_group_check=True)
        last.then_inc(self.l_ready, 1)
        if c["kind"] in ("L0", "L3"):
            pe.wait_ge(self.hot_ready, 1)
            n = NT * c["E"]
            for k in range(1 if c["kind"] == "L0" else 2):
                hot = self.hot[:, k].rearrange("p t e -> p (t e)")
                pe.matmul(self.psC[:, k, 0:n], m.const["earlier"], hot, start=True, stop=True, skip_group_check=True)
                last = pe.matmul(self.psC[:, k, 256:256 + n], m.ones, hot, start=False, stop=True, skip_group_check=True)
            last.then_inc(self.c_ready, 1)

    def scalar(self, act):
        nc, v = self.nc, self.v
        act.wait_ge(self.diff_ready, 1)
        last = nc.scalar.activation(v[:, 3], v[:, 2], ACT.Exp)
        if self.c["kind"] == "L3":
            last = nc.scalar.activation(self.rank[:], self.eq[:], ACT.Exp)
        last.then_inc(self.exp_ready, 1)

    def vector(self, dve, own):
        nc, c, v, m = self.nc, self.c, self.v, self.m
        E, kind, L, eq, rank, hot = c["E"], c["kind"], self.L, self.eq, self.rank, self.hot
        wide = lambda a: a.unsqueeze(2).broadcast_to([P, NT, E])
        order = m.const["rank%d" % E].unsqueeze(1).broadcast_to([P, NT, E])

        def step(ins):
            own.done(ins)
            own.wait()

        dve.wait_ge(self.l_ready, 1)
        if kind == "L0":
            step(nc.vector.tensor_scalar(L[:], self.psL[:], -1e4, 1e4, ALU.max, ALU.min))
        elif kind == "L1":
            step(nc.vector.tensor_tensor(L[:], self.psL[:], m.router_bias[:].unsqueeze(1).broadcast_to([P, NT, E]), ALU.add))
        else:
            step(nc.vector.tensor_copy(L[:], self.psL[:]))
        for k in range(2):
            step(nc.vector.tensor_reduce(v[:, k], L[:], AX_X, ALU.max))
            step(nc.vector.tensor_tensor(eq[:], L[:], wide(v[:, k]), ALU.is_equal))
            step(nc.vector.tensor_tensor(rank[:], eq[:], order, ALU.mult))
            step(nc.vector.tensor_reduce(v[:, 4], rank[:], AX_X, ALU.max))
            step(nc.vector.tensor_tensor(hot[:, k], rank[:], wide(v[:, 4]), ALU.is_equal))
            if k == 0:
                if kind == "L3":
                    step(nc.vector.tensor_tensor(self.run[:, 1], L[:], wide(v[:, 0]), ALU.subtract))
                step(nc.vector.scalar_tensor_tensor(L[:], hot[:, 0], LOW, L[:], ALU.mult, ALU.add))
        if kind == "L0":
            own.done(nc.vector.tensor_tensor(self.pos[:, 1], hot[:, 0], hot[:, 1], ALU.add))
            own.wait()
            own.done(nc.vector.tensor_copy(self.run[:, 1], hot[:, 0]))
            own.wait()
            nc.vector.tensor_copy(hot[:, 0], self.pos[:, 1]).then_inc(self.hot_ready, 1)
        elif kind == "L3":
            own.done(nc.vector.tensor_copy(eq[:], self.run[:, 1]))
            own.wait()
            dve.wait_ge(own.sem, own.base + own.k)
            nc.vector.memset(v[:, 11], 0.0).then_inc(self.hot_ready, 1)
        own.done(nc.vector.tensor_tensor(v[:, 2], v[:, 1], v[:, 0], ALU.subtract))
        own.wait()
        nc.vector.memset(v[:, 10], 0.0).then_inc(self.diff_ready, 1)
        dve.wait_ge(self.exp_ready, 1)
        if kind != "L3":
            step(nc.vector.tensor_scalar(v[:, 5], v[:, 3], 1.0, 1e-12 if kind == "L0" else 0.0, ALU.add, ALU.add))
            step(nc.vector.reciprocal(v[:, 6], v[:, 5]))
            step(nc.vector.tensor_tensor(v[:, 7], v[:, 3], v[:, 6], ALU.mult))
        if kind in ("L0", "L3"):
            self.positions(dve, own, step)
        if kind in ("L0", "L3"):
            cap = CAP0 if kind == "L0" else CAP3
            if kind == "L3":
                step(nc.vector.tensor_reduce(v[:, 5], rank[:], AX_X, ALU.add))
                step(nc.vector.reciprocal(v[:, 6], v[:, 5]))
                step(nc.vector.tensor_tensor(v[:, 7], v[:, 3], v[:, 6], ALU.mult))
            for k in range(2):
                pos = self.pos[:, 0 if kind == "L0" else k]
                chosen = self.run[:, 1] if kind == "L0" and k == 0 else hot[:, k]
                step(nc.vector.tensor_scalar(rank[:], pos, float(cap), NOWHERE, ALU.is_ge, ALU.mult))
                step(nc.vector.tensor_tensor(rank[:], rank[:], pos, ALU.add))
                step(nc.vector.tensor_tensor(rank[:], rank[:], m.const["slot%d" % E].unsqueeze(1).broadcast_to([P, NT, E]),
                                             ALU.add))
                step(nc.vector.tensor_tensor(rank[:], rank[:], chosen, ALU.mult))
                step(nc.vector.tensor_reduce(v[:, 8], rank[:], AX_X, ALU.add))
                step(nc.vector.tensor_copy(m.slot_to[:, k], v[:, 8]))
                step(nc.vector.tensor_scalar(v[:, 9], v[:, 8], float(E * cap - 1), None, ALU.min))
                step(nc.vector.tensor_copy(m.slot_from[:, k], v[:, 9]))
                step(nc.vector.tensor_scalar(v[:, 9], v[:, 8], NOWHERE, None, ALU.is_lt))
                step(nc.vector.tensor_tensor(v[:, 6 + k], v[:, 6 + k], v[:, 9], ALU.mult))
            if kind == "L3":
                step(nc.vector.tensor_tensor(v[:, 8], v[:, 6], v[:, 7], ALU.add))
                step(nc.vector.tensor_scalar(v[:, 8], v[:, 8], float(np.finfo(np.float32).eps), None, ALU.max))
                step(nc.vector.reciprocal(v[:, 9], v[:, 8]))
                for k in range(2):
                    step(nc.vector.tensor_tensor(v[:, 6 + k], v[:, 6 + k], v[:, 9], ALU.mult))
                step(nc.vector.tensor_scalar(v[:, 6:8], v[:, 6:8], 1.0 - 0.2, None, ALU.mult))
            step(nc.vector.tensor_scalar(m.slot_share[:], v[:, 6:8], m.gate(c["gate"]), None, ALU.mult))
            return
        step(nc.vector.tensor_tensor(eq[:], hot[:, 0], wide(v[:, 6]), ALU.mult))
        step(nc.vector.tensor_tensor(rank[:], hot[:, 1], wide(v[:, 7]), ALU.mult))
        step(nc.vector.tensor_tensor(eq[:], eq[:], rank[:], ALU.add))
        step(nc.vector.tensor_scalar(c["comb"], eq[:], m.gate(c["gate"]), None, ALU.mult))

    def positions(self, dve, own, step):
        nc, E = self.nc, self.c["E"]
        pos, run, n = self.pos, self.run, NT * E
        dve.wait_ge(self.c_ready, 1)
        ks = 1 if self.c["kind"] == "L0" else 2
        for k in range(ks):
            sums = self.psC[:, k, 256:256 + n].rearrange("p (t e) -> p t e", e=E)
            inside = self.psC[:, k, 0:n].rearrange("p (t e) -> p t e", e=E)
            r = run[:, 0]
            step(nc.vector.tensor_copy(r, sums))
            for t in range(1, NT):
                step(nc.vector.tensor_tensor(r[:, t], r[:, t], r[:, t - 1], ALU.add))
            if k == 0 and ks == 2:
                step(nc.vector.tensor_copy(run[:, 1, 0], r[:, NT - 1]))
            step(nc.vector.tensor_tensor(r, r, sums, ALU.subtract))
            step(nc.vector.tensor_tensor(pos[:, k], r, inside, ALU.add))
            if k == 1:
                step(nc.vector.tensor_tensor(pos[:, 1], pos[:, 1], run[:, 1, 0].unsqueeze(1).broadcast_to([P, NT, E]),
                                             ALU.add))


def experts(nc, m, name, c):
    EB, split, J = c["w1"].shape[0], c.get("split", 1), c["w1"].shape[2] // P
    C = NT // TB
    U = min(2, EB)
    glu = "w3" in c
    acc = c["dst"]
    with ExitStack() as ctx:
        sb = lambda s, shape: ctx.enter_context(nc.sbuf_tensor(f"{name}_{s}", shape, F32))
        ps = lambda s, shape: ctx.enter_context(nc.psum_tensor(f"{name}_{s}", shape, F32))
        sem = ctx.enter_context(stage(nc, m, name))
        w1, w2 = sb("w1", [P, U, J * P]), sb("w2", [P, U, J, D])
        b1 = sb("b1", [P, U, J]) if "b1" in c else None
        w3 = sb("w3", [P, U, J * P]) if glu else None
        h = sb("h", [P, 2, J, 512])
        psA = ps("psA", [P, 2, 512])
        psB = ps("psB", [P, 2, 512]) if glu else None
        psY = ps("psY", [P, 2 * split, 512])
        w_in = [sem(f"w_in{u}") for u in range(U)]
        a_full, a_free, b_full, b_free = sem("a_full"), sem("a_free"), sem("b_full"), sem("b_free")
        y_full, y_free, part = sem("y_full"), sem("y_free"), sem("part")
        block = ctx.enter_context(nc.Block())
        nw = 2 + glu + (b1 is not None)
        N = U * C * J

        def load(sp, e, u):
            sp.dma_start(w1[:, u], e(c["w1"])).then_inc(w_in[u], 16)
            if glu:
                sp.dma_start(w3[:, u], e(c["w3"])).then_inc(w_in[u], 16)
            if b1 is not None:
                sp.dma_start(b1[:, u], e(c["b1"])).then_inc(w_in[u], 16)
            sp.dma_start(w2[:, u], e(c["w2"])).then_inc(w_in[u], 16)

        @block.sync
        def _(sp):
            clear_last(m, sp)
            for u in range(U):
                load(sp, lambda a: a[u], u)
            if EB > U:
                with sp.Fori(0, EB // U - 1) as i:
                    for u in range(U):
                        sp.wait_ge(y_full, i * (U * C) + ((u + 1) * C + 2))
                        load(sp, lambda a: a[bass.ds(i * U + (U + u), 1)].rearrange(
                            "o p f -> p (o f)" if len(a.shape) == 3 else "o p j f -> p (o j) f"), u)

        @block.scalar
        def _(act):
            with act.Fori(0, EB // U) as i:
                a = Tally(N, i)
                for u in range(U):
                    for cc in range(C):
                        s = (u * C + cc) % 2
                        for j in range(J):
                            if j == 0:
                                act.wait_ge(y_full, i * (U * C) + (u * C + cc + 1))
                            act.wait_ge(a_full, a.take() + 1)
                            bias = 0.0
                            if "b1" in c:
                                bias = b1[:, u, j:j + 1]
                            nc.scalar.activation(h[:, s, j], psA[:, j % 2] if J > 1 else psA[:, s], c["act"], bias=bias
                                                 ).then_inc(a_free, 1)
                a.end()

        @block.tensor
        def _(pe):
            pe.sem_inc(a_free, 2)
            pe.sem_inc(b_free, 2)
            pe.sem_inc(y_free, 2)
            pe.sem_inc(y_full, 2)
            with pe.Fori(0, EB // U) as i:
                a = Tally(N, i)

                def hidden(k):
                    u, cc = divmod(k, C)
                    if cc == 0:
                        pe.wait_ge(w_in[u], i * (16 * nw) + 16 * nw)
                    x = m.XT[:, cc * 512:(cc + 1) * 512]
                    for j in range(J):
                        n = a.take()
                        bank = j % 2 if J > 1 else k % 2
                        pe.wait_ge(a_free, n + 1)
                        last = pe.matmul(psA[:, bank], w1[:, u, j * P:(j + 1) * P], x, start=True, stop=True)
                        if glu:
                            pe.wait_ge(b_free, n + 1)
                            last.then_inc(a_full, 1)
                            last = pe.matmul(psB[:, bank], w3[:, u, j * P:(j + 1) * P], x, start=True, stop=True)
                            last.then_inc(b_full, 1)
                        else:
                            last.then_inc(a_full, 1)

                def outputs(k):
                    u, cc = divmod(k, C)
                    pe.wait_ge(b_free if glu else a_free, i * N + ((k + 1) * J + 2))
                    pe.wait_ge(y_free, i * (U * C) + (k + 1))
                    for q in range(split):
                        r = slice(q * (P // split), (q + 1) * (P // split))
                        for t in range(TB):
                            for j in range(J):
                                last = pe.matmul(psY[:, (k % 2) * split + q, t * P:(t + 1) * P], h[r, k % 2, j, t * P:(t + 1) * P],
                                                 w2[r, u, j], start=(t == 0 and j == 0),
                                                 stop=(t == TB - 1 and j == J - 1 and "b2" not in c), skip_group_check=True)
                            if "b2" in c:
                                last = pe.matmul(psY[:, (k % 2) * split + q, t * P:(t + 1) * P], m.ones[0:1, :],
                                                 c["b2"](i, U, u), start=False, stop=(t == TB - 1), skip_group_check=True)
                    last.then_inc(y_full, 1)

                hidden(0)
                for k in range(U * C):
                    if k + 1 < U * C:
                        hidden(k + 1)
                    outputs(k)
                a.end()

        @block.vector
        def _(dve):
            with dve.Fori(0, EB // U) as i:
                n = Tally(N, i)

                def gate(k):
                    for j in range(J):
                        x = n.take()
                        bank = j % 2 if J > 1 else k % 2
                        dve.wait_ge(a_free, x + 3)
                        dve.wait_ge(b_full, x + 1)
                        nc.vector.tensor_tensor(h[:, k % 2, j], h[:, k % 2, j], psB[:, bank], ALU.mult).then_inc(b_free, 1)

                if glu:
                    gate(0)
                for k in range(U * C):
                    u, cc = divmod(k, C)
                    if glu and k + 1 < U * C:
                        gate(k + 1)
                    dve.wait_ge(y_full, i * (U * C) + (k + 3))
                    for q in range(split):
                        for t in range(TB):
                            x = acc[:, cc * TB + t]
                            if q == 0 and t == 0:
                                dve.wait_ge(y_free, i * (U * C) + (k + 2))
                            elif q > 0 and t == 0:
                                dve.wait_ge(part, i * (U * C * (split - 1)) + (k * (split - 1) + q))
                            last = nc.vector.scalar_tensor_tensor(x, psY[:, (k % 2) * split + q, t * P:(t + 1) * P],
                                                                  c["share"](i, U, u, q, cc * TB + t), x, ALU.mult, ALU.add)
                        if q < split - 1:
                            last.then_inc(part, 1)
                    last.then_inc(y_free, 1)
                if glu:
                    n.end()



def routed_experts(nc, m, name, c):
    EB, J, U, chunks = c["w1"].shape[0], c["w1"].shape[2] // P, c["U"], c["chunks"]
    T, CH = sum(chunks), len(chunks)
    NMAX = max(chunks) * P
    UC = U * CH
    assert UC % 2 == 0 and EB % U == 0
    TOT = EB * CH
    NS = EB * T * P
    glu = "w3" in c
    b1, b2 = "b1" in c, "b2" in c
    units = [(u, sum(chunks[:q]), chunks[q]) for u in range(U) for q in range(CH)]
    with ExitStack() as ctx:
        sb = lambda s, shape: ctx.enter_context(nc.sbuf_tensor(f"{name}_{s}", shape, F32))
        ps = lambda s, shape: ctx.enter_context(nc.psum_tensor(f"{name}_{s}", shape, F32))
        sem = ctx.enter_context(stage(nc, m, name))
        w1, w2 = sb("w1", [P, U, J * P]), sb("w2", [P, U, J, D])
        w3 = sb("w3", [P, U, J * P]) if glu else None
        b1s = sb("b1", [P, U, J]) if b1 else None
        b2s = sb("b2", [P, U, D]) if b2 else None
        xs, xsT = sb("xs", [P, U, T, D]), sb("xsT", [P, 2, NMAX])
        h, ys = sb("h", [P, 2, J, NMAX]), sb("ys", [P, 2, NMAX // P, D])
        psT, psA, psY = ps("psT", [P, 2, 512]), ps("psA", [P, 2, 512]), ps("psY", [P, 2, 512])
        psB = ps("psB", [P, 2, 512]) if glu else None
        w_in, x_in = [sem(f"w_in{u}") for u in range(U)], [sem(f"x_in{u}") for u in range(U)]
        stored = [sem("stored0"), sem("stored1")]
        scattered, gathered, before = m.scattered, m.gathered, c["before"]
        t_full, t_free = sem("t_full"), sem("t_free")
        a_full, a_free = sem("a_full"), sem("a_free")
        b_full, b_free = (sem("b_full"), sem("b_free")) if glu else (a_full, a_free)
        y_full, y_free, summed = sem("y_full"), sem("y_free"), sem("summed")
        block = ctx.enter_context(nc.Block())
        nw = 2 + glu + b1 + b2
        N = UC * J
        slots_in = m.slots_in[0:NS].rearrange("(e t p) d -> e p t d", p=P, t=T)
        slots_out = m.slots_out[0:NS].rearrange("(e t p) d -> e p t d", p=P, t=T)

        @block.sync
        def _(sp):
            clear_last(m, sp)
            sp.sem_inc(stored[0], 16)
            sp.sem_inc(stored[1], 16)

            def load_w(e, u):
                sp.dma_start(w1[:, u], e(c["w1"])).then_inc(w_in[u], 16)
                if glu:
                    sp.dma_start(w3[:, u], e(c["w3"])).then_inc(w_in[u], 16)
                if b1:
                    sp.dma_start(b1s[:, u], e(c["b1"])).then_inc(w_in[u], 16)
                if b2:
                    sp.dma_start(b2s[:, u], e(c["b2"]).broadcast_to([P, D])).then_inc(w_in[u], 16)
                sp.dma_start(w2[:, u], e(c["w2"])).then_inc(w_in[u], 16)

            for u in range(U):
                load_w(lambda a: a[u], u)
            sp.wait_ge(scattered, (before + 1) * 16 * 2 * NT)
            for u in range(U):
                sp.dma_start(xs[:, u], slots_in[u]).then_inc(x_in[u], 16)
            def store(k, i, i0=0):
                u, first, tiles = units[k]
                sp.wait_ge(y_free, (i0 + i) * UC + (k + 3))
                e = slots_out[bass.ds(i * U + u, 1)] if i0 == 0 else slots_out[i0 * U + u:i0 * U + u + 1]
                sp.dma_start(e.rearrange("o p t d -> p (o t) d")[:, first:first + tiles], ys[:, k % 2, 0:tiles]
                             ).then_inc(stored[k % 2], 16)

            rounds = EB // U
            with sp.Fori(0, rounds - 1) as i:
                for u in range(U):
                    at = lambda a: a[bass.ds(i * U + (U + u), 1)].rearrange(
                        "o p f -> p (o f)" if len(a.shape) == 3 else "o p j f -> p (o j) f")
                    sp.wait_ge(t_full, i * UC + (u + 1) * CH)
                    sp.dma_start(xs[:, u], at(slots_in)).then_inc(x_in[u], 16)
                    for q in range(CH):
                        store(u * CH + q, i)
                    load_w(at, u)
            for k in range(UC):
                store(k, 0, rounds - 1)

        @block.scalar
        def _(act):
            with act.Fori(0, EB // U) as i:
                a = Tally(N, i)

                def turned(k):
                    tiles = units[k][2]
                    act.wait_ge(t_full, i * UC + (k + 1))
                    act.wait_ge(b_full, i * N + (k + 1) * J)
                    src, dst = psT[:, k % 2, 0:tiles * P], xsT[:, k % 2, 0:tiles * P]
                    if c.get("scale") is None:
                        nc.scalar.copy(dst, src).then_inc(t_free, 1)
                    else:
                        nc.scalar.activation(dst, src, ACT.Identity, bias=c["bias"], scale=c["scale"]).then_inc(t_free, 1)

                turned(0)
                turned(1)
                for k, (u, _, tiles) in enumerate(units):
                    for j in range(J):
                        if j == 0:
                            act.wait_ge(y_full, i * UC + (k + 1))
                        act.wait_ge(a_full, a.take() + (2 * J + 1))
                        nc.scalar.activation(h[:, k % 2, j, 0:tiles * P], psA[:, j % 2, 0:tiles * P], c["act"],
                                             bias=b1s[:, u, j:j + 1] if b1 else 0.0).then_inc(a_free, 1)
                    if k + 2 < UC:
                        turned(k + 2)
                a.end()

        @block.tensor
        def _(pe):
            pe.sem_inc(t_free, 2)
            pe.sem_inc(a_free, 2)
            pe.sem_inc(a_full, 2 * J)
            if glu:
                pe.sem_inc(b_free, 2)
                pe.sem_inc(b_full, 2 * J)
            pe.sem_inc(y_free, 2)
            pe.sem_inc(y_full, 2)
            with pe.Fori(0, EB // U) as i:
                a = Tally(N, i)

                def turn(k):
                    u, first, tiles = units[k]
                    if first == 0:
                        pe.wait_ge(x_in[u], i * 16 + 16)
                    pe.wait_ge(t_free, i * UC + (k + 1))
                    for t in range(tiles):
                        last = pe.transpose(psT[:, k % 2, t * P:(t + 1) * P], xs[:, u, first + t], m.ident)
                    last.then_inc(t_full, 1)

                def hidden(k):
                    u, first, tiles = units[k]
                    w = tiles * P
                    if first == 0:
                        pe.wait_ge(w_in[u], i * (16 * nw) + 16 * nw)
                    pe.wait_ge(t_free, i * UC + (k + 3))
                    x = xsT[:, k % 2, 0:w]
                    for j in range(J):
                        n = a.take()
                        pe.wait_ge(a_free, n + 1)
                        pe.matmul(psA[:, j % 2, 0:w], w1[:, u, j * P:(j + 1) * P], x, start=True, stop=True).then_inc(a_full, 1)
                        if glu:
                            pe.wait_ge(b_free, n + 1)
                            pe.matmul(psB[:, j % 2, 0:w], w3[:, u, j * P:(j + 1) * P], x, start=True, stop=True).then_inc(b_full, 1)

                def outputs(k):
                    u, first, tiles = units[k]
                    pe.wait_ge(b_free, i * N + ((k + 1) * J + 2))
                    pe.wait_ge(y_free, i * UC + (k + 1))
                    for t in range(tiles):
                        for j in range(J):
                            last = pe.matmul(psY[:, k % 2, t * P:(t + 1) * P], h[:, k % 2, j, t * P:(t + 1) * P], w2[:, u, j],
                                             start=(t == 0 and j == 0), stop=(t == tiles - 1 and j == J - 1),
                                             skip_group_check=True)
                    last.then_inc(y_full, 1)

                turn(0)
                turn(1)
                hidden(0)
                for k in range(UC):
                    if k + 2 < UC:
                        turn(k + 2)
                    if k + 1 < UC:
                        hidden(k + 1)
                    outputs(k)
                a.end()

        @block.vector
        def _(dve):
            with dve.Fori(0, EB // U) as i:
                n = Tally(N, i)

                def gate(k):
                    w = units[k][2] * P
                    for j in range(J):
                        x = n.take()
                        dve.wait_ge(a_free, x + 3)
                        dve.wait_ge(b_full, x + (2 * J + 1))
                        nc.vector.tensor_tensor(h[:, k % 2, j, 0:w], h[:, k % 2, j, 0:w], psB[:, j % 2, 0:w], ALU.mult
                                                ).then_inc(b_free, 1)

                if glu:
                    gate(0)
                for k, (u, _, tiles) in enumerate(units):
                    if glu and k + 1 < UC:
                        gate(k + 1)
                    dve.wait_ge(y_full, i * UC + (k + 3))
                    dve.wait_ge(stored[k % 2], i * (8 * UC) + (16 * (k // 2) + 16))
                    src = psY[:, k % 2, 0:tiles * P].rearrange("p (t d) -> p t d", d=D)
                    if b2:
                        nc.vector.tensor_tensor(ys[:, k % 2, 0:tiles], src, b2s[:, u:u + 1].broadcast_to([P, tiles, D]), ALU.add
                                                ).then_inc(y_free, 1)
                    else:
                        nc.vector.tensor_copy(ys[:, k % 2, 0:tiles], src).then_inc(y_free, 1)
                if glu:
                    n.end()
            for g in range(TB):
                dve.wait_ge(gathered[g], (before + 1) * 16 * 2 * TB)
                for k, back in enumerate((m.XN, m.XT3)):
                    if k:
                        dve.wait_ge(summed, 2 * g + 1)
                    for t in range(g * TB, (g + 1) * TB):
                        last = nc.vector.scalar_tensor_tensor(m.X[:, t], back[:, t], m.slot_share[:, k, t:t + 1], m.X[:, t],
                                                              ALU.mult, ALU.add)
                    last.then_inc(summed, 1)

        @block.gpsimd
        def _(pool):
            pool.wait_ge(m.zeroed, 16 * 2)
            for k in range(2):
                for t in range(NT):
                    pool.indirect_dma_start(m.slots_in[0:NS], bass.IndirectOffsetOnAxis(ap=m.slot_to[:, k, t:t + 1], axis=0),
                                            c["rows"][:, t], None, bounds_check=NS - 1, oob_is_err=False
                                            ).then_inc(scattered, 16)
            for s in stored:
                pool.wait_ge(s, 16 * (TOT // 2 + 1))
            for t in range(NT):
                for k, back in enumerate((m.XN, m.XT3)):
                    pool.indirect_dma_start(back[:, t], None, m.slots_out[0:NS],
                                            bass.IndirectOffsetOnAxis(ap=m.slot_from[:, k, t:t + 1], axis=0),
                                            bounds_check=NS - 1, oob_is_err=False).then_inc(gathered[t // TB], 16)


def add_layer(nc, m, name, src, gate, w=None, b=None):
    with ExitStack() as ctx:
        own_v = ctx.enter_context(stage(nc, m, name))("own")
        block = ctx.enter_context(nc.Block())

        @block.sync
        def _(sp):
            clear_last(m, sp)

        @block.vector
        def _(dve):
            own = Own(dve, own_v)
            if w is not None:
                own.done(nc.vector.tensor_tensor(src[:], src[:], w.unsqueeze(1).broadcast_to([P, NT, D]), ALU.mult))
                own.wait()
                own.done(nc.vector.tensor_tensor(src[:], src[:], b.unsqueeze(1).broadcast_to([P, NT, D]), ALU.add))
                own.wait()
            nc.vector.scalar_tensor_tensor(m.X[:], src[:], m.gate(gate), m.X[:], ALU.mult, ALU.add)


def single_head(nc, m):
    nm, w = "L3x", m.w
    SC = 1.0 / float(np.sqrt(np.float32(D)))
    with ExitStack() as ctx:
        sb = lambda s, shape: ctx.enter_context(nc.sbuf_tensor(f"{nm}_{s}", shape, F32))
        ps = lambda s, shape: ctx.enter_context(nc.psum_tensor(f"{nm}_{s}", shape, F32))
        sem = ctx.enter_context(stage(nc, m, nm))
        stats, ln = sb("stats", [P, NT, 6]), sb("ln", [P, 9, NT])
        xn, xnT, ctm = sb("xn", [P, TB, D]), sb("xnT", [P, 512]), sb("ctm", [P, S2])
        KT, G, V, Vr = sb("KT", [P, S2]), sb("G", [P, S2]), sb("V", [P, D]), sb("Vr", [KR, D])
        bqr, nmx, rs, rin = sb("bqr", [P, P]), sb("nmx", [P, TB]), sb("rs", [P, TB]), sb("rin", [P, TB])
        nms = sb("nms", [P, TB])
        pr = sb("pr", [P, TB, S2])
        PT, PTr, OT = sb("PT", [P, 512]), sb("PTr", [KR, 512]), sb("OT", [P, 512])
        psX, psK, psS = ps("psX", [P, 512]), ps("psK", [P, 512]), ps("psS", [P, 2, 512])
        psP, psPr, psO, psY = ps("psP", [P, 512]), ps("psPr", [P, 512]), ps("psO", [P, 512]), ps("psY", [P, 512])
        own_v, var_ready, std_ready = sem("own_v"), sem("var_ready"), sem("std_ready")
        xn_ready, x_full, xt_done, k_full, k_done = sem("xn_ready"), sem("x_full"), sem("xt_done"), sem("k_full"), sem("k_done")
        s_full, m_ready, e_ready, p_ready = sem("s_full"), sem("m_ready"), sem("e_ready"), sem("p_ready")
        p_full, pt_done, o_full, ot_done, y_full, y_done = (
            sem("p_full"), sem("pt_done"), sem("o_full"), sem("ot_done"), sem("y_full"), sem("y_done"))
        block = ctx.enter_context(nc.Block())

        @block.sync
        def _(sp):
            clear_last(m, sp)

        @block.scalar
        def _(act):
            act.wait_ge(var_ready, 1)
            nc.scalar.activation(ln[:, 8], ln[:, 7], ACT.Sqrt).then_inc(std_ready, 1)
            with act.Fori(0, B) as b:
                act.wait_ge(x_full, b + 1)
                nc.scalar.copy(xnT[:], psX[:]).then_inc(xt_done, 1)
                act.wait_ge(k_full, b * 2 + 1)
                nc.scalar.copy(KT[:], psK[:, 0:S2]).then_inc(k_done, 1)
                nc.scalar.copy(V[:], psK[:, 160:160 + D]).then_inc(k_done, 1)
                nc.scalar.copy(Vr[:], psK[0:KR, 288:288 + D]).then_inc(k_done, 1)
                act.wait_ge(k_full, b * 2 + 2)
                nc.scalar.copy(G[:], psK[:, 0:S2]).then_inc(k_done, 1)
                act.wait_ge(m_ready, b + 1)
                for t in range(TB):
                    nc.scalar.activation(pr[:, t], psS[:, t // 2, (t % 2) * S2:(t % 2 + 1) * S2], ACT.Exp, scale=SC,
                                         bias=nms[:, t:t + 1], accum_out=rs[:, t:t + 1]).then_inc(e_ready, 1)
                act.wait_ge(p_full, b + 1)
                nc.scalar.copy(PT[:], psP[:]).then_inc(pt_done, 1)
                nc.scalar.copy(PTr[:], psPr[0:KR]).then_inc(pt_done, 1)
                act.wait_ge(o_full, b + 1)
                nc.scalar.copy(OT[:], psO[:]).then_inc(ot_done, 1)

        @block.tensor
        def _(pe):
            with pe.Fori(0, B) as b:
                pe.wait_ge(xn_ready, b + 1)
                for t in range(TB):
                    last = pe.transpose(psX[:, t * P:(t + 1) * P], xn[:, t], m.ident)
                last.then_inc(x_full, 1)
                pe.matmul(psK[:, 0:S2], w["L3_xattn_Wk"][:], ctm[:], start=True, stop=True, skip_group_check=True)
                pe.matmul(psK[:, 160:160 + D], ctm[:, 0:KM_], w["L3_xattn_Wv"][:], start=False, stop=False, skip_group_check=True)
                pe.matmul(psK[:, 160:160 + D], m.ones[0:1, :], m.row("L3_xattn_bv"), start=False, stop=True, skip_group_check=True)
                pe.matmul(psK[0:KR, 288:288 + D], ctm[:, KM_:S2], w["L3_xattn_Wv"][:], start=False, stop=False, skip_group_check=True)
                pe.matmul(psK[0:KR, 288:288 + D], m.ones[0:1, 0:KR], m.row("L3_xattn_bv"), start=False, stop=True,
                          skip_group_check=True).then_inc(k_full, 1)
                pe.wait_ge(k_done, b * 4 + 3)
                pe.matmul(psK[:, 0:S2], w["L3_xattn_Wq"][:], KT[:], start=True, stop=True).then_inc(k_full, 1)
                pe.wait_ge(k_done, b * 4 + 4)
                pe.wait_ge(xt_done, b + 1)
                for t in range(TB):
                    o = psS[:, t // 2, (t % 2) * S2:(t % 2 + 1) * S2]
                    pe.matmul(o, xnT[:, t * P:(t + 1) * P], G[:], start=(t % 2 == 0), stop=False, skip_group_check=True)
                    pe.matmul(o, bqr[:], KT[:], start=False, stop=True, skip_group_check=True).then_inc(s_full, 1)
                pe.wait_ge(p_ready, b + 1)
                for t in range(TB):
                    pe.transpose(psP[:, t * P:(t + 1) * P], pr[:, t, 0:KM_], m.ident)
                for t in range(TB):
                    last = pe.transpose(psPr[0:KR, t * P:(t + 1) * P], pr[:, t, KM_:S2], m.ident)
                last.then_inc(p_full, 1)
                pe.wait_ge(pt_done, b * 2 + 2)
                pe.matmul(psO[:], V[:], PT[:], start=True, stop=False)
                pe.matmul(psO[:], Vr[:], PTr[:], start=False, stop=True).then_inc(o_full, 1)
                pe.wait_ge(ot_done, b + 1)
                for t in range(TB):
                    o = psY[:, t * P:(t + 1) * P]
                    pe.matmul(o, OT[:, t * P:(t + 1) * P], w["L3_xattn_Wo"][:], start=(t == 0), stop=False, skip_group_check=True)
                    last = pe.matmul(o, m.ones[0:1, :], m.row("L3_xattn_bo"), start=False, stop=(t == TB - 1), skip_group_check=True)
                last.then_inc(y_full, 1)

        @block.vector
        def _(dve):
            own = Own(dve, own_v)
            own.done(nc.vector.tensor_copy(bqr[:], m.col("L3_xattn_bq").broadcast_to([P, P])))
            ln_stats_vector(nc, dve, own, stats, ln, m.X, var_ready, std_ready)
            with dve.Fori(0, B) as b:
                own.loop(b, 7)
                for t in range(TB):
                    tt = b * TB + t
                    own.done(nc.vector.tensor_scalar(xn[:, t], m.X[:, bass.ds(tt, 1), :].rearrange("p o d -> p (o d)"),
                                                     ln[:, 0, bass.ds(tt, 1)], ln[:, 1, bass.ds(tt, 1)], ALU.subtract, ALU.mult))
                own.wait()
                nc.vector.tensor_copy(ctm[:], m.ctxT[:, bass.ds(b, 1), :].rearrange("p o k -> p (o k)")).then_inc(xn_ready, 1)
                dve.wait_ge(s_full, b * TB + TB)
                own.done(nc.vector.tensor_reduce(nmx[:].rearrange("p (a t) -> p a t", a=2),
                                                 psS[:, :, 0:2 * S2].rearrange("p a (t k) -> p a t k", k=S2), AX_X, ALU.max))
                own.wait()
                nc.vector.tensor_scalar(nms[:], nmx[:], -SC, None, ALU.mult).then_inc(m_ready, 1)
                dve.wait_ge(e_ready, b * TB + TB)
                own.done(nc.vector.reciprocal(rin[:], rs[:]))
                own.wait()
                own.done(nc.vector.tensor_tensor(pr[:], pr[:], rin[:].unsqueeze(2).broadcast_to([P, TB, S2]), ALU.mult))
                own.wait()
                nc.vector.memset(stats[:, 0, 0:1], 0.0).then_inc(p_ready, 1)
                dve.wait_ge(y_full, b + 1)
                x = m.X[:, bass.ds(b * TB, TB), :].rearrange("p t d -> p (t d)")
                nc.vector.scalar_tensor_tensor(x, psY[:], m.gate(3), x, ALU.mult, ALU.add).then_inc(y_done, 1)
                dve.wait_ge(y_done, b + 1)
                own.end(B)


def self_attention(nc, m, d):
    nm, w = "L3s", m.w
    BF = mybir.dt.bfloat16
    DH = D // H
    TR = 9 * DH
    SC = 1.0 / float(np.sqrt(8.0))
    q_parts = nc.dram_tensor("q_parts", (3, 3, P, NT * P), BF).ap()
    k_parts = nc.dram_tensor("k_parts", (3, P, NT * P), BF).ap()
    max_parts = nc.dram_tensor("max_parts", (B * HG, 3, HG, S), BF).ap()
    with ExitStack() as ctx0:
        VW = H * (DH + 1) + 24
        V = ctx0.enter_context(nc.sbuf_tensor(f"{nm}_V", [P, NT, VW], F32))
        Vh = V[:, :, 0:H * (DH + 1)].rearrange("p t (h d) -> p t h d", d=DH + 1)
        with ExitStack() as ctx:
            sb = lambda s, shape, dt=F32: ctx.enter_context(nc.sbuf_tensor(f"{nm}_{s}", shape, dt))
            sem = ctx.enter_context(stage(nc, m, nm))
            C = NT // TB
            ps = ctx.enter_context(nc.psum_tensor(f"{nm}_psP", [P, 2, 512], F32))
            psV = ctx.enter_context(nc.psum_tensor(f"{nm}_psV", [P, 2, 512], F32))
            parts = sb("parts", [P, 2, 3, NT * P], BF)
            full, rest = sb("full", [P, 2, 512]), sb("rest", [P, 2, 512])
            qb = sb("qb", [P, 1])
            qb_ready, p_full, f_ready, hi_ready = sem("qb_ready"), sem("p_full"), sem("f_ready"), sem("hi_ready")
            r_ready, mid_ready, lo_ready = sem("r_ready"), sem("mid_ready"), sem("lo_ready")
            v_full, v_done, stored = sem("v_full"), sem("v_done"), sem("stored")
            block = ctx.enter_context(nc.Block())

            @block.tensor
            def _(pe):
                for k in range(2):
                    for c in range(C):
                        n = k * C + c
                        if n >= 2:
                            pe.wait_ge(f_ready, n - 1)
                        pe.matmul(ps[:, n % 2], w["L3_ffn_q_w" if k == 0 else "L3_ffn_k_w"][:], m.XT[:, c * 512:(c + 1) * 512],
                                  start=True, stop=True).then_inc(p_full, 1)
                for c in range(C):
                    if c >= 2:
                        pe.wait_ge(v_done, c - 1)
                    for t in range(TB):
                        o = psV[:, c % 2, t * P:(t + 1) * P]
                        tt = c * TB + t
                        pe.matmul(o, m.XT[:, tt * P:(tt + 1) * P], w["L3_ffn_v_w"][:], start=(t == 0), stop=False, skip_group_check=True)
                        last = pe.matmul(o, m.ones[0:1, :], m.row("L3_ffn_v_b"), start=False, stop=(t == TB - 1), skip_group_check=True)
                    last.then_inc(v_full, 1)

            @block.scalar
            def _(act):
                act.wait_ge(qb_ready, 1)
                for k in range(2):
                    for c in range(C):
                        n = k * C + c
                        cs = slice(c * 512, (c + 1) * 512)
                        act.wait_ge(p_full, n + 1)
                        if n >= 2:
                            act.wait_ge(r_ready, n - 1)
                        if k == 0:
                            nc.scalar.activation(full[:, n % 2], ps[:, n % 2], ACT.Identity, scale=SC, bias=qb[:]).then_inc(f_ready, 1)
                        else:
                            nc.scalar.activation(full[:, n % 2], ps[:, n % 2], ACT.Identity, bias=m.col("L3_ffn_k_b")).then_inc(f_ready, 1)
                        act.wait_ge(f_ready, n + 1)
                        nc.scalar.copy(parts[:, k, 0, cs], full[:, n % 2]).then_inc(hi_ready, 1)
                        act.wait_ge(r_ready, n + 1)
                        nc.scalar.copy(parts[:, k, 1, cs], rest[:, n % 2]).then_inc(mid_ready, 1)
                for c in range(C):
                    act.wait_ge(v_full, c + 1)
                    nc.scalar.copy(Vh[:, c * TB:(c + 1) * TB, :, 0:DH],
                                   psV[:, c % 2].rearrange("p (t h d) -> p t h d", h=H, d=DH)).then_inc(v_done, 1)

            @block.vector
            def _(dve):
                nc.vector.tensor_scalar(qb[:], m.col("L3_ffn_q_b"), SC, None, ALU.mult).then_inc(qb_ready, 1)
                nc.vector.memset(Vh[:, :, :, DH:DH + 1], 1.0)
                nc.vector.memset(V[:, :, H * (DH + 1):VW], 0.0)
                for k in range(2):
                    for c in range(C):
                        n = k * C + c
                        cs = slice(c * 512, (c + 1) * 512)
                        dve.wait_ge(hi_ready, n + 1)
                        if n >= 2:
                            dve.wait_ge(lo_ready, n - 1)
                        nc.vector.tensor_tensor(rest[:, n % 2], full[:, n % 2], parts[:, k, 0, cs], ALU.subtract).then_inc(r_ready, 1)
                        dve.wait_ge(mid_ready, n + 1)
                        nc.vector.tensor_tensor(parts[:, k, 2, cs], rest[:, n % 2], parts[:, k, 1, cs], ALU.subtract).then_inc(lo_ready, 1)

            @block.sync
            def _(sp):
                clear_last(m, sp)
                sp.wait_ge(lo_ready, C)
                for i in range(3):
                    sp.dma_start(q_parts[i].rearrange("j p t -> p j t"), parts[:, 0, i:i + 1].broadcast_to([P, 3, NT * P])
                                 ).then_inc(stored, 16)
                sp.wait_ge(lo_ready, 2 * C)
                sp.dma_start(k_parts.rearrange("s p t -> p s t"), parts[:, 1]).then_inc(stored, 16)
                sp.wait_ge(stored, 64)

        with ExitStack() as ctx:
            sb = lambda s, shape, dt=F32: ctx.enter_context(nc.sbuf_tensor(f"{nm}_{s}", shape, dt))
            ps = lambda s, shape: ctx.enter_context(nc.psum_tensor(f"{nm}_{s}", shape, F32))
            sem = ctx.enter_context(stage(nc, m, nm))
            QS, KS = sb("QS", [TR + 3, 4, HG, S], BF), sb("KS", [TR + 3, 4, HG, S], BF)
            identb, trilb, triub = sb("identb", [P, P], BF), sb("trilb", [P, P], BF), sb("triub", [P, P], BF)
            onesb = sb("onesb", [3, HG, S], BF)
            mx, mr = sb("mx", [P, TB, HG]), sb("mr", [P, 2, TB, HG])
            mparts = sb("mparts", [P, TB, 3, HG], BF)
            MT = sb("MT", [3 * HG, 2, S], BF)
            EO = {0: 0, 1: S, 3: 2 * S - P, 2: 2 * S}
            EW = 2 * S + 2 * P
            E = sb("E", [P, 2, HG, EW])
            VW4 = 3 * (DH + 1) + 32
            VG = sb("VG", [P, 2, TB, VW4])
            OG, rin, OT = sb("OG", [P, S]), sb("rin", [P, TB, HG, 1]), sb("OT", [P, 2, S])
            psS, psT, psO, psM = ps("psS", [P, 3, 512]), ps("psT", [P, 3, 512]), ps("psO", [P, 512]), ps("psM", [P, 512])
            own_v, const_ready = sem("own_v2"), sem("const_ready")
            ones_in, max_out, stack_in, max_in = sem("ones_in"), sem("max_out"), [sem(f"stack_in{u}") for u in range(4)], [sem("max_in0"), sem("max_in1")]
            s_full, s_free, t_full, t_free = sem("s_full"), sem("s_free"), sem("t_full"), sem("t_free")
            mp_ready, tm_full, tm_done = sem("mp_ready"), sem("tm_full"), sem("tm_done")
            vg_ready, av_full, og_done, to_full = sem("vg_ready"), sem("av_full"), sem("og_done"), sem("to_full")
            rin_done, divided = sem("rin_done"), sem("divided")
            ot_full, ot_done, y_full, y_done = sem("ot_full"), sem("ot_done"), sem("y_full"), sem("y_done")
            block = ctx.enter_context(nc.Block())
            NGR = B * HG
            SG = [[3], [2, 0], [1]]
            TG = [[0], [1, 3], [2]]
            ND = 4 * 16

            def place(group, width):
                at, out = 0, []
                for t in group:
                    out.append((t, at, width(t)))
                    at += width(t)
                return out

            class At:

                def __init__(self, i, r):
                    self.i, self.r = i, r
                    self.slot, self.par, self.hg, self.b = r % 4, r % 2, r % 4, i + r // 4

                def __add__(self, k):
                    return At(self.i, self.r + k)

                def exists(self):
                    return not isinstance(self.i, int) or 0 <= self.r < NGR

                def n(self, per, add):
                    return self.i * (4 * per) + (self.r * per + add)

            def over_steps(eng, step, around=lambda i: None):
                for g in range(-2, 2):
                    step(At(0, g))
                with eng.Fori(0, (NGR - 4) // 4) as i:
                    around(i)
                    for r in range(2, 6):
                        step(At(i, r))
                around(None)
                for g in range(NGR - 2, NGR + 2):
                    step(At(0, g))

            @block.sync
            def _(sp):
                clear_last(m, sp)

                def stacks(g):
                    cols = bass.ds(g.b * S, S) if not isinstance(g.b, int) else slice(g.b * S, (g.b + 1) * S)
                    heads = slice(g.hg * HG, (g.hg + 1) * HG)
                    sp.dma_start(QS[0:TR, g.slot], q_parts.rearrange("i j (d h) t -> (i j d) h t", h=H)[:, heads, cols]
                                 ).then_inc(stack_in[g.slot], 16)
                    for i in range(3):
                        sp.dma_start(KS[3 * i * DH:3 * (i + 1) * DH, g.slot],
                                     k_parts.rearrange("s (d h) t -> (s d) h t", h=H)[:, heads, cols]
                                     ).then_inc(stack_in[g.slot], 16)

                def maxima_to(g):
                    sp.wait_ge(tm_done, g.n(1, 1))
                    at = max_parts[bass.ds(g.n(1, 0), 1)] if not isinstance(g.i, int) else max_parts[g.r:g.r + 1]
                    sp.dma_start(at.rearrange("o s h t -> (o s h) t"), MT[:, g.par]).then_inc(max_out, 16)
                    sp.wait_ge(max_out, g.n(16, 16))
                    sp.dma_start(QS[TR:TR + 3, g.slot], at.rearrange("o s h t -> (o s) h t")).then_inc(max_in[g.par], 16)

                for g in range(2):
                    stacks(At(0, g))
                sp.wait_ge(const_ready, 1)
                for u in range(4):
                    sp.dma_start(KS[TR:TR + 3, u], onesb[:]).then_inc(ones_in, 16)
                for g in range(2, 4):
                    stacks(At(0, g))
                maxima_to(At(0, 0))
                with sp.Fori(0, (NGR - 4) // 4) as i:
                    for r in range(4):
                        maxima_to(At(i, r) + 1)
                        sp.wait_ge(t_full, At(i, r).n(12, 12))
                        stacks(At(i, r) + 4)
                for g in range(NGR - 3, NGR):
                    maxima_to(At(0, g))

            @block.gpsimd
            def _(pool):
                with pool.Fori(0, B) as i:
                    for r in range(4):
                        g = At(i, r)
                        pool.wait_ge(av_full, g.n(1, 1))
                        nc.gpsimd.tensor_copy(VG[:, g.par], V[:, bass.ds(i * TB, TB), r * HG * (DH + 1):r * HG * (DH + 1) + VW4]
                                              ).then_inc(vg_ready, 1)

            @block.tensor
            def _(pe):
                pe.sem_inc(s_free, 3)
                pe.sem_inc(t_free, 3)
                pe.sem_inc(av_full, 2)
                pe.sem_inc(og_done, 1)
                pe.sem_inc(to_full, 1)
                pe.sem_inc(divided, 1)
                pe.wait_ge(const_ready, 1)

                def scores(g, h):
                    if h == 0:
                        pe.wait_ge(stack_in[g.slot], g.b * ND + ND)
                    for k, group in enumerate(SG):
                        pe.wait_ge(s_free, g.n(12, 3 * h + k + 1))
                        tiles = place(group, lambda t: (t + 1) * P)
                        for n, (t, at, wd) in enumerate(tiles):
                            pe.matmul(psS[:, k, at:at + wd], QS[0:TR, g.slot, h, t * P:(t + 1) * P], KS[0:TR, g.slot, h, 0:wd],
                                      start=(n == 0), stop=False, skip_group_check=True)
                            last = pe.matmul(psS[:, k, at + wd - P:at + wd], identb[:], trilb[:], start=False,
                                             stop=(n == len(tiles) - 1), skip_group_check=True)
                        last.then_inc(s_full, 1)

                def shifted(g, h):
                    if h == 0:
                        pe.wait_ge(max_in[g.par], g.i * 32 + 16 * (g.r // 2 + 1))
                    for k, group in enumerate(TG):
                        pe.wait_ge(t_free, g.n(12, 3 * h + k + 1))
                        tiles = place(group, lambda t: (TB - t) * P)
                        for n, (t, at, wd) in enumerate(tiles):
                            pe.matmul(psT[:, k, at:at + wd], KS[0:TR + 3, g.slot, h, t * P:(t + 1) * P], QS[0:TR + 3, g.slot, h, t * P:S],
                                      start=(n == 0), stop=False, skip_group_check=True)
                            last = pe.matmul(psT[:, k, at:at + P], identb[:], triub[:], start=False,
                                             stop=(n == len(tiles) - 1), skip_group_check=True)
                        last.then_inc(t_full, 1)

                def values(g, j):
                    if j == 0:
                        pe.wait_ge(t_free, g.n(12, 15))
                        pe.wait_ge(vg_ready, g.n(1, 1))
                        pe.wait_ge(og_done, g.n(1, 1))
                    for h in range(HG):
                        last = pe.matmul(psO[32 * h:32 * h + 32, j * P:S], VG[:, g.par, j, h * (DH + 1):h * (DH + 1) + 32],
                                         E[:, g.par, h, EO[j]:EO[j] + S - j * P], start=(j == 0), stop=(j == TB - 1),
                                         skip_group_check=True)
                    if j == TB - 1:
                        last.then_inc(av_full, 1)

                def turn_maxima(g):
                    pe.wait_ge(mp_ready, g.n(1, 1))
                    if not isinstance(g.i, int) or g.r >= 3:
                        pe.wait_ge(divided, g.n(1, -2))
                    for t in range(TB):
                        last = pe.transpose(psM[0:3 * HG].bitcast(BF)[:, t * P:(t + 1) * P], mparts[:, t].rearrange("p s h -> p (s h)"), identb[:])
                    last.then_inc(tm_full, 1)

                def turn_outputs(g):
                    pe.wait_ge(og_done, g.n(1, 2))
                    pe.wait_ge(tm_done, g.n(1, 4) if not isinstance(g.i, int) else min(g.r + 4, NGR))
                    pe.wait_ge(divided, g.n(1, 1))
                    for t in range(TB):
                        last = pe.transpose(psM[:, t * P:(t + 1) * P], OG[:, t * P:(t + 1) * P], m.ident)
                    last.then_inc(to_full, 1)

                def step(g):
                    for h in range(HG):
                        if (g + 2).exists():
                            scores(g + 2, h)
                        if h == 1 and (g + 1).exists():
                            turn_maxima(g + 1)
                        if h == 2 and (g + -2).exists():
                            turn_outputs(g + -2)
                        if (g + -1).exists():
                            values(g + -1, h)
                        if g.exists():
                            if isinstance(g.i, int) and g.r == 0 and h == 0:
                                pe.wait_ge(ones_in, 64)
                            shifted(g, h)

                over_steps(pe, step)
                for b in range(B):
                    pe.wait_ge(divided, NGR + 1)
                    if b == 0:
                        pe.wait_ge(t_free, 12 * NGR + 3)
                        pe.wait_ge(s_free, 12 * NGR + 3)
                    for t in range(TB):
                        last = pe.transpose(psT[:, b % 2, t * P:(t + 1) * P], m.X1[:, b * TB + t], m.ident)
                    last.then_inc(ot_full, 1)
                    pe.wait_ge(ot_done, b + 1)
                    if b >= 2:
                        pe.wait_ge(y_done, b - 1)
                    for t in range(TB):
                        o = psS[:, b % 2, t * P:(t + 1) * P]
                        pe.matmul(o, OT[:, b % 2, t * P:(t + 1) * P], w["L3_ffn_o_w"][:], start=(t == 0), stop=False, skip_group_check=True)
                        last = pe.matmul(o, m.ones[0:1, :], m.row("L3_ffn_o_b"), start=False, stop=(t == TB - 1), skip_group_check=True)
                    last.then_inc(y_full, 1)

            @block.scalar
            def _(act):
                def exponentials(g, h):
                    if h == 0:
                        act.wait_ge(av_full, g.n(1, 1))
                    for k, group in enumerate(TG):
                        act.wait_ge(t_full, g.n(12, 3 * h + k + 1))
                        wd = sum((TB - t) * P for t in group)
                        nc.scalar.activation(E[:, g.par, h, EO[group[0]]:EO[group[0]] + wd], psT[:, k, 0:wd], ACT.Exp
                                             ).then_inc(t_free, 1)

                def step(g):
                    for h in range(HG):
                        if h == 1 and (g + 1).exists():
                            x = g + 1
                            act.wait_ge(tm_full, x.n(1, 1))
                            if not isinstance(x.i, int) or x.r >= 2:
                                act.wait_ge(max_in[x.par], x.i * 32 + 16 * (x.r // 2))
                            nc.scalar.copy(MT[:, x.par], psM[0:3 * HG].bitcast(BF)[:, 0:S]).then_inc(tm_done, 1)
                        if h == 3 and (g + -1).exists():
                            x = g + -1
                            act.wait_ge(av_full, x.n(1, 3))
                            act.wait_ge(to_full, x.n(1, 1))
                            nc.scalar.copy(OG[:], psO[:]).then_inc(og_done, 1)
                        if g.exists():
                            exponentials(g, h)

                over_steps(act, step)
                for b in range(B):
                    act.wait_ge(ot_full, b + 1)
                    if b >= 2:
                        act.wait_ge(y_full, b - 1)
                    nc.scalar.copy(OT[:, b % 2], psT[:, b % 2]).then_inc(ot_done, 1)

            @block.vector
            def _(dve):
                own = Own(dve, own_v)
                own.done(nc.vector.memset(onesb[:], 1.0))
                own.done(nc.vector.tensor_copy(identb[:], m.ident))
                own.done(nc.vector.tensor_copy(trilb[:], m.const["tril"]))
                own.wait()
                nc.vector.tensor_copy(triub[:], m.const["triu"]).then_inc(const_ready, 1)

                def maxima(g, h):
                    for k, group in enumerate(SG):
                        dve.wait_ge(s_full, g.n(12, 3 * h + k + 1))
                        for t, at, wd in place(group, lambda t: (t + 1) * P):
                            last = nc.vector.tensor_reduce(mx[:, t, h:h + 1], psS[:, k, at:at + wd], AX_X, ALU.max)
                        last.then_inc(s_free, 1)

                def cut_maxima(g):
                    dve.wait_ge(s_free, g.n(12, 15))
                    if not isinstance(g.i, int) or g.r >= 1:
                        dve.wait_ge(tm_full, g.n(1, 0))
                    own.done(nc.vector.tensor_scalar(mr[:, 0], mx[:], -1.0, None, ALU.mult))
                    own.wait()
                    own.done(nc.vector.tensor_copy(mparts[:, :, 0], mr[:, 0]))
                    own.wait()
                    own.done(nc.vector.tensor_tensor(mr[:, 1], mr[:, 0], mparts[:, :, 0], ALU.subtract))
                    own.wait()
                    own.done(nc.vector.tensor_copy(mparts[:, :, 1], mr[:, 1]))
                    own.wait()
                    nc.vector.tensor_tensor(mparts[:, :, 2], mr[:, 1], mparts[:, :, 1], ALU.subtract).then_inc(mp_ready, 1)
                    dve.wait_ge(mp_ready, g.n(1, 1))

                def divide(g):
                    out = psM[:].rearrange("p (t h d) -> p t h d", t=TB, h=HG)
                    dve.wait_ge(to_full, g.n(1, 2))
                    dve.wait_ge(divided, g.n(1, 1))
                    nc.vector.reciprocal(rin[:], out[:, :, :, DH:DH + 1]).then_inc(rin_done, 1)
                    dve.wait_ge(rin_done, g.n(1, 1))
                    rows = bass.ds(g.b * TB, TB) if not isinstance(g.b, int) else slice(g.b * TB, (g.b + 1) * TB)
                    dst = m.X1[:, rows, g.hg * HG * DH:(g.hg + 1) * HG * DH].rearrange("p t (h d) -> p t h d", d=DH)
                    nc.vector.tensor_tensor(dst, out[:, :, :, 0:DH], rin[:].broadcast_to([P, TB, HG, DH]), ALU.mult
                                            ).then_inc(divided, 1)

                def step(g):
                    for h in range(HG):
                        if (g + 2).exists():
                            maxima(g + 2, h)
                        if h == 3 and (g + -2).exists():
                            divide(g + -2)
                    if (g + 2).exists():
                        cut_maxima(g + 2)

                def around(i):
                    if i is not None:
                        own.loop(i, 16)
                    else:
                        own.end((NGR - 4) // 4)

                over_steps(dve, step, around)
                for b in range(B):
                    dve.wait_ge(y_full, b + 1)
                    x = m.XN[:, b * TB:(b + 1) * TB].rearrange("p t d -> p (t d)")
                    nc.vector.tensor_tensor(x, x, psS[:, b % 2], ALU.add).then_inc(y_done, 1)


def hd(h):
    return slice(h, h + 1) if isinstance(h, int) else bass.ds(h, 1)


def stage_list(nc, m, d, upto):
    w = m.w

    def share(E, split):
        return lambda i, U, u, q, t: m.comb[:, t, bass.ds(i * (U * split) + (u * split + q), 1)]

    attention(nc, m, dict(name="L0", dv=8, tiles=range(TB), mode="bias", gate=0, weights=[],
                          wq=w["L0_xattn_Wq"][:], wk=w["L0_xattn_Wk"][:], wv=w["L0_xattn_Wv"][:],
                          wo=w["L0_xattn_Wo"][:].unsqueeze(1)))
    norm_transpose(nc, m, "L0n1", m.X1, m.XN, m.col("L0_xattn_g1"), m.col("L0_xattn_be1"))
    experts(nc, m, "L0h", dict(w1=d["L0_xattn_W1"].unsqueeze(0), w2=d["L0_xattn_W2"].unsqueeze(0), act=ACT.Gelu,
                               b1=d["L0_xattn_b1"].unsqueeze(0), b2=lambda i, U, u: m.row("L0_xattn_b2"),
                               dst=m.X1, share=lambda *a: m.ones[:, 0:1]))
    norm_transpose(nc, m, "L0n2", m.X1, m.XN, turn=False)
    add_layer(nc, m, "L0a", m.XN, 0, m.wide("L0_xattn_g2"), m.wide("L0_xattn_be2"))
    if upto == 0: return
    norm_transpose(nc, m, "L0r", m.X, m.XN, router=dict(E=8, kind="L0", w=w["L0_ffn_Wr"][:], gate=4, comb=m.comb[:, :, 0:8]))
    m.slots_in, m.slots_out = m.slots0, nc.dram_tensor("results0", (8 * CAP0, D), F32).ap()
    routed_experts(nc, m, "L0f", dict(w1=d["L0_ffn_W1"], w3=d["L0_ffn_W3"], w2=d["L0_ffn_W2"], act=ACT.Silu, rows=m.XN,
                                      U=2, chunks=[3, 2], before=0))
    if upto == 1: return
    attention(nc, m, dict(name="L1", dv=64, tiles=range(TB), mode="mask", gate=1, weights=[],
                          wq=w["L1_xattn_W_Q"][:], wk=w["L1_xattn_W_K"][:], wv=w["L1_xattn_W_V"][:],
                          wo=w["L1_xattn_W_O"][:]))
    if upto == 2: return
    norm_transpose(nc, m, "L1r", m.X, m.XN, router=dict(E=16, kind="L1", w=w["L1_ffn_router_w"][:], gate=5, comb=m.comb[:]))
    experts(nc, m, "L1s", dict(w1=d["L1_ffn_sh_gate"], w3=d["L1_ffn_sh_up"], w2=d["L1_ffn_sh_down"], act=ACT.Silu,
                               dst=m.X, share=lambda *a: m.gate(5)))
    experts(nc, m, "L1f", dict(w1=d["L1_ffn_gate_proj"], w3=d["L1_ffn_up_proj"], w2=d["L1_ffn_down_proj"], act=ACT.Silu,
                               dst=m.X, share=share(16, 2), split=2))
    if upto == 3: return
    attention(nc, m, dict(name="L2", dv=8, tiles=[2, 3], mode="causal", gate=2, weights=[],
                          wq=w["L2_xattn_Wq"][:], wk=w["L2_xattn_Wk"][:], wv=w["L2_xattn_Wv"][:],
                          wo=w["L2_xattn_Wo"][:].unsqueeze(1)))
    if upto == 4: return
    norm_transpose(nc, m, "L2r", m.X, m.XN, router=dict(E=8, kind="L2", w=w["L2_ffn_Wr"][:], gate=6, comb=m.comb[:, :, 0:8]))
    experts(nc, m, "L2f", dict(w1=d["L2_ffn_W1"], w2=d["L2_ffn_W2"], act=ACT.Silu, dst=m.X, share=share(8, 1)))
    if upto == 5: return
    single_head(nc, m)
    if upto == 6: return
    norm_transpose(nc, m, "L3n0", m.X, m.XN, turn=False)
    norm_transpose(nc, m, "L3n1", m.XN, m.X1, m.col("L3_ffn_ln1_w"), m.col("L3_ffn_ln1_b"))
    self_attention(nc, m, d)
    norm_transpose(nc, m, "L3r", m.XN, m.X1, m.col("L3_ffn_ln2_w"), m.col("L3_ffn_ln2_b"),
                   router=dict(E=16, kind="L3", w=w["L3_ffn_router_w"][:], gate=7, comb=m.comb[:]))
    add_layer(nc, m, "L3a", m.XN, 7)
    m.slots_in, m.slots_out = m.slots3, nc.dram_tensor("results3", (16 * CAP3, D), F32).ap()
    routed_experts(nc, m, "L3f", dict(w1=d["L3_ffn_fc1_w"], w2=d["L3_ffn_fc2_w"], b1=d["L3_ffn_fc1_b"], b2=d["L3_ffn_fc2_b"],
                                      act=ACT.Gelu, rows=m.X1, scale=m.col("L3_ffn_ln2_w"), bias=m.col("L3_ffn_ln2_b"),
                                      U=4, chunks=[2], before=1))


def _t(a):
    return a.T


def _dh(a):
    return a.reshape(a.shape[:-1] + (H, D // H)).swapaxes(-1, -2).reshape(a.shape)


INPUTS = {
    "x": lambda a: a.reshape(NT, P, D),
    "ctx_1024": lambda a: a.transpose(2, 0, 1),
    "fside_Bx16xSxS2_0": lambda a: a,
    "mask_1x1xSxS2_ik0": lambda a: a.reshape(S, S2),
    "g_xattn": lambda a: a.reshape(1, 4),
    "g_ffn": lambda a: a.reshape(1, 4),
    "L0_xattn_Wq": lambda a: a, "L0_xattn_Wk": _t, "L0_xattn_Wv": _t, "L0_xattn_Wo": _t,
    "L0_xattn_W1": _t, "L0_xattn_b1": lambda a: a.reshape(4, P).T, "L0_xattn_W2": lambda a: a.T.reshape(4, P, D).transpose(1, 0, 2),
    "L0_ffn_Wr": lambda a: a, "L0_ffn_W1": lambda a: a, "L0_ffn_W3": lambda a: a,
    "L0_ffn_W2": lambda a: a.reshape(8, 4, P, D).transpose(0, 2, 1, 3),
    "L1_xattn_W_Q": lambda a: a.T.reshape(8, P, D).transpose(1, 0, 2), "L1_xattn_W_K": lambda a: a,
    "L1_xattn_W_V": lambda a: a, "L1_xattn_W_O": lambda a: a.reshape(8, P, D).transpose(1, 0, 2),
    "L1_ffn_router_w": _t,
    "L1_ffn_router_bias": lambda a: a.reshape(1, 16),
    "L1_ffn_up_proj": lambda a: a.reshape(8, 2, D, 64).transpose(0, 2, 1, 3).reshape(8, D, P),
    "L1_ffn_gate_proj": lambda a: a.reshape(8, 2, D, 64).transpose(0, 2, 1, 3).reshape(8, D, P),
    "L1_ffn_down_proj": lambda a: a.reshape(8, P, 1, D),
    "L1_ffn_sh_gate": lambda a: a.T.reshape(1, D, P), "L1_ffn_sh_up": lambda a: a.T.reshape(1, D, P),
    "L1_ffn_sh_down": lambda a: a.T.reshape(1, P, 1, D),
    "L2_xattn_Wq": _t, "L2_xattn_Wk": lambda a: a, "L2_xattn_Wv": lambda a: a, "L2_xattn_Wo": lambda a: a,
    "L2_ffn_Wr": _t, "L2_ffn_W1": lambda a: a, "L2_ffn_W2": lambda a: a.reshape(8, 4, P, D).transpose(0, 2, 1, 3),
    "L3_xattn_Wk": _t, "L3_xattn_Wv": _t, "L3_xattn_Wq": lambda a: a, "L3_xattn_Wo": _t,
    "L3_ffn_q_w": _dh, "L3_ffn_k_w": _dh, "L3_ffn_v_w": lambda a: a, "L3_ffn_o_w": lambda a: a,
    "L3_ffn_router_w": lambda a: a, "L3_ffn_fc1_w": lambda a: a,
    "L3_ffn_fc1_b": lambda a: a.reshape(16, 4, P).transpose(0, 2, 1),
    "L3_ffn_fc2_w": lambda a: a.reshape(16, 4, P, D).transpose(0, 2, 1, 3),
    "L3_ffn_fc2_b": lambda a: a.reshape(16, 1, D),
}
KEPT = ["L0_xattn_Wk", "L0_xattn_Wv", "L0_xattn_Wq", "L0_xattn_Wo", 
        "L0_ffn_Wr", "L1_xattn_W_Q", "L1_xattn_W_K", "L1_xattn_W_V", "L1_xattn_W_O", "L1_ffn_router_w",
        "L2_xattn_Wq", "L2_xattn_Wk", "L2_xattn_Wv", "L2_xattn_Wo", "L2_ffn_Wr",
        "L3_xattn_Wk", "L3_xattn_Wv", "L3_xattn_Wq", "L3_xattn_Wo",
        "L3_ffn_q_w", "L3_ffn_k_w", "L3_ffn_v_w", "L3_ffn_o_w", "L3_ffn_router_w"]


def setup(nc, ctx, m, d):
    sb = lambda s, shape: ctx.enter_context(nc.sbuf_tensor(s, shape, F32))
    m.X, m.XN, m.X1, m.XT = (sb(s, [P, NT, D]) for s in ("X", "XN", "X1", "XT"))
    m.XT3 = m.XT
    m.XT = m.XT[:].rearrange("p t d -> p (t d)")
    const = sb("const", list(CONSTS.shape))
    m.const = {}
    for name, (at, w) in CONST.items():
        m.const[name] = const[:, at:at + w]
    m.ident, m.ones, m.first, m.rest = (m.const[k] for k in ("ident", "ones", "first", "rest"))
    m.head8, m.head64 = m.const["head8"], m.const["head64"]
    m.causal = [m.const["causal%d" % i] for i in range(TB)]
    rows, cols = sb("rows", [P, len(ROWS), D]), sb("cols", [P, len(COLS)])
    m.row = lambda s: rows[0:1, ROWS.index(s), :]
    m.wide = lambda s: rows[:, ROWS.index(s), :]
    m.col = lambda s: cols[:, COLS.index(s):COLS.index(s) + 1]
    gates = sb("gates", [P, 8])
    m.gate = lambda k: gates[:, k:k + 1]
    m.ctxT = sb("ctxT", [P, B, S2])
    m.comb = sb("comb", [P, NT, 16])
    m.slot_share = sb("slot_share", [P, 2, NT])
    m.slot_to, m.slot_from = (ctx.enter_context(nc.sbuf_tensor(s, [P, 2, NT], I32)) for s in ("slot_to", "slot_from"))
    m.slots0, m.slots3 = nc.dram_tensor("slots0", (8 * CAP0, D), F32).ap(), nc.dram_tensor("slots3", (16 * CAP3, D), F32).ap()
    m.scattered = ctx.enter_context(nc.semaphore("scattered"))
    m.gathered = [ctx.enter_context(nc.semaphore(f"gathered{g}")) for g in range(TB)]
    m.zeroed = ctx.enter_context(nc.semaphore("zeroed"))
    zeros, zeros_ready = sb("zeros", [P, 512]), ctx.enter_context(nc.semaphore("zeros_ready"))
    m.w = {}
    for k in KEPT:
        shape = list(d[k].shape)
        m.w[k] = sb("w_" + k, shape)
    rb = sb("router_bias", [P, 16])
    m.router_bias = rb
    loaded, gates_in = ctx.enter_context(nc.semaphore("loaded")), ctx.enter_context(nc.semaphore("gates_in"))
    tanh_done = ctx.enter_context(nc.semaphore("tanh_done"))
    with nc.Block() as block:
        @block.sync
        def _(sp):
            clear_last(m, sp)
            n = 0
            for dst, src in [(const[:], d["consts"]), (cols[:], d["cols"]), (m.ctxT[:], d["ctx_1024"]),
                             (m.X[:], d["x"].rearrange("t p d -> p t d"))]:
                sp.dma_start(dst, src).then_inc(loaded, 16)
                n += 16
            sp.dma_start(rows[:], d["rows"].unsqueeze(0).broadcast_to([P, len(ROWS), D])).then_inc(loaded, 16)
            sp.dma_start(rb[:], d["L1_ffn_router_bias"].broadcast_to([P, 16])).then_inc(loaded, 16)
            n += 32
            for k in KEPT:
                sp.dma_start(m.w[k][:], d[k]).then_inc(loaded, 16)
                n += 16
            sp.wait_ge(loaded, n)

        @block.vector
        def _(dve):
            nc.vector.memset(zeros[:], 0.0).then_inc(zeros_ready, 1)

        @block.gpsimd
        def _(pool):
            pool.wait_ge(zeros_ready, 1)
            for table in (m.slots0, m.slots3):
                r = table.shape[0] * D // P // 512
                pool.dma_start(table.rearrange("(p r) d -> p (r d)", p=P).rearrange("p (r f) -> p r f", f=512),
                               zeros[:].unsqueeze(1).broadcast_to([P, r, 512])).then_inc(m.zeroed, 16)

        @block.scalar
        def _(act):
            act.dma_start(gates[:, 0:4], d["g_xattn"].broadcast_to([P, 4])).then_inc(gates_in, 16)
            act.dma_start(gates[:, 4:8], d["g_ffn"].broadcast_to([P, 4])).then_inc(gates_in, 16)
            act.wait_ge(gates_in, 32)
            nc.scalar.activation(gates[:], gates[:], ACT.Tanh).then_inc(tanh_done, 1)
            act.wait_ge(tanh_done, 1)


def program(nc, d, out, upto=99):
    m = Model()
    m.mask, m.bias = d["mask_1x1xSxS2_ik0"], d["fside_Bx16xSxS2_0"]
    with ExitStack() as ctx:
        setup(nc, ctx, m, d)
        stage_list(nc, m, d, upto)
        res = m.X
        stored = ctx.enter_context(nc.semaphore("stored"))
        with nc.Block() as block:
            @block.sync
            def _(sp):
                sp.dma_start(out.rearrange("t p d -> p t d"), res[:]).then_inc(stored, 16)
                sp.wait_ge(stored, 16)


def kernel(**inputs):
    import concourse.bacc as bacc
    from concourse.bass_utils import run_bass_kernel_spmd

    nc = bacc.Bacc("TRN2", target_bir_lowering=False, num_devices=1)
    arrays, d = {}, {}
    laid = {k: np.ascontiguousarray(f(np.asarray(inputs[k]))) for k, f in INPUTS.items()}
    laid["rows"] = np.stack([np.asarray(inputs[k]) for k in ROWS])
    laid["cols"] = np.ascontiguousarray(np.stack(
        [_dh(np.asarray(inputs[k])) if k in ("L3_ffn_q_b", "L3_ffn_k_b") else np.asarray(inputs[k]) for k in COLS], 1))
    laid["consts"] = CONSTS
    for k, a in laid.items():
        arrays["in_" + k] = a
        d[k] = nc.dram_tensor("in_" + k, a.shape, mybir.dt.from_np(a.dtype), kind="ExternalInput").ap()
    out = nc.dram_tensor("out", (NT, P, D), F32, kind="ExternalOutput").ap()
    program(nc, d, out)
    r = run_bass_kernel_spmd(nc, [arrays], core_ids=[0])
    return r.results[0]["out"].reshape(B, S, D)
```

```python
from contextlib import ExitStack, contextmanager

import numpy as np
import concourse.bass as bass
from concourse import mybir

ALU = mybir.AluOpType
ACT = mybir.ActivationFunctionType
F32 = mybir.dt.float32
I32 = mybir.dt.int32
AX_X = mybir.AxisListType.X

P = 128
B, S, D = 4, 512, 128
NT = B * S // P
TB = S // P
S2 = 154
KM_, KR = 128, S2 - 128
H = 16
HG = 4
RR = HG * KR
GH = 3
NG = -(-H // GH)
EPS = 1e-5
LOW = -3.0e38
MASKED = -1.0e30
NOWHERE = 1.0e6
UL2 = 6
PAY = D + 2
CAP0 = 640
CAP3 = 256
BT = 3
BLOCK = BT * P
NFULL = -(-NT * P // BLOCK)
NBLOCKS = (2 * NT * P + 8 * (BLOCK - 1)) // BLOCK

CONST = {}


def constants():
    p = np.arange(P)[:, None]
    f = np.arange(P)[None, :]
    parts = {
        "ident": (p == f) * 1.0,
        "ones": np.ones((P, P)),
        "earlier": (p < f) * 1.0,
        "first": (p == 0) * np.ones((1, P)),
        "head8": (p // 8 == np.arange(16)[None]) * (1 / np.sqrt(8.0)),
        "head64": (p // 64 == np.arange(2)[None]) * 0.125,
        "rest": (p // KR == np.arange(HG)[None]) * 1.0,
        "slot8": np.broadcast_to(float(CAP0) * np.arange(8)[None], (P, 8)),
        "slot16": np.broadcast_to(float(CAP3) * np.arange(16)[None], (P, 16)),
        "rows": p * np.ones((1, 1)),
        "home": np.arange(2)[None].repeat(NT, 1) * NT * P + np.tile(np.arange(NT) * P, 2)[None] + p,
        "full": np.broadcast_to(float(BLOCK) * np.arange(NFULL)[None], (P, NFULL)),
        "block": np.broadcast_to(1.0 * np.arange(NBLOCKS)[None], (P, NBLOCKS)),
        "rank8": np.broadcast_to(8.0 - np.arange(8)[None], (P, 8)),
        "rank16": np.broadcast_to(16.0 - np.arange(16)[None], (P, 16)),
    }
    for i in range(TB):
        q = i * P + p
        parts[f"causal{i}"] = np.where(q >= np.arange(S2)[None] + S - S2, 0.0, MASKED)
    parts["tril"] = np.where(p >= f, 0.0, MASKED)
    parts["triu"] = np.where(f >= p, 0.0, MASKED)
    at, cols = 0, []
    for name, a in parts.items():
        CONST[name] = (at, a.shape[1])
        at += a.shape[1]
        cols.append(a.astype(np.float32))
    return np.ascontiguousarray(np.concatenate(cols, 1))


CONSTS = constants()

ROWS = ["L0_xattn_g2", "L0_xattn_be2", "L0_xattn_b2", "L2_xattn_bv", "L2_xattn_bo", "L3_xattn_bv", "L3_xattn_bo",
        "L3_ffn_v_b", "L3_ffn_o_b"]
COLS = ["L0_xattn_g1", "L0_xattn_be1", "L2_xattn_bq", "L2_xattn_bk", "L3_xattn_bq", "L3_ffn_q_b", "L3_ffn_k_b",
        "L3_ffn_ln1_w", "L3_ffn_ln1_b", "L3_ffn_ln2_w", "L3_ffn_ln2_b"]


class Tally:

    def __init__(self, per, i=0):
        self.per, self.i, self.k = per, i, 0

    def take(self):
        n = self.i * self.per + self.k
        self.k += 1
        return n

    def end(self):
        assert self.k == self.per, (self.k, self.per)


class Own:

    def __init__(self, eng, sem, base=0):
        self.eng, self.sem, self.base, self.i, self.per, self.k = eng, sem, base, 0, 0, 0

    def done(self, ins):
        ins.then_inc(self.sem, 1)
        self.k += 1

    def wait(self):
        self.eng.wait_ge(self.sem, self.i * self.per + (self.base + self.k))

    def loop(self, i, per):
        self.base, self.k, self.i, self.per = self.base + self.k, 0, i, per

    def end(self, count):
        assert self.k == self.per, (self.k, self.per)
        self.base, self.i, self.k, self.per = self.base + count * self.per, 0, 0, 0


class Model:

    def __init__(self):
        self.last_sems, self.now_sems = [], []
        self.cleared, self.sent, self.back, self.got = 0, 0, [0, 0], 0


@contextmanager
def stage(nc, m, name):
    m.now_sems = []

    def sem(s):
        m.now_sems.append(nc.alloc_semaphore(f"{name}_{s}"))
        return m.now_sems[-1]

    yield sem
    for s in m.last_sems:
        nc.release_semaphore(s)
    m.last_sems = m.now_sems


def clear_last(m, sp):
    for s in m.last_sems:
        sp.sem_clear(s)


def ln_stats_vector(nc, dve, own, stats, tmp, src, var_ready, std_ready, std_count=1):
    for t in range(NT):
        own.done(nc.vector.bn_stats(stats[:, t], src[:, t]))
    own.wait()
    mean_e, m2_e, mean_o, m2_o = (stats[:, :, k] for k in (1, 2, 4, 5))
    own.done(nc.vector.tensor_tensor(tmp[:, 2], mean_e, mean_o, ALU.subtract))
    own.done(nc.vector.tensor_tensor(tmp[:, 3], mean_e, mean_o, ALU.add))
    own.done(nc.vector.tensor_tensor(tmp[:, 4], m2_e, m2_o, ALU.add))
    own.wait()
    own.done(nc.vector.tensor_scalar(tmp[:, 0], tmp[:, 3], 0.5, None, ALU.mult))
    own.done(nc.vector.tensor_scalar(tmp[:, 5], tmp[:, 4], 1.0 / D, EPS, ALU.mult, ALU.add))
    own.done(nc.vector.tensor_tensor(tmp[:, 6], tmp[:, 2], tmp[:, 2], ALU.mult))
    own.wait()
    nc.vector.scalar_tensor_tensor(tmp[:, 7], tmp[:, 6], 0.25, tmp[:, 5], ALU.mult, ALU.add).then_inc(var_ready, 1)
    dve.wait_ge(std_ready, std_count)
    own.done(nc.vector.reciprocal(tmp[:, 1], tmp[:, 8]))
    own.wait()


class At:

    def __init__(self, i, r, per):
        self.i, self.r, self.per = i, r, per
        self.k, self.b, self.par = r % per, i + r // per, r % 2

    def __add__(self, k):
        return At(self.i, self.r + k, self.per)

    def static(self):
        return isinstance(self.i, int)

    def exists(self, total):
        return not self.static() or 0 <= self.r < total

    def n(self, each, add):
        return self.i * (self.per * each) + (self.r * each + add)

    def among(self, count):
        return bass.ds(self.b * count, count) if not isinstance(self.b, int) else slice(self.b * count, (self.b + 1) * count)


def attention(nc, m, c):
    nm, dv, tiles, mode = c["name"], c["dv"], c["tiles"], c["mode"]
    W = dv + 1
    n = len(tiles)
    NTL = B * n
    KB = H * dv // P
    OB = 1 if dv == 8 else HG
    OH = H // OB
    NV = -(-KB // 4)
    NK = -(-KB // GH)
    NTT = HG + 1
    NZ = TB if mode == "bias" else 2
    NKM = B if mode == "causal" else 2
    VC = min(512, H * dv)
    COL = dv == 8
    with ExitStack() as ctx:
        sb = lambda s, shape: ctx.enter_context(nc.sbuf_tensor(f"{nm}_{s}", shape, F32))
        ps = lambda s, shape: ctx.enter_context(nc.psum_tensor(f"{nm}_{s}", shape, F32))
        sem = ctx.enter_context(stage(nc, m, nm))
        stats, ln = sb("stats", [P, NT, 6]), sb("ln", [P, 9, NT])
        xn, xnT = sb("xn", [P, 2, D]), sb("xnT", [P, 2, P])
        G = sb("G", [P, B, H, S2])
        Z = sb("Z", [P, NZ, H, S2])
        if mode == "bias":
            room = m.pair[:].rearrange("p a t d -> p (a t d)")[:, 0:H * S2].rearrange("p (h k) -> p h k", k=S2)
            keys_of = [sb("KM", [P, H, S2])[:], room]
        else:
            KM = Z if mode == "mask" else sb("KM", [P, NKM, H, S2])
            keys_of = [KM[:, j] for j in range(NKM)]
        Zr = sb("Zr", [P, 2, HG, RR])
        mask = sb("mask", [P, TB, S2]) if mode == "mask" else None
        mx = sb("mx", [P, 2, H])
        E, Er = sb("E", [P, 2, H, P]), sb("Er", [RR, 2, HG, P])
        KT = E[:].rearrange("p a h q -> p (a h q)")[:, 0:2 * KB * S2].rearrange("p (a j k) -> p a j k", a=2, k=S2)
        V, Vr = sb("V", [P, B, H, W]), sb("Vr", [RR, B, HG, HG * W])
        On, rin, OT = sb("On", [P, H, dv]), sb("rin", [P, H, 1]), sb("OT", [P, KB, P])
        ctr = sb("ctr", [P, B, HG, KR])
        pad = sb("pad", [P, n * NG])
        ys = sb("ys", [P, D]) if mode == "causal" else None
        bqr = sb("bqr", [P, P]) if mode == "causal" else None
        if mode == "mask":
            maski = ctx.enter_context(nc.sbuf_tensor(f"{nm}_maski", [P, TB, S2], I32))
        psS, psT, psO = ps("psS", [P, 2, 512]), ps("psT", [P, 2, 512]), ps("psO", [P, 2, 512])
        psM, psY = ps("psM", [P, 512]), ps("psY", [P, 512])
        own_v = sem("own_v")
        var_ready, std_ready = sem("var_ready"), sem("std_ready")
        loaded, bias_in = sem("loaded"), [sem(f"bias_in{i}") for i in range(TB if mode == "bias" else 0)]
        ctr_ready, kv_full, kv_free = sem("ctr_ready"), sem("kv_full"), sem("kv_free")
        r_full, r_free, g_full, g_free, km_ready = sem("r_full"), sem("r_free"), sem("g_full"), sem("g_free"), sem("km_ready")
        xn_ready, x_full, x_done = sem("xn_ready"), sem("x_full"), sem("x_done")
        if COL:
            VF = H * W + 32 - W
            VG, VrG, OG = sb("VG", [P, 2, VF]), sb("VrG", [RR, 2, VF]), (
                sb("OG", [P, HG * P]) if mode == "bias" else m.XT)
            waited = sb("waited", [P, n])
            vg_ready, og_done, tb_full = sem("vg_ready"), sem("og_done"), sem("tb_full")
        s_full, s_free, t_full, t_free = sem("s_full"), sem("s_free"), sem("t_full"), sem("t_free")
        o_full, o_free, m_full, m_free = sem("o_full"), sem("o_free"), sem("m_full"), sem("m_free")
        y_full, y_free, z_ready = sem("y_full"), sem("y_free"), sem("z_ready")
        yr_full, yr_free = (sem("yr_full"), sem("yr_free")) if mode == "causal" else (None, None)
        block = ctx.enter_context(nc.Block())
        kv_bank = [psS[:, 0], psS[:, 1], psO[:, 0], psO[:, 1]]
        r_bank = [psM[:], psY[:]]

        def over_steps(eng, step, around=lambda i: None):
            for t in range(-2, n):
                step(At(0, t, n))
            with eng.Fori(0, B - 2) as i:
                around(i)
                for k in range(n, 2 * n):
                    step(At(i, k, n))
            around(None)
            for t in range(NTL - n, NTL + 2):
                step(At(0, t, n))

        @block.sync
        def _(sp):
            clear_last(m, sp)
            if mode == "mask":
                sp.dma_start(maski[:], m.mask.rearrange("(i p) k -> p i k", p=P)).then_inc(loaded, 16)
            if mode == "bias":
                for i in range(TB):
                    sp.dma_start(Z[:, i], m.bias[0, :, i * P:(i + 1) * P].rearrange("h p k -> p h k")).then_inc(bias_in[i], 16)
                with sp.Fori(0, B - 1) as b:
                    for i in range(TB):
                        sp.wait_ge(t_full, At(b, i, TB).n(NTT, NTT * (NZ + 1)))
                        sp.dma_start(Z[:, i], m.bias[bass.ds(b + 1, 1), :, i * P:(i + 1) * P].rearrange(
                            "o h p k -> p (o h) k")).then_inc(bias_in[i], 16)

        @block.scalar
        def _(act):
            kv, gt = Tally(0), Tally(0)

            def keys(b):
                for j in range(0, KB, GH):
                    w = min(GH, KB - j)
                    u = kv.take()
                    act.wait_ge(kv_full, u + 1)
                    if j == 0 and b >= 2:
                        act.wait_ge(km_ready, b - 1)
                    if mode == "causal":
                        last = nc.scalar.activation(KT[:, b % 2, 0], kv_bank[u % 4][:, 0:S2], ACT.Identity, bias=m.col("L2_xattn_bk"))
                    else:
                        last = nc.scalar.copy(KT[:, b % 2, j:j + w], kv_bank[u % 4][:, 0:w * S2].rearrange("p (j k) -> p j k", k=S2))
                    last.then_inc(kv_free, 1)

            keys(0)
            keys(1)
            act.wait_ge(var_ready, 1)
            nc.scalar.activation(ln[:, 8], ln[:, 7], ACT.Sqrt).then_inc(std_ready, 1)
            for b in range(B):
                for j in range(NV):
                    u = kv.take()
                    hh = VC // dv
                    act.wait_ge(kv_full, u + 1)
                    nc.scalar.copy(V[:, b, hh * j:hh * (j + 1), 0:dv],
                                   kv_bank[u % 4][:, 0:VC].rearrange("p (h d) -> p h d", d=dv)).then_inc(kv_free, 1)
                for g in range(NG):
                    w = min(GH, H - GH * g)
                    act.wait_ge(g_full, gt.take() + 1)
                    nc.scalar.copy(G[:, b, GH * g:GH * g + w],
                                   psT[:, g % 2, 0:w * S2].rearrange("p (h k) -> p h k", k=S2)).then_inc(g_free, 1)
                if b + 2 < B:
                    keys(b + 2)

            def step(t):
                u, x = t + -2, t + 2

                def turned_outputs():
                    for j in range(NV):
                        w = min(4, KB)
                        act.wait_ge(m_full, u.n(NV, NV + j + 1))
                        if j == 0:
                            act.wait_ge(y_full, u.n(1, 1))
                        nc.scalar.copy(OT[:, 4 * j:4 * j + w], psM[:, 0:w * P].rearrange("p (j q) -> p j q", q=P)
                                       ).then_inc(m_free, 1)

                def exponentials(g):
                    if g == 0:
                        act.wait_ge(o_full, t.n(OB, OB))
                    act.wait_ge(t_full, t.n(NTT, NTT * NZ + g + 1))
                    bank = (t.r * NTT + g) % 2
                    rows, dst = (P, E[:, t.par, HG * g:HG * g + HG]) if g < HG else (RR, Er[:, t.par])
                    nc.scalar.activation(dst, psT[0:rows, bank].rearrange("p (h q) -> p h q", q=P), ACT.Exp).then_inc(t_free, 1)

                if u.exists(NTL) and not COL:
                    turned_outputs()
                for g in range(NTT):
                    if g == HG and COL:
                        o = t + -1
                        if o.exists(NTL):
                            act.wait_ge(o_full, o.n(1, 3))
                            act.wait_ge(tb_full, o.n(1, 1))
                            nc.scalar.copy(OG[:, 0:HG * P], psO[:, o.par]).then_inc(og_done, 1)
                        if u.exists(NTL):
                            turned_outputs()
                    if t.exists(NTL):
                        exponentials(g)
                    if x.exists(NTL) and g == (HG if COL else HG - 1):
                        act.wait_ge(x_full, x.n(1, 3))
                        act.wait_ge(s_full, x.n(NG, NG))
                        nc.scalar.copy(xnT[:, x.par], psM[:, 0:P]).then_inc(x_done, 1)

            over_steps(act, step)

        @block.gpsimd
        def _(pool):
            for key in c["clear"]:
                pool.wait_ge(m.empty_ready, 3)
                table = m.slots[key]
                r = table.shape[0] // P
                pool.dma_start(table.rearrange("(p r) d -> p r d", p=P), m.empty[:].broadcast_to([P, r, PAY])).then_inc(m.zeroed, 16)
                m.cleared += 1
                for k, done in enumerate(m.returned):
                    half = m.results[key][k * NT * P:(k + 1) * NT * P].rearrange("(p r) d -> p r d", p=P)
                    pool.dma_start(half, m.empty[:, :, 0:D].broadcast_to([P, NT, D])).then_inc(done, 16)
                    m.back[k] += 1
            if COL:
                nc.gpsimd.memset(VG[:, :, H * W:VF], 0.0)
                nc.gpsimd.memset(VrG[:, :, H * W:VF], 0.0)
            with pool.Fori(0, B) as b:
                for k in range(n):
                    t = At(b, k, n)
                    pool.wait_ge(t_full, t.n(NTT, NTT * (NZ - 1)))
                    for g in range(HG):
                        need = -(-(HG * g + HG) // GH)
                        pool.wait_ge(s_free, t.n(NG, need + 2))
                        h = slice(HG * g, HG * g + HG)
                        zz = Z[:, k % NZ, h, 0:KM_]
                        nc.gpsimd.tensor_tensor(zz, zz, mx[:, k % 2, h].unsqueeze(2).broadcast_to([P, HG, KM_]),
                                                ALU.subtract).then_inc(z_ready, 1)
                        nc.gpsimd.tensor_tensor(Zr[:, k % 2, g].rearrange("p (h k) -> p h k", k=KR), Z[:, k % NZ, h, KM_:S2],
                                                mx[:, k % 2, h].unsqueeze(2).broadcast_to([P, HG, KR]),
                                                ALU.subtract).then_inc(z_ready, 1)
                    if COL:
                        pool.wait_ge(o_full, t.n(1, 1))
                        if k == 0:
                            pool.wait_ge(g_free, B * NG + 2)
                        nc.gpsimd.tensor_tensor(waited[:, k:k + 1], m.ones[:, 0:1], m.ones[:, 0:1], ALU.mult)
                        nc.gpsimd.tensor_copy(VG[:, k % 2, 0:H * W], V[:, bass.ds(b, 1)].rearrange("p o h d -> p (o h d)")
                                              ).then_inc(vg_ready, 1)
                        nc.gpsimd.tensor_copy(VrG[:, k % 2, 0:H * W], Vr[:, bass.ds(b, 1)].rearrange("p o g d -> p (o g d)")
                                              ).then_inc(vg_ready, 1)

        @block.tensor
        def _(pe):
            pe.sem_inc(kv_free, 4)
            pe.sem_inc(r_free, 2)
            pe.sem_inc(g_free, 2)
            pe.sem_inc(s_free, 2)
            pe.sem_inc(s_full, 2 * NG)
            pe.sem_inc(t_free, 2)
            pe.sem_inc(t_full, NZ * NTT)
            pe.sem_inc(z_ready, 4 * HG)
            pe.sem_inc(o_free, 2)
            pe.sem_inc(o_full, 2 * OB)
            pe.sem_inc(m_free, 4 * NV)
            pe.sem_inc(m_full, NV)
            pe.sem_inc(x_full, 2)
            pe.sem_inc(y_free, 4)
            pe.sem_inc(y_full, 1)
            if COL:
                pe.sem_inc(tb_full, 1)
            kv, rt, gt = Tally(0), Tally(0), Tally(0)

            def keys(b):
                for j in range(0, KB, GH):
                    w = min(GH, KB - j)
                    u = kv.take()
                    pe.wait_ge(kv_free, u + 1)
                    for jj in range(w):
                        last = pe.matmul(kv_bank[u % 4][:, jj * S2:(jj + 1) * S2], c["wk"][:, (j + jj) * P:(j + jj + 1) * P],
                                         m.ctxT[:, b], start=(jj == 0), stop=(jj == w - 1), skip_group_check=True)
                    last.then_inc(kv_full, 1)

            keys(0)
            keys(1)
            pe.wait_ge(ctr_ready, 1)
            for b in range(B):
                for j in range(NV):
                    u = kv.take()
                    pe.wait_ge(kv_free, u + 1)
                    last = pe.matmul(kv_bank[u % 4][:, 0:VC], m.ctxT[:, b, 0:KM_], c["wv"][:, j * VC:(j + 1) * VC], start=True,
                                     stop=mode != "causal")
                    if mode == "causal":
                        last = pe.matmul(kv_bank[u % 4][:, 0:VC], m.ones[0:1, :], m.row("L2_xattn_bv"), start=False, stop=True)
                    last.then_inc(kv_full, 1)
                for j in range(NV):
                    u = rt.take()
                    pe.wait_ge(r_free, u + 1)
                    last = pe.matmul(r_bank[u % 2][0:RR, 0:VC], ctr[:, b].rearrange("p h k -> p (h k)"),
                                     c["wv"][:, j * VC:(j + 1) * VC], start=True, stop=mode != "causal")
                    if mode == "causal":
                        last = pe.matmul(r_bank[u % 2][0:RR, 0:VC], m.ones[0:1, 0:RR], m.row("L2_xattn_bv"), start=False, stop=True)
                    last.then_inc(r_full, 1)
                pe.wait_ge(km_ready, b + 1)
                for g in range(NG):
                    w = min(GH, H - GH * g)
                    pe.wait_ge(g_free, gt.take() + 1)
                    for hh in range(w) if KB > 1 else range(1):
                        h = GH * g + hh
                        if KB > 1:
                            last = pe.matmul(psT[:, g % 2, hh * S2:(hh + 1) * S2], c["wq"][:, h // 2], keys_of[b % NKM][:, h],
                                             start=(hh == 0), stop=(hh == w - 1), skip_group_check=True)
                        else:
                            last = pe.matmul(psT[:, g % 2, 0:w * S2], c["wq"],
                                             keys_of[b % NKM][:, h:h + w].rearrange("p h k -> p (h k)"), start=True, stop=True)
                    last.then_inc(g_full, 1)
                if b + 2 < B:
                    keys(b + 2)
            pe.wait_ge(g_free, B * NG + 2)
            pe.wait_ge(kv_free, kv.k + 4)
            pe.wait_ge(r_free, rt.k + 2)

            def scores(t, g):
                w = min(GH, H - GH * g)
                hs = slice(GH * g, GH * g + w)
                if g == 0:
                    pe.wait_ge(x_done, t.n(1, 1))
                pe.wait_ge(s_free, t.n(NG, g + 1))
                last = pe.matmul(psS[:, g % 2, 0:w * S2], xnT[:, t.par],
                                 G[:, t.among(1), hs].rearrange("p o h k -> p (o h k)"), start=True, stop=mode != "causal")
                if mode == "causal":
                    last = pe.matmul(psS[:, g % 2, 0:w * S2], bqr[:],
                                     KM[:, t.among(1), hs].rearrange("p o h k -> p (o h k)"), start=False, stop=True)
                last.then_inc(s_full, 1)

            def turn_x(t):
                pe.wait_ge(xn_ready, t.n(1, 1))
                pe.wait_ge(m_free, t.n(NV, NV))
                pe.wait_ge(x_done, t.n(1, 0)) if not t.static() or t.r >= 1 else None
                pe.transpose(psM[:, 0:P], xn[:, t.par], m.ident).then_inc(x_full, 1)

            def turn_outputs(t, js=range(NV)):
                if js[0] == 0:
                    pe.wait_ge(o_free, t.n(OB, OB + 2))
                    pe.wait_ge(x_done, t.n(1, 4) if not t.static() else min(t.r + 4, NTL))
                for j in js:
                    pe.wait_ge(m_free, t.n(NV, 4 * NV + j))
                    for jj in range(min(4, KB)):
                        x = On[:].rearrange("p h d -> p (h d)")[:, (4 * j + jj) * P:(4 * j + jj + 1) * P]
                        last = pe.transpose(psM[:, jj * P:(jj + 1) * P], x, m.ident)
                    last.then_inc(m_full, 1)

            def project(t):
                pe.wait_ge(m_free, t.n(NV, 5 * NV))
                pe.wait_ge(y_free, t.n(1, 4))
                if mode == "causal" and t.k == 0 and (not t.static() or t.b > 0):
                    pe.wait_ge(yr_free, t.b)
                for j in range(KB):
                    last = pe.matmul(psY[:, 0:D], OT[:, j], c["wo"][:, j], start=(j == 0),
                                     stop=(j == KB - 1 and mode != "causal"))
                if mode == "causal":
                    last = pe.matmul(psY[:, 0:D], m.ones[0:1, :], m.row("L2_xattn_bo"), start=False, stop=True)
                last.then_inc(y_full, 1)
                if mode == "causal" and t.k == n - 1:
                    pe.wait_ge(y_free, t.n(1, 5))
                    pe.matmul(psY[:, 0:D], m.first, ys[:], start=True, stop=True).then_inc(yr_full, 1)

            def turn_scores(t, g):
                pe.wait_ge(z_ready, t.n(2 * HG, 4 * HG + 2 * min(g + 1, HG)))
                pe.wait_ge(t_free, t.n(NTT, g + 1))
                bank = (t.r * NTT + g) % 2
                for j in range(HG):
                    if g < HG:
                        last = pe.transpose(psT[:, bank, j * P:(j + 1) * P], Z[:, t.r % NZ, HG * g + j, 0:KM_], m.ident)
                    else:
                        last = pe.transpose(psT[0:RR, bank, j * P:(j + 1) * P], Zr[:, t.par, j], m.ident)
                last.then_inc(t_full, 1)

            def values(t, g):
                if g == 0:
                    pe.wait_ge(t_free, t.n(NTT, NTT + 2))
                o, h0 = (0, HG * g) if OB == 1 else (g, 0)
                if h0 == 0:
                    pe.wait_ge(o_free, t.n(OB, o + 1))
                if COL:
                    if g == 0:
                        pe.wait_ge(vg_ready, t.n(2, 2))
                    for v, e in ((VG, lambda h: E[:, t.par, h]), (VrG, lambda h: Er[:, t.par, g])):
                        for j in range(HG):
                            h = HG * g + j
                            last = pe.matmul(psO[32 * j:32 * j + 32, t.par, g * P:(g + 1) * P], v[:, t.par, h * W:h * W + 32], e(h),
                                             start=(g == 0 and v is VG), stop=(g == HG - 1 and v is VrG), skip_group_check=True)
                    if g == HG - 1:
                        last.then_inc(o_full, 1)
                    return
                bank = (t.r * OB + o) % 2
                out = psO[:, bank, 0:OH * W].rearrange("p (h d) -> p h d", d=W)
                for j in range(HG):
                    pe.matmul(out[:, h0 + j], E[:, t.par, HG * g + j], V[:, t.among(1), HG * g + j].rearrange("p o d -> p (o d)"),
                              start=(h0 + j == 0), stop=False, skip_group_check=True)
                last = pe.matmul(psO[:, bank, h0 * W:(h0 + HG) * W], Er[:, t.par, g],
                                 Vr[:, t.among(1), g].rearrange("p o d -> p (o d)"),
                                 start=False, stop=(h0 + HG == OH), skip_group_check=True)
                if h0 + HG == OH:
                    last.then_inc(o_full, 1)

            def turn_back(t):
                pe.wait_ge(og_done, t.n(1, 1))
                for g in range(HG):
                    last = pe.transpose(psO[:, t.par, g * P:(g + 1) * P], OG[:, g * P:(g + 1) * P], m.ident)
                last.then_inc(tb_full, 1)

            def step(t):
                u = t + -2
                for g in range(NG):
                    if g == 0 and not COL and u.exists(NTL):
                        turn_outputs(u, [0])
                    if (t + 1).exists(NTL):
                        scores(t + 1, g)
                    if g == 0 and not COL and u.exists(NTL):
                        turn_outputs(u, [1])
                    if g < NTT and t.exists(NTL):
                        turn_scores(t, g)
                    if g < HG and (t + -1).exists(NTL):
                        values(t + -1, g)
                    if u.exists(NTL):
                        if COL and g == 1:
                            turn_back(u)
                        if COL and g == 3:
                            turn_outputs(u)
                        if g == (5 if COL else 1):
                            project(u)
                    if g == (NG - 1 if COL else 3) and (t + 2).exists(NTL):
                        turn_x(t + 2)

            over_steps(pe, step)

        @block.vector
        def _(dve):
            own = Own(dve, own_v)
            nc.vector.tensor_copy(ctr[:].rearrange("p b h k -> p h b k"),
                                  m.ctxT[:, :, KM_:S2].unsqueeze(1).broadcast_to([P, HG, B, KR])).then_inc(ctr_ready, 1)
            if mode == "mask":
                dve.wait_ge(loaded, 16)
                own.done(nc.vector.tensor_copy(mask[:], maski[:]))
                own.wait()
                own.done(nc.vector.tensor_scalar(mask[:], mask[:], 0.0, MASKED, ALU.is_equal, ALU.mult))
            if mode == "causal":
                own.done(nc.vector.tensor_copy(bqr[:], m.col("L2_xattn_bq").broadcast_to([P, P])))
            own.done(nc.vector.memset(V[:, :, :, dv:W], 1.0))

            def masked_keys(b):
                dve.wait_ge(kv_free, 4 + NK * (b + 1) + (NV * (b - 1) if b >= 2 else 0))
                if b >= NKM:
                    dve.wait_ge(g_full, NG * (b - NKM + 1))
                if KB == 1:
                    nc.vector.tensor_tensor(keys_of[b % NKM], KT[:, b % 2].broadcast_to([P, H, S2]),
                                            m.head8.unsqueeze(2).broadcast_to([P, H, S2]), ALU.mult).then_inc(km_ready, 1)
                else:
                    kmv = keys_of[b % NKM].rearrange("p (j a) k -> p j a k", a=2)
                    nc.vector.tensor_scalar(kmv[:, :, 0], KT[:, b % 2], m.head64[:, 0:1], None, ALU.mult)
                    nc.vector.tensor_scalar(kmv[:, :, 1], KT[:, b % 2], m.head64[:, 1:2], None, ALU.mult).then_inc(km_ready, 1)

            masked_keys(0)
            ln_stats_vector(nc, dve, own, stats, ln, m.X, var_ready, std_ready)
            for b in range(B):
                for j in range(NV):
                    u = b * NV + j
                    dve.wait_ge(r_full, u + 1)
                    gs = HG // NV
                    vv = Vr[:, b, j * gs:(j + 1) * gs].rearrange("p g (h d) -> p (g h) d", d=W)[:, :, 0:dv]
                    src = r_bank[u % 2][0:RR, 0:gs * HG * dv].rearrange("p (h d) -> p h d", d=dv)
                    for g in range(gs):
                        last = nc.vector.tensor_tensor(
                            vv[:, g * HG:(g + 1) * HG], src[:, g * HG:(g + 1) * HG],
                            m.rest[0:RR].unsqueeze(2).broadcast_to([RR, HG, dv]), ALU.mult)
                    if j == NV - 1:
                        own.done(nc.vector.tensor_copy(Vr[:, b].rearrange("p g (h d) -> p g h d", d=W)[:, :, :, dv],
                                                       m.rest[0:RR].unsqueeze(1).broadcast_to([RR, HG, HG])))
                        own.wait()
                    last = nc.vector.memset(pad[:, 0:1], 0.0) if j == NV - 1 else last
                    last.then_inc(r_free, 1)
                if b + 1 < B:
                    masked_keys(b + 1)

            def normalise(t):
                at = t.b * TB + tiles[t.k]
                at = slice(at, at + 1) if t.static() else bass.ds(at, 1)
                src, mean, r = m.X[:, at].rearrange("p o d -> p (o d)"), ln[:, 0, at], ln[:, 1, at]
                if mode == "bias":
                    nc.vector.tensor_scalar(m.XN[:, at].rearrange("p o d -> p (o d)"), src, mean, r, ALU.subtract, ALU.mult)
                dve.wait_ge(x_full, t.n(1, 1))
                nc.vector.tensor_scalar(xn[:, t.par], src, mean, r, ALU.subtract, ALU.mult).then_inc(xn_ready, 1)

            def maxima(t, g):
                w = min(GH, H - GH * g)
                if g == 0:
                    if mode == "bias":
                        dve.wait_ge(bias_in[t.k], t.b * 16 + 16)
                    dve.wait_ge(t_full, t.n(NTT, NTT))
                    dve.wait_ge(z_ready, t.n(2 * HG, 2 * HG))
                dve.wait_ge(s_full, t.n(NG, 2 * NG + g + 1))
                nc.vector.memset(pad[:, t.k * NG + g:t.k * NG + g + 1], 0.0)
                for hh in range(w):
                    h = GH * g + hh
                    add = Z[:, t.k, h] if mode == "bias" else mask[:, t.k] if mode == "mask" else m.causal[tiles[t.k]]
                    last = nc.vector.tensor_tensor_reduce(
                        Z[:, t.r % NZ, h], psS[:, g % 2, hh * S2:(hh + 1) * S2], add, 1.0, LOW, ALU.add, ALU.max,
                        mx[:, t.par, h:h + 1])
                last.then_inc(s_free, 1)

            def residual(t):
                at = t.b * TB + tiles[t.k]
                at = slice(at, at + 1) if t.static() else bass.ds(at, 1)
                x = m.X[:, at, :].rearrange("p o d -> p (o d)")
                dve.wait_ge(y_full, t.n(1, 2))
                if mode == "causal" and t.k == 0:
                    own.done(nc.vector.tensor_copy(ys[:], psY[:, 0:D]))
                    own.wait()
                if mode == "bias":
                    x1 = m.X1[:, at, :].rearrange("p o d -> p (o d)")
                    dve.wait_ge(xn_ready, t.n(1, 1))
                    nc.vector.tensor_tensor(x1, psY[:, 0:D], m.XN[:, at].rearrange("p o d -> p (o d)"), ALU.add
                                            ).then_inc(y_free, 1)
                else:
                    nc.vector.scalar_tensor_tensor(x, psY[:, 0:D], m.gate(c["gate"]), x, ALU.mult, ALU.add
                                                   ).then_inc(y_free, 1)
                if mode == "causal" and t.k == n - 1:
                    dve.wait_ge(yr_full, t.b + 1)
                    for i in range(2):
                        at = t.b * TB + i
                        at = slice(at, at + 1) if t.static() else bass.ds(at, 1)
                        x = m.X[:, at, :].rearrange("p o d -> p (o d)")
                        last = nc.vector.scalar_tensor_tensor(x, psY[:, 0:D], m.gate(c["gate"]), x, ALU.mult, ALU.add)
                    last.then_inc(yr_free, 1)

            def divide(t, o):
                if o == 0:
                    dve.wait_ge(m_full, t.n(NV, NV))
                bank = (t.r * OB + o) % 2
                if COL:
                    dve.wait_ge(tb_full, t.n(1, 2))
                    out = psO[:, bank].rearrange("p (h d) -> p h d", d=32)
                else:
                    dve.wait_ge(o_full, t.n(OB, 2 * OB + o + 1))
                    out = psO[:, bank, 0:OH * W].rearrange("p (h d) -> p h d", d=W)
                hs = slice(o * OH, (o + 1) * OH)
                own.done(nc.vector.reciprocal(rin[:, hs], out[:, :, dv:W]))
                own.wait()
                nc.vector.tensor_tensor(On[:, hs], out[:, :, 0:dv], rin[:, hs].broadcast_to([P, OH, dv]), ALU.mult
                                        ).then_inc(o_free, 1)

            def step(t):
                u, o = t + -2, t + -1
                for g in range(NG):
                    if (t + 1).exists(NTL):
                        maxima(t + 1, g)
                    if COL and g == 1 and u.exists(NTL):
                        divide(u, 0)
                    if not COL and 1 <= g <= OB and o.exists(NTL):
                        divide(o, g - 1)
                    if g == 2 and (t + 2).exists(NTL):
                        normalise(t + 2)
                    if not COL and g == 3 and u.exists(NTL):
                        residual(u)
                if COL and u.exists(NTL):
                    residual(u)

            def around(i):
                if i is not None:
                    own.loop(i, n * OB + (mode == "causal"))
                else:
                    own.end(B - 2)

            over_steps(dve, step, around)


def norm_transpose(nc, m, name, src, dst, w=None, b=None, router=None, turn=True):
    with ExitStack() as ctx:
        sb = lambda s, shape: ctx.enter_context(nc.sbuf_tensor(f"{name}_{s}", shape, F32))
        ps = lambda s, shape: ctx.enter_context(nc.psum_tensor(f"{name}_{s}", shape, F32))
        sem = ctx.enter_context(stage(nc, m, name))
        stats, ln = sb("stats", [P, NT, 6]), sb("ln", [P, 9, NT])
        psT = ps("psT", [P, NT // TB, 512])
        own_v, var_ready, std_ready = sem("own_v"), sem("var_ready"), sem("std_ready")
        x_ready, t_full, xt_ready = sem("x_ready"), sem("t_full"), sem("xt_ready")
        if router:
            r = Router(nc, sb, ps, sem, m, router)
        block = ctx.enter_context(nc.Block())

        @block.sync
        def _(sp):
            clear_last(m, sp)
            if name == "L0n1":
                sp.wait_ge(m.rest_loaded, 16 * (len(KEPT) - NFIRST))

        @block.scalar
        def _(act):
            act.wait_ge(var_ready, 1)
            nc.scalar.activation(ln[:, 8], ln[:, 7], ACT.Sqrt).then_inc(std_ready, 1)
            for c in range(NT // TB if turn else 0):
                act.wait_ge(t_full, c + 1)
                dst_t = m.XT[:, c * 512:(c + 1) * 512]
                if w is None:
                    nc.scalar.copy(dst_t, psT[:, c]).then_inc(xt_ready, 1)
                else:
                    nc.scalar.activation(dst_t, psT[:, c], ACT.Identity, bias=b, scale=w).then_inc(xt_ready, 1)
            if router:
                r.scalar(act)

        @block.tensor
        def _(pe):
            for t in range(NT if turn else 0):
                pe.wait_ge(x_ready, t + 1)
                last = pe.transpose(psT[:, t // TB, (t % TB) * P:(t % TB + 1) * P], dst[:, t], m.ident)
                if t % TB == TB - 1:
                    last.then_inc(t_full, 1)
            if router:
                r.tensor(pe, xt_ready)

        @block.vector
        def _(dve):
            own = Own(dve, own_v)
            ln_stats_vector(nc, dve, own, stats, ln, src, var_ready, std_ready)
            for t in range(NT):
                nc.vector.tensor_scalar(dst[:, t], src[:, t], ln[:, 0, t:t + 1], ln[:, 1, t:t + 1], ALU.subtract, ALU.mult
                                        ).then_inc(x_ready, 1)
            if router:
                r.vector(dve, own)


class Router:

    def __init__(self, nc, sb, ps, sem, m, c):
        self.nc, self.m, self.c = nc, m, c
        E = c["E"]
        self.psL = ps("psL", [P, NT, E])
        self.psC = ps("psC", [P, 2, 512])
        self.L, self.eq, self.rank = sb("logits", [P, NT, E]), sb("eq", [P, NT, E]), sb("rank", [P, NT, E])
        self.hot = sb("hot", [P, 2, NT, E])
        self.v = sb("rv", [P, 12, NT])
        self.pos, self.run = sb("pos", [P, 2, NT, E]), sb("run", [P, 2, NT, E])
        if c["kind"] == "L2":
            self.total, self.w, self.be = sb("total", [P, E]), sb("fills", [P, NBLOCKS, E]), sb("blocks", [P, 3, NBLOCKS])
        self.l_ready, self.diff_ready, self.exp_ready = sem("l_ready"), sem("diff_ready"), sem("exp_ready")
        self.hot_ready, self.c_ready = sem("hot_ready"), sem("c_ready")

    def tensor(self, pe, xt_ready):
        c, m = self.c, self.m
        for t in range(NT):
            pe.wait_ge(xt_ready, t // TB + 1)
            last = pe.matmul(self.psL[:, t], m.XT[:, t * P:(t + 1) * P], c["w"], start=(t == 0), stop=(t == NT - 1),
                             skip_group_check=True)
        last.then_inc(self.l_ready, 1)
        if c["kind"] != "L1":
            pe.wait_ge(self.hot_ready, 1)
            n = NT * c["E"]
            for k in range(2 if c["kind"] == "L3" else 1):
                hot = self.hot[:, k].rearrange("p t e -> p (t e)")
                pe.matmul(self.psC[:, k, 0:n], m.const["earlier"], hot, start=True, stop=True, skip_group_check=True)
                last = pe.matmul(self.psC[:, k, 256:256 + n], m.ones, hot, start=False, stop=True, skip_group_check=True)
            last.then_inc(self.c_ready, 1)

    def scalar(self, act):
        nc, v = self.nc, self.v
        act.wait_ge(self.diff_ready, 1)
        last = nc.scalar.activation(v[:, 3], v[:, 2], ACT.Exp)
        if self.c["kind"] == "L3":
            last = nc.scalar.activation(self.rank[:], self.eq[:], ACT.Exp)
        last.then_inc(self.exp_ready, 1)

    def vector(self, dve, own):
        nc, c, v, m = self.nc, self.c, self.v, self.m
        E, kind, L, eq, rank, hot = c["E"], c["kind"], self.L, self.eq, self.rank, self.hot
        wide = lambda a: a.unsqueeze(2).broadcast_to([P, NT, E])
        order = m.const["rank%d" % E].unsqueeze(1).broadcast_to([P, NT, E])

        def step(ins):
            own.done(ins)
            own.wait()

        dve.wait_ge(self.l_ready, 1)
        if kind == "L0":
            step(nc.vector.tensor_scalar(L[:], self.psL[:], -1e4, 1e4, ALU.max, ALU.min))
        elif kind == "L1":
            step(nc.vector.tensor_tensor(L[:], self.psL[:], m.router_bias[:].unsqueeze(1).broadcast_to([P, NT, E]), ALU.add))
        else:
            step(nc.vector.tensor_copy(L[:], self.psL[:]))
        for k in range(2):
            step(nc.vector.tensor_reduce(v[:, k], L[:], AX_X, ALU.max))
            step(nc.vector.tensor_tensor(eq[:], L[:], wide(v[:, k]), ALU.is_equal))
            step(nc.vector.tensor_tensor(rank[:], eq[:], order, ALU.mult))
            step(nc.vector.tensor_reduce(v[:, 4], rank[:], AX_X, ALU.max))
            step(nc.vector.tensor_tensor(hot[:, k], rank[:], wide(v[:, 4]), ALU.is_equal))
            if k == 0:
                if kind == "L3":
                    step(nc.vector.tensor_tensor(self.run[:, 1], L[:], wide(v[:, 0]), ALU.subtract))
                step(nc.vector.scalar_tensor_tensor(L[:], hot[:, 0], LOW, L[:], ALU.mult, ALU.add))
        if kind in ("L0", "L2"):
            own.done(nc.vector.tensor_tensor(self.pos[:, 1], hot[:, 0], hot[:, 1], ALU.add))
            own.wait()
            own.done(nc.vector.tensor_copy(self.run[:, 1], hot[:, 0]))
            own.wait()
            nc.vector.tensor_copy(hot[:, 0], self.pos[:, 1]).then_inc(self.hot_ready, 1)
        elif kind == "L3":
            own.done(nc.vector.tensor_copy(eq[:], self.run[:, 1]))
            own.wait()
            dve.wait_ge(own.sem, own.base + own.k)
            nc.vector.memset(v[:, 11], 0.0).then_inc(self.hot_ready, 1)
        own.done(nc.vector.tensor_tensor(v[:, 2], v[:, 1], v[:, 0], ALU.subtract))
        own.wait()
        nc.vector.memset(v[:, 10], 0.0).then_inc(self.diff_ready, 1)
        dve.wait_ge(self.exp_ready, 1)
        if kind != "L3":
            step(nc.vector.tensor_scalar(v[:, 5], v[:, 3], 1.0, 1e-12 if kind == "L0" else 0.0, ALU.add, ALU.add))
            step(nc.vector.reciprocal(v[:, 6], v[:, 5]))
            step(nc.vector.tensor_tensor(v[:, 7], v[:, 3], v[:, 6], ALU.mult))
        if kind != "L1":
            self.positions(dve, own, step)
        if kind == "L2":
            self.blocks(step)
        if kind != "L1":
            cap = {"L0": CAP0, "L2": NT * P, "L3": CAP3}[kind]
            first = v[:, 11, 0:E] if kind == "L2" else m.const["slot%d" % E]
            if kind == "L3":
                step(nc.vector.tensor_reduce(v[:, 5], rank[:], AX_X, ALU.add))
                step(nc.vector.reciprocal(v[:, 6], v[:, 5]))
                step(nc.vector.tensor_tensor(v[:, 7], v[:, 3], v[:, 6], ALU.mult))
            for k in range(2):
                pos = self.pos[:, k if kind == "L3" else 0]
                chosen = self.run[:, 1] if kind != "L3" and k == 0 else hot[:, k]
                step(nc.vector.tensor_scalar(rank[:], pos, float(cap), NOWHERE, ALU.is_ge, ALU.mult))
                step(nc.vector.tensor_tensor(rank[:], rank[:], pos, ALU.add))
                step(nc.vector.tensor_tensor(rank[:], rank[:], first.unsqueeze(1).broadcast_to([P, NT, E]), ALU.add))
                step(nc.vector.tensor_tensor(rank[:], rank[:], chosen, ALU.mult))
                step(nc.vector.tensor_reduce(v[:, 8], rank[:], AX_X, ALU.add))
                step(nc.vector.tensor_copy(m.slot_to[:, k], v[:, 8]))
                step(nc.vector.tensor_scalar(v[:, 9], v[:, 8], NOWHERE, None, ALU.is_lt))
                step(nc.vector.tensor_tensor(v[:, 6 + k], v[:, 6 + k], v[:, 9], ALU.mult))
            if kind == "L3":
                step(nc.vector.tensor_tensor(v[:, 8], v[:, 6], v[:, 7], ALU.add))
                step(nc.vector.tensor_scalar(v[:, 8], v[:, 8], float(np.finfo(np.float32).eps), None, ALU.max))
                step(nc.vector.reciprocal(v[:, 9], v[:, 8]))
                for k in range(2):
                    step(nc.vector.tensor_tensor(v[:, 6 + k], v[:, 6 + k], v[:, 9], ALU.mult))
                step(nc.vector.tensor_scalar(v[:, 6:8], v[:, 6:8], 1.0 - 0.2, None, ALU.mult))
            step(nc.vector.tensor_scalar(m.slot_share[:], v[:, 6:8], m.gate(c["gate"]), None, ALU.mult))
            return
        step(nc.vector.tensor_tensor(eq[:], hot[:, 0], wide(v[:, 6]), ALU.mult))
        step(nc.vector.tensor_tensor(rank[:], hot[:, 1], wide(v[:, 7]), ALU.mult))
        step(nc.vector.tensor_tensor(eq[:], eq[:], rank[:], ALU.add))
        step(nc.vector.tensor_scalar(c["comb"], eq[:], m.gate(c["gate"]), None, ALU.mult))

    def blocks(self, step):
        nc, m, v, E = self.nc, self.m, self.v, self.c["E"]
        used, end, w = v[:, 8, 0:E], v[:, 9, 0:E], self.w
        step(nc.vector.tensor_tensor(w[:, 0:E, 0:NFULL], self.total[:].unsqueeze(2).broadcast_to([P, E, NFULL]),
                                     m.const["full"].unsqueeze(1).broadcast_to([P, E, NFULL]), ALU.is_gt))
        step(nc.vector.tensor_reduce(used, w[:, 0:E, 0:NFULL], AX_X, ALU.add))
        step(nc.vector.tensor_copy(end, used))
        for e in range(1, E):
            step(nc.vector.tensor_tensor(end[:, e:e + 1], end[:, e:e + 1], end[:, e - 1:e], ALU.add))
        step(nc.vector.tensor_tensor(v[:, 11, 0:E], end, used, ALU.subtract))
        step(nc.vector.tensor_scalar(v[:, 11, 0:E], v[:, 11, 0:E], float(BLOCK), None, ALU.mult))
        step(nc.vector.tensor_tensor(w[:, 0:NBLOCKS, 0:E], end.unsqueeze(1).broadcast_to([P, NBLOCKS, E]),
                                     m.const["block"].unsqueeze(2).broadcast_to([P, NBLOCKS, E]), ALU.is_le))
        step(nc.vector.tensor_reduce(self.be[:, 0], w[:, 0:NBLOCKS, 0:E], AX_X, ALU.add))
        step(nc.vector.tensor_scalar(self.be[:, 1], self.be[:, 0], float(E - 1), float(P), ALU.min, ALU.mult))
        step(nc.vector.tensor_tensor(self.be[:, 2], self.be[:, 1], m.const["rows"].broadcast_to([P, NBLOCKS]), ALU.add))
        step(nc.vector.tensor_copy(m.block_rows[:], self.be[:, 2]))

    def positions(self, dve, own, step):
        nc, E = self.nc, self.c["E"]
        pos, run, n = self.pos, self.run, NT * E
        dve.wait_ge(self.c_ready, 1)
        ks = 2 if self.c["kind"] == "L3" else 1
        for k in range(ks):
            sums = self.psC[:, k, 256:256 + n].rearrange("p (t e) -> p t e", e=E)
            inside = self.psC[:, k, 0:n].rearrange("p (t e) -> p t e", e=E)
            r = run[:, 0]
            step(nc.vector.tensor_copy(r, sums))
            for t in range(1, NT):
                step(nc.vector.tensor_tensor(r[:, t], r[:, t], r[:, t - 1], ALU.add))
            if self.c["kind"] == "L2":
                step(nc.vector.tensor_copy(self.total[:], r[:, NT - 1]))
            if k == 0 and ks == 2:
                step(nc.vector.tensor_copy(run[:, 1, 0], r[:, NT - 1]))
            step(nc.vector.tensor_tensor(r, r, sums, ALU.subtract))
            step(nc.vector.tensor_tensor(pos[:, k], r, inside, ALU.add))
            if k == 1:
                step(nc.vector.tensor_tensor(pos[:, 1], pos[:, 1], run[:, 1, 0].unsqueeze(1).broadcast_to([P, NT, E]),
                                             ALU.add))


def experts(nc, m, name, c):
    EB, split, J = c["w1"].shape[0], c.get("split", 1), c["w1"].shape[2] // P
    C = NT // TB
    U = min(4, EB)
    glu = "w3" in c
    acc = c["dst"]
    with ExitStack() as ctx:
        sb = lambda s, shape: ctx.enter_context(nc.sbuf_tensor(f"{name}_{s}", shape, F32))
        ps = lambda s, shape: ctx.enter_context(nc.psum_tensor(f"{name}_{s}", shape, F32))
        sem = ctx.enter_context(stage(nc, m, name))
        w1, w2 = sb("w1", [P, U, J * P]), sb("w2", [P, U, J, D])
        b1 = sb("b1", [P, U, J]) if "b1" in c else None
        w3 = sb("w3", [P, U, J * P]) if glu else None
        h = sb("h", [P, 2, J, 512])
        psA = ps("psA", [P, 2, 512])
        psB = ps("psB", [P, 2, 512]) if glu else None
        psY = ps("psY", [P, 2 * split, 512])
        w_in = [sem(f"w_in{u}") for u in range(U)]
        a_full, a_free, b_full, b_free = sem("a_full"), sem("a_free"), sem("b_full"), sem("b_free")
        y_full, y_free, part = sem("y_full"), sem("y_free"), sem("part")
        block = ctx.enter_context(nc.Block())
        nw = 2 + glu + (b1 is not None)
        N = U * C * J

        def load(sp, e, u):
            sp.dma_start(w1[:, u], e(c["w1"])).then_inc(w_in[u], 16)
            if glu:
                sp.dma_start(w3[:, u], e(c["w3"])).then_inc(w_in[u], 16)
            if b1 is not None:
                sp.dma_start(b1[:, u], e(c["b1"])).then_inc(w_in[u], 16)
            sp.dma_start(w2[:, u], e(c["w2"])).then_inc(w_in[u], 16)

        @block.sync
        def _(sp):
            clear_last(m, sp)
            for u in range(U):
                load(sp, lambda a: a[u], u)
            if EB > U:
                with sp.Fori(0, EB // U - 1) as i:
                    for u in range(U):
                        sp.wait_ge(y_full, i * (U * C) + ((u + 1) * C + 2))
                        load(sp, lambda a: a[bass.ds(i * U + (U + u), 1)].rearrange(
                            "o p f -> p (o f)" if len(a.shape) == 3 else "o p j f -> p (o j) f"), u)

        @block.scalar
        def _(act):
            with act.Fori(0, EB // U) as i:
                a = Tally(N, i)
                for u in range(U):
                    for cc in range(C):
                        s = (u * C + cc) % 2
                        for j in range(J):
                            if j == 0:
                                act.wait_ge(y_full, i * (U * C) + (u * C + cc + 1))
                            act.wait_ge(a_full, a.take() + 1)
                            bias = 0.0
                            if "b1" in c:
                                bias = b1[:, u, j:j + 1]
                            nc.scalar.activation(h[:, s, j], psA[:, j % 2] if J > 1 else psA[:, s], c["act"], bias=bias
                                                 ).then_inc(a_free, 1)
                a.end()

        @block.tensor
        def _(pe):
            pe.sem_inc(a_free, 2)
            pe.sem_inc(b_free, 2)
            pe.sem_inc(y_free, 2)
            pe.sem_inc(y_full, 2)
            with pe.Fori(0, EB // U) as i:
                a = Tally(N, i)

                def hidden(k):
                    u, cc = divmod(k, C)
                    if cc == 0:
                        pe.wait_ge(w_in[u], i * (16 * nw) + 16 * nw)
                    x = m.XT[:, cc * 512:(cc + 1) * 512]
                    for j in range(J):
                        n = a.take()
                        bank = j % 2 if J > 1 else k % 2
                        pe.wait_ge(a_free, n + 1)
                        last = pe.matmul(psA[:, bank], w1[:, u, j * P:(j + 1) * P], x, start=True, stop=True)
                        if glu:
                            pe.wait_ge(b_free, n + 1)
                            last.then_inc(a_full, 1)
                            last = pe.matmul(psB[:, bank], w3[:, u, j * P:(j + 1) * P], x, start=True, stop=True)
                            last.then_inc(b_full, 1)
                        else:
                            last.then_inc(a_full, 1)

                def outputs(k):
                    u, cc = divmod(k, C)
                    pe.wait_ge(b_free if glu else a_free, i * N + ((k + 1) * J + 2))
                    pe.wait_ge(y_free, i * (U * C) + (k + 1))
                    for q in range(split):
                        r = slice(q * (P // split), (q + 1) * (P // split))
                        for t in range(TB):
                            for j in range(J):
                                last = pe.matmul(psY[:, (k % 2) * split + q, t * P:(t + 1) * P], h[r, k % 2, j, t * P:(t + 1) * P],
                                                 w2[r, u, j], start=(t == 0 and j == 0),
                                                 stop=(t == TB - 1 and j == J - 1 and "b2" not in c), skip_group_check=True)
                            if "b2" in c:
                                last = pe.matmul(psY[:, (k % 2) * split + q, t * P:(t + 1) * P], m.ones[0:1, :],
                                                 c["b2"](i, U, u), start=False, stop=(t == TB - 1), skip_group_check=True)
                    last.then_inc(y_full, 1)

                hidden(0)
                for k in range(U * C):
                    if k + 1 < U * C:
                        hidden(k + 1)
                    outputs(k)
                a.end()

        @block.vector
        def _(dve):
            with dve.Fori(0, EB // U) as i:
                n = Tally(N, i)

                def gate(k):
                    for j in range(J):
                        x = n.take()
                        bank = j % 2 if J > 1 else k % 2
                        dve.wait_ge(a_free, x + 3)
                        dve.wait_ge(b_full, x + 1)
                        nc.vector.tensor_tensor(h[:, k % 2, j], h[:, k % 2, j], psB[:, bank], ALU.mult).then_inc(b_free, 1)

                if glu:
                    gate(0)
                for k in range(U * C):
                    u, cc = divmod(k, C)
                    if glu and k + 1 < U * C:
                        gate(k + 1)
                    dve.wait_ge(y_full, i * (U * C) + (k + 3))
                    for q in range(split):
                        for t in range(TB):
                            x = acc[:, cc * TB + t]
                            if q == 0 and t == 0:
                                dve.wait_ge(y_free, i * (U * C) + (k + 2))
                            elif q > 0 and t == 0:
                                dve.wait_ge(part, i * (U * C * (split - 1)) + (k * (split - 1) + q))
                            last = nc.vector.scalar_tensor_tensor(x, psY[:, (k % 2) * split + q, t * P:(t + 1) * P],
                                                                  c["share"](i, U, u, q, cc * TB + t), x, ALU.mult, ALU.add)
                        if q < split - 1:
                            last.then_inc(part, 1)
                    last.then_inc(y_free, 1)
                if glu:
                    n.end()



def routed_experts(nc, m, name, c):
    J, U, chunks = c["w1"].shape[2] // P, c["U"], c["chunks"]
    T, CH = sum(chunks), len(chunks)
    blocks = c.get("blocks")
    EB = blocks or c["w1"].shape[0]
    NMAX = max(chunks) * P
    UC = U * CH
    assert UC % 2 == 0 and UC >= 4 and EB % U == 0
    TOT = EB * CH
    NS = EB * T * P
    glu = "w3" in c
    b1, b2 = "b1" in c, "b2" in c
    units = [(u, sum(chunks[:q]), chunks[q]) for u in range(U) for q in range(CH)]
    slots, results = m.slots[c["key"]], m.results[c["key"]]
    cleared, sent0, back0 = m.cleared, m.sent, list(m.back)
    per = [units[0][2], units[1][2]]
    assert all(x[2] == per[k % 2] for k, x in enumerate(units))
    m.sent += 2 * NT
    m.back = [back0[p] + TOT // 2 * per[p] for p in range(2)]
    with ExitStack() as ctx:
        sb = lambda s, shape: ctx.enter_context(nc.sbuf_tensor(f"{name}_{s}", shape, F32))
        ps = lambda s, shape: ctx.enter_context(nc.psum_tensor(f"{name}_{s}", shape, F32))
        sem = ctx.enter_context(stage(nc, m, name))
        w1, w2 = sb("w1", [P, U, J * P]), sb("w2", [P, U, J, D])
        w3 = sb("w3", [P, U, J * P]) if glu else None
        b1s = sb("b1", [P, U, J]) if b1 else None
        b2s = sb("b2", [P, U, D]) if b2 else None
        pay, waited = sb("pay", [P, 2, NT, PAY]), sb("waited", [P, 1])
        xs, xsT = sb("xs", [P, U, T, PAY]), sb("xsT", [P, 2, NMAX])
        home = ctx.enter_context(nc.sbuf_tensor(f"{name}_home", [P, U, T], I32))
        h, ys = sb("h", [P, 2, J, NMAX]), sb("ys", [P, 2, NMAX // P, D])
        psT, psA, psY = ps("psT", [P, 2, 512]), ps("psA", [P, 2, 512]), ps("psY", [P, 2, 512])
        psB = ps("psB", [P, 2, 512]) if glu else None
        w_in = m.fetched if blocks else [sem(f"w_in{u}") for u in range(U)]
        x_in = [sem(f"x_in{u}") for u in range(U)]
        scattered, returned = m.scattered, m.returned
        back_in = [sem(f"back_in{g}") for g in range(TB)]
        rows_ready, tags_ready = sem("rows_ready"), sem("tags_ready")
        t_full, t_free = sem("t_full"), sem("t_free")
        a_full, a_free = sem("a_full"), sem("a_free")
        b_full, b_free = (sem("b_full"), sem("b_free")) if glu else (a_full, a_free)
        turn = sem("turn")
        y_full, y_free, y_ready, summed = sem("y_full"), sem("y_free"), sem("y_ready"), sem("summed")
        block = ctx.enter_context(nc.Block())
        nw = 2 + glu + b1 + b2
        N = UC * J
        slots_in = slots.rearrange("(e t p) d -> e p t d", p=P, t=T)

        @block.sync
        def _(sp):
            clear_last(m, sp)

            def load_w(e, u):
                if blocks:
                    return
                sp.dma_start(w1[:, u], e(c["w1"])).then_inc(w_in[u], 16)
                if glu:
                    sp.dma_start(w3[:, u], e(c["w3"])).then_inc(w_in[u], 16)
                if b1:
                    sp.dma_start(b1s[:, u], e(c["b1"])).then_inc(w_in[u], 16)
                if b2:
                    sp.dma_start(b2s[:, u], e(c["b2"]).broadcast_to([P, D])).then_inc(w_in[u], 16)
                sp.dma_start(w2[:, u], e(c["w2"])).then_inc(w_in[u], 16)

            for u in range(U):
                load_w(lambda a: a[u], u)
            sp.wait_ge(scattered, 16 * (sent0 + 2 * NT))
            for u in range(U):
                sp.dma_start(xs[:, u], slots_in[u]).then_inc(x_in[u], 16)
            with sp.Fori(0, EB // U - 1) as i:
                for u in range(U):
                    at = lambda a: a[bass.ds(i * U + (U + u), 1)].rearrange(
                        "o p f -> p (o f)" if len(a.shape) == 3 else "o p j f -> p (o j) f")
                    sp.wait_ge(y_free, i * UC + ((u + 1) * CH + 2))
                    sp.dma_start(xs[:, u], at(slots_in)).then_inc(x_in[u], 16)
                    load_w(at, u)
            for p in range(2):
                sp.wait_ge(returned[p], 16 * m.back[p])
            for g in range(TB):
                for k, back in enumerate((m.XN, m.XT3)):
                    src = results[(k * NT + g * TB) * P:(k * NT + (g + 1) * TB) * P].rearrange("(t p) d -> p t d", p=P)
                    sp.dma_start(back[:, g * TB:(g + 1) * TB], src).then_inc(back_in[g], 16)

        @block.scalar
        def _(act):
            for k in range(2):
                for g in range(TB):
                    ts = slice(g * TB, (g + 1) * TB)
                    nc.scalar.copy(pay[:, k, ts, 0:D], c["rows"][:, ts]).then_inc(rows_ready, 1)
            with act.Fori(0, EB // U) as i:
                a = Tally(N, i)

                def turned(k):
                    tiles = units[k][2]
                    act.wait_ge(t_full, i * UC + (k + 1))
                    act.wait_ge(b_full, i * N + (k + 1) * J)
                    src, dst = psT[:, k % 2, 0:tiles * P], xsT[:, k % 2, 0:tiles * P]
                    if c.get("scale") is None:
                        nc.scalar.copy(dst, src).then_inc(t_free, 1)
                    else:
                        nc.scalar.activation(dst, src, ACT.Identity, bias=c["bias"], scale=c["scale"]).then_inc(t_free, 1)

                turned(0)
                turned(1)
                for k, (u, _, tiles) in enumerate(units):
                    for j in range(J):
                        if j == 0:
                            act.wait_ge(y_full, i * UC + (k + 1))
                        act.wait_ge(a_full, a.take() + (2 * J + 1))
                        nc.scalar.activation(h[:, k % 2, j, 0:tiles * P], psA[:, j % 2, 0:tiles * P], c["act"],
                                             bias=b1s[:, u, j:j + 1] if b1 else 0.0).then_inc(a_free, 1)
                    if k + 2 < UC:
                        turned(k + 2)
                a.end()

        @block.tensor
        def _(pe):
            pe.sem_inc(t_free, 2)
            pe.sem_inc(a_free, 2)
            pe.sem_inc(a_full, 2 * J)
            if glu:
                pe.sem_inc(b_free, 2)
                pe.sem_inc(b_full, 2 * J)
            pe.sem_inc(y_free, 2)
            pe.sem_inc(y_full, 2)
            with pe.Fori(0, EB // U) as i:
                a = Tally(N, i)

                def turn(k):
                    u, first, tiles = units[k]
                    if first == 0:
                        pe.wait_ge(x_in[u], i * 16 + 16)
                    pe.wait_ge(t_free, i * UC + (k + 1))
                    for t in range(tiles):
                        last = pe.transpose(psT[:, k % 2, t * P:(t + 1) * P], xs[:, u, first + t, 0:D], m.ident)
                    last.then_inc(t_full, 1)

                def hidden(k):
                    u, first, tiles = units[k]
                    w = tiles * P
                    if first == 0:
                        pe.wait_ge(w_in[u], i * (16 * nw) + 16 * nw)
                    pe.wait_ge(t_free, i * UC + (k + 3))
                    x = xsT[:, k % 2, 0:w]
                    for j in range(J):
                        n = a.take()
                        pe.wait_ge(a_free, n + 1)
                        pe.matmul(psA[:, j % 2, 0:w], w1[:, u, j * P:(j + 1) * P], x, start=True, stop=True).then_inc(a_full, 1)
                        if glu:
                            pe.wait_ge(b_free, n + 1)
                            pe.matmul(psB[:, j % 2, 0:w], w3[:, u, j * P:(j + 1) * P], x, start=True, stop=True).then_inc(b_full, 1)

                def outputs(k):
                    u, first, tiles = units[k]
                    pe.wait_ge(b_free, i * N + ((k + 1) * J + 2))
                    pe.wait_ge(y_free, i * UC + (k + 1))
                    for t in range(tiles):
                        for j in range(J):
                            last = pe.matmul(psY[:, k % 2, t * P:(t + 1) * P], h[:, k % 2, j, t * P:(t + 1) * P], w2[:, u, j],
                                             start=(t == 0 and j == 0), stop=(t == tiles - 1 and j == J - 1),
                                             skip_group_check=True)
                    last.then_inc(y_full, 1)

                turn(0)
                turn(1)
                hidden(0)
                for k in range(UC):
                    if k + 2 < UC:
                        turn(k + 2)
                    if k + 1 < UC:
                        hidden(k + 1)
                    outputs(k)
                a.end()

        @block.vector
        def _(dve):
            nc.vector.tensor_copy(pay[:, :, :, D], m.const["home"].rearrange("p (k t) -> p k t", k=2))
            nc.vector.tensor_copy(pay[:, :, :, D + 1], m.slot_share[:]).then_inc(tags_ready, 1)
            with dve.Fori(0, EB // U) as i:
                n = Tally(N, i)

                def gate(k):
                    w = units[k][2] * P
                    for j in range(J):
                        x = n.take()
                        dve.wait_ge(a_free, x + 3)
                        dve.wait_ge(b_full, x + (2 * J + 1))
                        nc.vector.tensor_tensor(h[:, k % 2, j, 0:w], h[:, k % 2, j, 0:w], psB[:, j % 2, 0:w], ALU.mult
                                                ).then_inc(b_free, 1)

                if glu:
                    gate(0)
                for k, (u, first, tiles) in enumerate(units):
                    if glu and k + 1 < UC:
                        gate(k + 1)
                    p = k % 2
                    dve.wait_ge(y_full, i * UC + (k + 3))
                    dve.wait_ge(returned[p], i * (8 * UC * per[p]) + 16 * (back0[p] + k // 2 * per[p]))
                    share = xs[:, u, first:first + tiles, D + 1:PAY].broadcast_to([P, tiles, D])
                    src, dst = psY[:, p, 0:tiles * P].rearrange("p (t d) -> p t d", d=D), ys[:, p, 0:tiles]
                    nc.vector.tensor_copy(home[:, u, first:first + tiles], xs[:, u, first:first + tiles, D])
                    if b2:
                        nc.vector.tensor_tensor(dst, src, b2s[:, u:u + 1].broadcast_to([P, tiles, D]), ALU.add
                                                ).then_inc(y_ready, 1)
                        dve.wait_ge(y_ready, i * UC + (k + 1))
                        src = dst
                    nc.vector.tensor_tensor(dst, src, share, ALU.mult).then_inc(y_free, 1)
                if glu:
                    n.end()
            for g in range(TB):
                dve.wait_ge(back_in[g], 32)
                for k, back in enumerate((m.XN, m.XT3)):
                    if k:
                        dve.wait_ge(summed, 2 * g + 1)
                    ts = slice(g * TB, (g + 1) * TB)
                    nc.vector.tensor_tensor(m.X[:, ts], m.X[:, ts], back[:, ts], ALU.add).then_inc(summed, 1)

        @block.gpsimd
        def _(pool):
            pool.wait_ge(m.zeroed, 16 * cleared)
            pool.wait_ge(tags_ready, 1)
            for k in range(2):
                for t in range(NT):
                    if t % TB == 0:
                        pool.wait_ge(rows_ready, (k * NT + t) // TB + 1)
                    pool.indirect_dma_start(slots, bass.IndirectOffsetOnAxis(ap=m.slot_to[:, k, t:t + 1], axis=0),
                                            pay[:, k, t], None, bounds_check=NS - 1, oob_is_err=False
                                            ).then_inc(scattered, 16)

            def fetch(e):
                rows, u = m.block_rows[:, e:e + 1], e % U
                for dst, src in ((w1[:, u], c["w1"].rearrange("e p f -> (e p) f")),
                                 (w2[:, u].rearrange("p j d -> p (j d)"), c["w2"].rearrange("e p j d -> (e p) (j d)"))):
                    pool.indirect_dma_start(dst, None, src, bass.IndirectOffsetOnAxis(ap=rows, axis=0),
                                            bounds_check=8 * P - 1, oob_is_err=False).then_inc(w_in[u], 16)

            def give_back(k):
                u, first, tiles = units[k]
                for t in range(tiles):
                    pool.indirect_dma_start(results, bass.IndirectOffsetOnAxis(ap=home[:, u, first + t:first + t + 1], axis=0),
                                            ys[:, k % 2, t], None, bounds_check=2 * NT * P - 1, oob_is_err=False
                                            ).then_inc(returned[k % 2], 16)

            if blocks:
                for e in range(U):
                    fetch(e)
                for e in range(EB):
                    pool.wait_ge(y_free, e + 3)
                    give_back(e % U)
                    if e + U < EB:
                        fetch(e + U)
            else:
                pool.sem_inc(turn, 1)
                with pool.Fori(0, EB // U) as i:
                    for k in range(UC):
                        pool.wait_ge(turn, i * UC + (k + 1))
                        pool.wait_ge(y_free, i * UC + (k + 3))
                        nc.gpsimd.tensor_tensor(waited[:], m.ones[:, 0:1], m.ones[:, 0:1], ALU.mult).then_inc(turn, 1)
                        give_back(k)


def add_layer(nc, m, name, src, gate, w=None, b=None):
    with ExitStack() as ctx:
        own_v = ctx.enter_context(stage(nc, m, name))("own")
        block = ctx.enter_context(nc.Block())

        @block.sync
        def _(sp):
            clear_last(m, sp)

        @block.vector
        def _(dve):
            own = Own(dve, own_v)
            if w is not None:
                own.done(nc.vector.tensor_tensor(src[:], src[:], w.unsqueeze(1).broadcast_to([P, NT, D]), ALU.mult))
                own.wait()
                own.done(nc.vector.tensor_tensor(src[:], src[:], b.unsqueeze(1).broadcast_to([P, NT, D]), ALU.add))
                own.wait()
            nc.vector.scalar_tensor_tensor(m.X[:], src[:], m.gate(gate), m.X[:], ALU.mult, ALU.add)


def single_head(nc, m):
    nm, w = "L3x", m.w
    SC = 1.0 / float(np.sqrt(np.float32(D)))
    BK = B * S2
    with ExitStack() as ctx:
        sb = lambda s, shape: ctx.enter_context(nc.sbuf_tensor(f"{nm}_{s}", shape, F32))
        ps = lambda s, shape: ctx.enter_context(nc.psum_tensor(f"{nm}_{s}", shape, F32))
        sem = ctx.enter_context(stage(nc, m, nm))
        stats, ln = sb("stats", [P, NT, 6]), sb("ln", [P, 9, NT])
        xnT = sb("xnT", [P, 2, 512])
        KT, G, V, Vr = sb("KT", [P, BK]), sb("G", [P, BK]), sb("V", [P, B, D]), sb("Vr", [KR, B, D])
        bqr, nmx, nms = sb("bqr", [P, P]), sb("nmx", [P, 2, TB]), sb("nms", [P, 2, TB])
        rs, rin = sb("rs", [P, 2, TB]), sb("rin", [P, 2, TB])
        pr = sb("pr", [P, 2, TB, S2])
        PT, PTr, OT = sb("PT", [P, 512]), sb("PTr", [KR, 512]), sb("OT", [P, 512])
        psX, psS, psP, psPr = ps("psX", [P, 512]), ps("psS", [P, 2, 512]), ps("psP", [P, 512]), ps("psPr", [P, 512])
        psO, psY, psK = ps("psO", [P, 512]), ps("psY", [P, 512]), ps("psK", [P, 512])
        own_v, var_ready, std_ready = sem("own_v"), sem("var_ready"), sem("std_ready")
        b_ready, k_full, k_done, g_full, g_done, v_full, v_done = (
            sem(s) for s in ("b_ready", "k_full", "k_done", "g_full", "g_done", "v_full", "v_done"))
        xn_ready, x_full, xt_done = sem("xn_ready"), sem("x_full"), sem("xt_done")
        s_full, m_ready, e_ready, p_ready = sem("s_full"), sem("m_ready"), sem("e_ready"), sem("p_ready")
        p_full, pt_done, o_full, ot_done, y_full, y_done = (
            sem("p_full"), sem("pt_done"), sem("o_full"), sem("ot_done"), sem("y_full"), sem("y_done"))
        block = ctx.enter_context(nc.Block())
        ctx_all = m.ctxT[:].rearrange("p b k -> p (b k)")
        parts = [slice(0, 512), slice(512, BK)]

        @block.sync
        def _(sp):
            clear_last(m, sp)

        @block.scalar
        def _(act):
            for k, c in enumerate(parts):
                act.wait_ge(k_full, k + 1)
                nc.scalar.copy(KT[:, c], psS[:, k, 0:c.stop - c.start]).then_inc(k_done, 1)
            act.wait_ge(v_full, 1)
            nc.scalar.copy(V[:], psK[:].rearrange("p (b d) -> p b d", d=D)).then_inc(v_done, 1)
            act.wait_ge(v_full, 2)
            nc.scalar.copy(Vr[:], psY[0:KR].rearrange("p (b d) -> p b d", d=D)).then_inc(v_done, 1)
            for k, c in enumerate(parts):
                act.wait_ge(g_full, k + 1)
                nc.scalar.copy(G[:, c], (psO if k else psP)[:, 0:c.stop - c.start]).then_inc(g_done, 1)
            act.wait_ge(var_ready, 1)
            nc.scalar.activation(ln[:, 8], ln[:, 7], ACT.Sqrt).then_inc(std_ready, 1)
            for s in range(-1, B + 1):
                if 0 <= s - 1:
                    act.wait_ge(p_full, s)
                    if s >= 2:
                        act.wait_ge(o_full, s - 1)
                    nc.scalar.copy(PT[:], psP[:]).then_inc(pt_done, 1)
                    nc.scalar.copy(PTr[:], psPr[0:KR]).then_inc(pt_done, 1)
                if s + 1 < B:
                    act.wait_ge(x_full, s + 2)
                    if s >= 1:
                        act.wait_ge(s_full, TB * s)
                    nc.scalar.copy(xnT[:, (s + 1) % 2], psX[:]).then_inc(xt_done, 1)
                if 0 <= s < B:
                    act.wait_ge(m_ready, s + 1)
                    for t in range(TB):
                        nc.scalar.activation(pr[:, s % 2, t], psS[:, t // 2, (t % 2) * S2:(t % 2 + 1) * S2], ACT.Exp, scale=SC,
                                             bias=nms[:, s % 2, t:t + 1], accum_out=rs[:, s % 2, t:t + 1]).then_inc(e_ready, 1)
                if 0 <= s - 1:
                    act.wait_ge(o_full, s)
                    if s >= 2:
                        act.wait_ge(y_full, s - 1)
                    nc.scalar.copy(OT[:], psO[:]).then_inc(ot_done, 1)

        @block.tensor
        def _(pe):
            for k, c in enumerate(parts):
                pe.matmul(psS[:, k, 0:c.stop - c.start], w["L3_xattn_Wk"][:], ctx_all[:, c], start=True, stop=True).then_inc(k_full, 1)
            for r, bank, lo, hi in ((P, psK, 0, KM_), (KR, psY, KM_, S2)):
                for b in range(B):
                    o = bank[0:r, b * D:(b + 1) * D]
                    pe.matmul(o, m.ctxT[:, b, lo:hi], w["L3_xattn_Wv"][:], start=(b == 0), stop=False, skip_group_check=True)
                    last = pe.matmul(o, m.ones[0:1, 0:r], m.row("L3_xattn_bv"), start=False, stop=(b == B - 1), skip_group_check=True)
                last.then_inc(v_full, 1)
            for k, c in enumerate(parts):
                pe.wait_ge(k_done, k + 1)
                pe.matmul((psO if k else psP)[:, 0:c.stop - c.start], w["L3_xattn_Wq"][:], KT[:, c], start=True, stop=True
                          ).then_inc(g_full, 1)
            pe.wait_ge(v_done, 2)
            pe.wait_ge(g_done, 2)
            pe.wait_ge(b_ready, 1)
            for s in range(-1, B + 2):
                if 0 <= s < B:
                    pe.wait_ge(xt_done, s + 1)
                    if s >= 1:
                        pe.wait_ge(e_ready, TB * s)
                    for t in range(TB):
                        o = psS[:, t // 2, (t % 2) * S2:(t % 2 + 1) * S2]
                        keys = slice(s * S2, (s + 1) * S2)
                        pe.matmul(o, xnT[:, s % 2, t * P:(t + 1) * P], G[:, keys], start=(t % 2 == 0), stop=False, skip_group_check=True)
                        pe.matmul(o, bqr[:], KT[:, keys], start=False, stop=(t % 2 == 1), skip_group_check=True).then_inc(s_full, 1)
                if 0 <= s - 1 < B:
                    pe.wait_ge(p_ready, s)
                    if s >= 2:
                        pe.wait_ge(pt_done, 2 * (s - 1))
                    for t in range(TB):
                        pe.transpose(psP[:, t * P:(t + 1) * P], pr[:, (s - 1) % 2, t, 0:KM_], m.ident)
                    for t in range(TB):
                        last = pe.transpose(psPr[0:KR, t * P:(t + 1) * P], pr[:, (s - 1) % 2, t, KM_:S2], m.ident)
                    last.then_inc(p_full, 1)
                if s + 1 < B:
                    pe.wait_ge(xn_ready, s + 2)
                    if s >= 0:
                        pe.wait_ge(xt_done, s + 1)
                    for t in range(TB):
                        last = pe.transpose(psX[:, t * P:(t + 1) * P], m.XN[:, (s + 1) * TB + t], m.ident)
                    last.then_inc(x_full, 1)
                if 0 <= s - 2:
                    pe.wait_ge(ot_done, s - 1)
                    if s >= 3:
                        pe.wait_ge(y_done, s - 2)
                    for t in range(TB):
                        o = psY[:, t * P:(t + 1) * P]
                        pe.matmul(o, OT[:, t * P:(t + 1) * P], w["L3_xattn_Wo"][:], start=(t == 0), stop=False, skip_group_check=True)
                        last = pe.matmul(o, m.ones[0:1, :], m.row("L3_xattn_bo"), start=False, stop=(t == TB - 1), skip_group_check=True)
                    last.then_inc(y_full, 1)
                if 0 <= s - 1 < B:
                    pe.wait_ge(pt_done, 2 * s)
                    if s >= 2:
                        pe.wait_ge(ot_done, s - 1)
                    pe.matmul(psO[:], V[:, s - 1], PT[:], start=True, stop=False)
                    pe.matmul(psO[:], Vr[:, s - 1], PTr[:], start=False, stop=True).then_inc(o_full, 1)

        @block.vector
        def _(dve):
            own = Own(dve, own_v)
            nc.vector.tensor_copy(bqr[:], m.col("L3_xattn_bq").broadcast_to([P, P])).then_inc(b_ready, 1)
            ln_stats_vector(nc, dve, own, stats, ln, m.X, var_ready, std_ready)
            for t in range(NT):
                last = nc.vector.tensor_scalar(m.XN[:, t], m.X[:, t], ln[:, 0, t:t + 1], ln[:, 1, t:t + 1], ALU.subtract, ALU.mult)
                if t % TB == TB - 1:
                    last.then_inc(xn_ready, 1)
            for s in range(B + 2):
                if s < B:
                    p = s % 2
                    dve.wait_ge(s_full, TB * (s + 1))
                    own.done(nc.vector.tensor_reduce(nmx[:, p].rearrange("p (a t) -> p a t", a=2),
                                                     psS[:, :, 0:2 * S2].rearrange("p a (t k) -> p a t k", k=S2), AX_X, ALU.max))
                    own.wait()
                    nc.vector.tensor_scalar(nms[:, p], nmx[:, p], -SC, None, ALU.mult).then_inc(m_ready, 1)
                    dve.wait_ge(e_ready, TB * (s + 1))
                    own.done(nc.vector.reciprocal(rin[:, p], rs[:, p]))
                    own.wait()
                    nc.vector.tensor_tensor(pr[:, p], pr[:, p], rin[:, p].unsqueeze(2).broadcast_to([P, TB, S2]), ALU.mult
                                            ).then_inc(p_ready, 1)
                if s >= 2:
                    dve.wait_ge(y_full, s - 1)
                    x = m.X[:, (s - 2) * TB:(s - 1) * TB].rearrange("p t d -> p (t d)")
                    nc.vector.scalar_tensor_tensor(x, psY[:], m.gate(3), x, ALU.mult, ALU.add).then_inc(y_done, 1)


def self_attention(nc, m, d):
    nm, w = "L3s", m.w
    BF = mybir.dt.bfloat16
    DH = D // H
    TR = 9 * DH
    SC = 1.0 / float(np.sqrt(8.0))
    q_parts = nc.dram_tensor("q_parts", (3, 3, P, NT * P), BF).ap()
    k_parts = nc.dram_tensor("k_parts", (3, P, NT * P), BF).ap()
    max_parts = nc.dram_tensor("max_parts", (B * HG, 3, HG, S), BF).ap()
    with ExitStack() as ctx0:
        VW = H * (DH + 1) + 24
        V = ctx0.enter_context(nc.sbuf_tensor(f"{nm}_V", [P, NT, VW], F32))
        Vh = V[:, :, 0:H * (DH + 1)].rearrange("p t (h d) -> p t h d", d=DH + 1)
        with ExitStack() as ctx:
            sb = lambda s, shape, dt=F32: ctx.enter_context(nc.sbuf_tensor(f"{nm}_{s}", shape, dt))
            sem = ctx.enter_context(stage(nc, m, nm))
            C = NT // TB
            ps = ctx.enter_context(nc.psum_tensor(f"{nm}_psP", [P, 2, 512], F32))
            psV = ctx.enter_context(nc.psum_tensor(f"{nm}_psV", [P, 2, 512], F32))
            parts = sb("parts", [P, 2, 3, NT * P], BF)
            full, rest = sb("full", [P, 2, 512]), sb("rest", [P, 2, 512])
            qb = sb("qb", [P, 1])
            qb_ready, p_full, f_ready, hi_ready = sem("qb_ready"), sem("p_full"), sem("f_ready"), sem("hi_ready")
            r_ready, mid_ready, lo_ready = sem("r_ready"), sem("mid_ready"), sem("lo_ready")
            v_full, v_done, stored = sem("v_full"), sem("v_done"), sem("stored")
            block = ctx.enter_context(nc.Block())

            @block.tensor
            def _(pe):
                for k in range(2):
                    for c in range(C):
                        n = k * C + c
                        if n >= 2:
                            pe.wait_ge(f_ready, n - 1)
                        pe.matmul(ps[:, n % 2], w["L3_ffn_q_w" if k == 0 else "L3_ffn_k_w"][:], m.XT[:, c * 512:(c + 1) * 512],
                                  start=True, stop=True).then_inc(p_full, 1)
                for c in range(C):
                    if c >= 2:
                        pe.wait_ge(v_done, c - 1)
                    for t in range(TB):
                        o = psV[:, c % 2, t * P:(t + 1) * P]
                        tt = c * TB + t
                        pe.matmul(o, m.XT[:, tt * P:(tt + 1) * P], w["L3_ffn_v_w"][:], start=(t == 0), stop=False, skip_group_check=True)
                        last = pe.matmul(o, m.ones[0:1, :], m.row("L3_ffn_v_b"), start=False, stop=(t == TB - 1), skip_group_check=True)
                    last.then_inc(v_full, 1)

            @block.scalar
            def _(act):
                act.wait_ge(qb_ready, 1)
                for k in range(2):
                    for c in range(C):
                        n = k * C + c
                        cs = slice(c * 512, (c + 1) * 512)
                        act.wait_ge(p_full, n + 1)
                        if n >= 2:
                            act.wait_ge(r_ready, n - 1)
                        if k == 0:
                            nc.scalar.activation(full[:, n % 2], ps[:, n % 2], ACT.Identity, scale=SC, bias=qb[:]).then_inc(f_ready, 1)
                        else:
                            nc.scalar.activation(full[:, n % 2], ps[:, n % 2], ACT.Identity, bias=m.col("L3_ffn_k_b")).then_inc(f_ready, 1)
                        act.wait_ge(f_ready, n + 1)
                        nc.scalar.copy(parts[:, k, 0, cs], full[:, n % 2]).then_inc(hi_ready, 1)
                        act.wait_ge(r_ready, n + 1)
                        nc.scalar.copy(parts[:, k, 1, cs], rest[:, n % 2]).then_inc(mid_ready, 1)
                for c in range(C):
                    act.wait_ge(v_full, c + 1)
                    nc.scalar.copy(Vh[:, c * TB:(c + 1) * TB, :, 0:DH],
                                   psV[:, c % 2].rearrange("p (t h d) -> p t h d", h=H, d=DH)).then_inc(v_done, 1)

            @block.vector
            def _(dve):
                nc.vector.tensor_scalar(qb[:], m.col("L3_ffn_q_b"), SC, None, ALU.mult).then_inc(qb_ready, 1)
                nc.vector.memset(Vh[:, :, :, DH:DH + 1], 1.0)
                nc.vector.memset(V[:, :, H * (DH + 1):VW], 0.0)
                for k in range(2):
                    for c in range(C):
                        n = k * C + c
                        cs = slice(c * 512, (c + 1) * 512)
                        dve.wait_ge(hi_ready, n + 1)
                        if n >= 2:
                            dve.wait_ge(lo_ready, n - 1)
                        nc.vector.tensor_tensor(rest[:, n % 2], full[:, n % 2], parts[:, k, 0, cs], ALU.subtract).then_inc(r_ready, 1)
                        dve.wait_ge(mid_ready, n + 1)
                        nc.vector.tensor_tensor(parts[:, k, 2, cs], rest[:, n % 2], parts[:, k, 1, cs], ALU.subtract).then_inc(lo_ready, 1)

            @block.sync
            def _(sp):
                clear_last(m, sp)
                sp.wait_ge(lo_ready, C)
                for i in range(3):
                    sp.dma_start(q_parts[i].rearrange("j p t -> p j t"), parts[:, 0, i:i + 1].broadcast_to([P, 3, NT * P])
                                 ).then_inc(stored, 16)
                sp.wait_ge(lo_ready, 2 * C)
                sp.dma_start(k_parts.rearrange("s p t -> p s t"), parts[:, 1]).then_inc(stored, 16)
                sp.wait_ge(stored, 64)

        with ExitStack() as ctx:
            sb = lambda s, shape, dt=F32: ctx.enter_context(nc.sbuf_tensor(f"{nm}_{s}", shape, dt))
            ps = lambda s, shape: ctx.enter_context(nc.psum_tensor(f"{nm}_{s}", shape, F32))
            sem = ctx.enter_context(stage(nc, m, nm))
            QS, KS = sb("QS", [TR + 3, 4, HG, S], BF), sb("KS", [TR + 3, 4, HG, S], BF)
            identb, trilb, triub = sb("identb", [P, P], BF), sb("trilb", [P, P], BF), sb("triub", [P, P], BF)
            onesb = sb("onesb", [3, HG, S], BF)
            mx, mr = sb("mx", [P, TB, HG]), sb("mr", [P, 2, TB, HG])
            mparts = sb("mparts", [P, TB, 3, HG], BF)
            MT = sb("MT", [3 * HG, 2, S], BF)
            EO = {0: 0, 1: S, 3: 2 * S - P, 2: 2 * S}
            EW = 2 * S + 2 * P
            E = sb("E", [P, 2, HG, EW])
            VW4 = 3 * (DH + 1) + 32
            VG = sb("VG", [P, 2, TB, VW4])
            OG, rin, OT = sb("OG", [P, S]), sb("rin", [P, TB, HG, 1]), sb("OT", [P, 2, S])
            psS, psT, psO, psM = ps("psS", [P, 3, 512]), ps("psT", [P, 3, 512]), ps("psO", [P, 512]), ps("psM", [P, 512])
            own_v, const_ready = sem("own_v2"), sem("const_ready")
            ones_in, max_out, stack_in, max_in = sem("ones_in"), sem("max_out"), [sem(f"stack_in{u}") for u in range(4)], [sem("max_in0"), sem("max_in1")]
            s_full, s_free, t_full, t_free = sem("s_full"), sem("s_free"), sem("t_full"), sem("t_free")
            mp_ready, tm_full, tm_done = sem("mp_ready"), sem("tm_full"), sem("tm_done")
            vg_ready, av_full, og_done, to_full = sem("vg_ready"), sem("av_full"), sem("og_done"), sem("to_full")
            rin_done, divided = sem("rin_done"), sem("divided")
            ot_full, ot_done, y_full, y_done = sem("ot_full"), sem("ot_done"), sem("y_full"), sem("y_done")
            block = ctx.enter_context(nc.Block())
            NGR = B * HG
            SG = [[3], [2, 0], [1]]
            TG = [[0], [1, 3], [2]]
            ND = 4 * 16

            def place(group, width):
                at, out = 0, []
                for t in group:
                    out.append((t, at, width(t)))
                    at += width(t)
                return out

            class At:

                def __init__(self, i, r):
                    self.i, self.r = i, r
                    self.slot, self.par, self.hg, self.b = r % 4, r % 2, r % 4, i + r // 4

                def __add__(self, k):
                    return At(self.i, self.r + k)

                def exists(self):
                    return not isinstance(self.i, int) or 0 <= self.r < NGR

                def n(self, per, add):
                    return self.i * (4 * per) + (self.r * per + add)

            def over_steps(eng, step, around=lambda i: None):
                for g in range(-2, 2):
                    step(At(0, g))
                with eng.Fori(0, (NGR - 4) // 4) as i:
                    around(i)
                    for r in range(2, 6):
                        step(At(i, r))
                around(None)
                for g in range(NGR - 2, NGR + 2):
                    step(At(0, g))

            @block.sync
            def _(sp):
                clear_last(m, sp)

                def stacks(g):
                    cols = bass.ds(g.b * S, S) if not isinstance(g.b, int) else slice(g.b * S, (g.b + 1) * S)
                    heads = slice(g.hg * HG, (g.hg + 1) * HG)
                    sp.dma_start(QS[0:TR, g.slot], q_parts.rearrange("i j (d h) t -> (i j d) h t", h=H)[:, heads, cols]
                                 ).then_inc(stack_in[g.slot], 16)
                    for i in range(3):
                        sp.dma_start(KS[3 * i * DH:3 * (i + 1) * DH, g.slot],
                                     k_parts.rearrange("s (d h) t -> (s d) h t", h=H)[:, heads, cols]
                                     ).then_inc(stack_in[g.slot], 16)

                def maxima_to(g):
                    sp.wait_ge(tm_done, g.n(1, 1))
                    at = max_parts[bass.ds(g.n(1, 0), 1)] if not isinstance(g.i, int) else max_parts[g.r:g.r + 1]
                    sp.dma_start(at.rearrange("o s h t -> (o s h) t"), MT[:, g.par]).then_inc(max_out, 16)
                    sp.wait_ge(max_out, g.n(16, 16))
                    sp.dma_start(QS[TR:TR + 3, g.slot], at.rearrange("o s h t -> (o s) h t")).then_inc(max_in[g.par], 16)

                for g in range(2):
                    stacks(At(0, g))
                sp.wait_ge(const_ready, 1)
                for u in range(4):
                    sp.dma_start(KS[TR:TR + 3, u], onesb[:]).then_inc(ones_in, 16)
                for g in range(2, 4):
                    stacks(At(0, g))
                maxima_to(At(0, 0))
                with sp.Fori(0, (NGR - 4) // 4) as i:
                    for r in range(4):
                        maxima_to(At(i, r) + 1)
                        sp.wait_ge(t_full, At(i, r).n(12, 12))
                        stacks(At(i, r) + 4)
                for g in range(NGR - 3, NGR):
                    maxima_to(At(0, g))

            @block.gpsimd
            def _(pool):
                with pool.Fori(0, B) as i:
                    for r in range(4):
                        g = At(i, r)
                        pool.wait_ge(av_full, g.n(1, 1))
                        nc.gpsimd.tensor_copy(VG[:, g.par], V[:, bass.ds(i * TB, TB), r * HG * (DH + 1):r * HG * (DH + 1) + VW4]
                                              ).then_inc(vg_ready, 1)

            @block.tensor
            def _(pe):
                pe.sem_inc(s_free, 3)
                pe.sem_inc(t_free, 3)
                pe.sem_inc(av_full, 2)
                pe.sem_inc(og_done, 1)
                pe.sem_inc(to_full, 1)
                pe.sem_inc(divided, 1)
                pe.wait_ge(const_ready, 1)

                def scores(g, h):
                    if h == 0:
                        pe.wait_ge(stack_in[g.slot], g.b * ND + ND)
                    for k, group in enumerate(SG):
                        pe.wait_ge(s_free, g.n(12, 3 * h + k + 1))
                        tiles = place(group, lambda t: (t + 1) * P)
                        for n, (t, at, wd) in enumerate(tiles):
                            pe.matmul(psS[:, k, at:at + wd], QS[0:TR, g.slot, h, t * P:(t + 1) * P], KS[0:TR, g.slot, h, 0:wd],
                                      start=(n == 0), stop=False, skip_group_check=True)
                            last = pe.matmul(psS[:, k, at + wd - P:at + wd], identb[:], trilb[:], start=False,
                                             stop=(n == len(tiles) - 1), skip_group_check=True)
                        last.then_inc(s_full, 1)

                def shifted(g, h):
                    if h == 0:
                        pe.wait_ge(max_in[g.par], g.i * 32 + 16 * (g.r // 2 + 1))
                    for k, group in enumerate(TG):
                        pe.wait_ge(t_free, g.n(12, 3 * h + k + 1))
                        tiles = place(group, lambda t: (TB - t) * P)
                        for n, (t, at, wd) in enumerate(tiles):
                            pe.matmul(psT[:, k, at:at + wd], KS[0:TR + 3, g.slot, h, t * P:(t + 1) * P], QS[0:TR + 3, g.slot, h, t * P:S],
                                      start=(n == 0), stop=False, skip_group_check=True)
                            last = pe.matmul(psT[:, k, at:at + P], identb[:], triub[:], start=False,
                                             stop=(n == len(tiles) - 1), skip_group_check=True)
                        last.then_inc(t_full, 1)

                def values(g, j):
                    if j == 0:
                        pe.wait_ge(t_free, g.n(12, 15))
                        pe.wait_ge(vg_ready, g.n(1, 1))
                        pe.wait_ge(og_done, g.n(1, 1))
                    for h in range(HG):
                        last = pe.matmul(psO[32 * h:32 * h + 32, j * P:S], VG[:, g.par, j, h * (DH + 1):h * (DH + 1) + 32],
                                         E[:, g.par, h, EO[j]:EO[j] + S - j * P], start=(j == 0), stop=(j == TB - 1),
                                         skip_group_check=True)
                    if j == TB - 1:
                        last.then_inc(av_full, 1)

                def turn_maxima(g):
                    pe.wait_ge(mp_ready, g.n(1, 1))
                    if not isinstance(g.i, int) or g.r >= 3:
                        pe.wait_ge(divided, g.n(1, -2))
                    for t in range(TB):
                        last = pe.transpose(psM[0:3 * HG].bitcast(BF)[:, t * P:(t + 1) * P], mparts[:, t].rearrange("p s h -> p (s h)"), identb[:])
                    last.then_inc(tm_full, 1)

                def turn_outputs(g):
                    pe.wait_ge(og_done, g.n(1, 2))
                    pe.wait_ge(tm_done, g.n(1, 4) if not isinstance(g.i, int) else min(g.r + 4, NGR))
                    pe.wait_ge(divided, g.n(1, 1))
                    for t in range(TB):
                        last = pe.transpose(psM[:, t * P:(t + 1) * P], OG[:, t * P:(t + 1) * P], m.ident)
                    last.then_inc(to_full, 1)

                def step(g):
                    for h in range(HG):
                        if (g + 2).exists():
                            scores(g + 2, h)
                        if h == 1 and (g + 1).exists():
                            turn_maxima(g + 1)
                        if h == 2 and (g + -2).exists():
                            turn_outputs(g + -2)
                        if (g + -1).exists():
                            values(g + -1, h)
                        if g.exists():
                            if isinstance(g.i, int) and g.r == 0 and h == 0:
                                pe.wait_ge(ones_in, 64)
                            shifted(g, h)

                over_steps(pe, step)
                for b in range(B):
                    pe.wait_ge(divided, NGR + 1)
                    if b == 0:
                        pe.wait_ge(t_free, 12 * NGR + 3)
                        pe.wait_ge(s_free, 12 * NGR + 3)
                    for t in range(TB):
                        last = pe.transpose(psT[:, b % 2, t * P:(t + 1) * P], m.X1[:, b * TB + t], m.ident)
                    last.then_inc(ot_full, 1)
                    pe.wait_ge(ot_done, b + 1)
                    if b >= 2:
                        pe.wait_ge(y_done, b - 1)
                    for t in range(TB):
                        o = psS[:, b % 2, t * P:(t + 1) * P]
                        pe.matmul(o, OT[:, b % 2, t * P:(t + 1) * P], w["L3_ffn_o_w"][:], start=(t == 0), stop=False, skip_group_check=True)
                        last = pe.matmul(o, m.ones[0:1, :], m.row("L3_ffn_o_b"), start=False, stop=(t == TB - 1), skip_group_check=True)
                    last.then_inc(y_full, 1)

            @block.scalar
            def _(act):
                def exponentials(g, h):
                    if h == 0:
                        act.wait_ge(av_full, g.n(1, 1))
                    for k, group in enumerate(TG):
                        act.wait_ge(t_full, g.n(12, 3 * h + k + 1))
                        wd = sum((TB - t) * P for t in group)
                        nc.scalar.activation(E[:, g.par, h, EO[group[0]]:EO[group[0]] + wd], psT[:, k, 0:wd], ACT.Exp
                                             ).then_inc(t_free, 1)

                def step(g):
                    for h in range(HG):
                        if h == 1 and (g + 1).exists():
                            x = g + 1
                            act.wait_ge(tm_full, x.n(1, 1))
                            if not isinstance(x.i, int) or x.r >= 2:
                                act.wait_ge(max_in[x.par], x.i * 32 + 16 * (x.r // 2))
                            nc.scalar.copy(MT[:, x.par], psM[0:3 * HG].bitcast(BF)[:, 0:S]).then_inc(tm_done, 1)
                        if h == 3 and (g + -1).exists():
                            x = g + -1
                            act.wait_ge(av_full, x.n(1, 3))
                            act.wait_ge(to_full, x.n(1, 1))
                            nc.scalar.copy(OG[:], psO[:]).then_inc(og_done, 1)
                        if g.exists():
                            exponentials(g, h)

                over_steps(act, step)
                for b in range(B):
                    act.wait_ge(ot_full, b + 1)
                    if b >= 2:
                        act.wait_ge(y_full, b - 1)
                    nc.scalar.copy(OT[:, b % 2], psT[:, b % 2]).then_inc(ot_done, 1)

            @block.vector
            def _(dve):
                own = Own(dve, own_v)
                own.done(nc.vector.memset(onesb[:], 1.0))
                own.done(nc.vector.tensor_copy(identb[:], m.ident))
                own.done(nc.vector.tensor_copy(trilb[:], m.const["tril"]))
                own.wait()
                nc.vector.tensor_copy(triub[:], m.const["triu"]).then_inc(const_ready, 1)

                def maxima(g, h):
                    for k, group in enumerate(SG):
                        dve.wait_ge(s_full, g.n(12, 3 * h + k + 1))
                        for t, at, wd in place(group, lambda t: (t + 1) * P):
                            last = nc.vector.tensor_reduce(mx[:, t, h:h + 1], psS[:, k, at:at + wd], AX_X, ALU.max)
                        last.then_inc(s_free, 1)

                def cut_maxima(g):
                    dve.wait_ge(s_free, g.n(12, 15))
                    if not isinstance(g.i, int) or g.r >= 1:
                        dve.wait_ge(tm_full, g.n(1, 0))
                    own.done(nc.vector.tensor_scalar(mr[:, 0], mx[:], -1.0, None, ALU.mult))
                    own.wait()
                    own.done(nc.vector.tensor_copy(mparts[:, :, 0], mr[:, 0]))
                    own.wait()
                    own.done(nc.vector.tensor_tensor(mr[:, 1], mr[:, 0], mparts[:, :, 0], ALU.subtract))
                    own.wait()
                    own.done(nc.vector.tensor_copy(mparts[:, :, 1], mr[:, 1]))
                    own.wait()
                    nc.vector.tensor_tensor(mparts[:, :, 2], mr[:, 1], mparts[:, :, 1], ALU.subtract).then_inc(mp_ready, 1)
                    dve.wait_ge(mp_ready, g.n(1, 1))

                def divide(g):
                    out = psM[:].rearrange("p (t h d) -> p t h d", t=TB, h=HG)
                    dve.wait_ge(to_full, g.n(1, 2))
                    dve.wait_ge(divided, g.n(1, 1))
                    nc.vector.reciprocal(rin[:], out[:, :, :, DH:DH + 1]).then_inc(rin_done, 1)
                    dve.wait_ge(rin_done, g.n(1, 1))
                    rows = bass.ds(g.b * TB, TB) if not isinstance(g.b, int) else slice(g.b * TB, (g.b + 1) * TB)
                    dst = m.X1[:, rows, g.hg * HG * DH:(g.hg + 1) * HG * DH].rearrange("p t (h d) -> p t h d", d=DH)
                    nc.vector.tensor_tensor(dst, out[:, :, :, 0:DH], rin[:].broadcast_to([P, TB, HG, DH]), ALU.mult
                                            ).then_inc(divided, 1)

                def step(g):
                    for h in range(HG):
                        if (g + 2).exists():
                            maxima(g + 2, h)
                        if h == 3 and (g + -2).exists():
                            divide(g + -2)
                    if (g + 2).exists():
                        cut_maxima(g + 2)

                def around(i):
                    if i is not None:
                        own.loop(i, 16)
                    else:
                        own.end((NGR - 4) // 4)

                over_steps(dve, step, around)
                for b in range(B):
                    dve.wait_ge(y_full, b + 1)
                    x = m.XN[:, b * TB:(b + 1) * TB].rearrange("p t d -> p (t d)")
                    nc.vector.tensor_tensor(x, x, psS[:, b % 2], ALU.add).then_inc(y_done, 1)


def stage_list(nc, m, d, upto):
    w = m.w

    def share(E, split):
        return lambda i, U, u, q, t: m.comb[:, t, bass.ds(i * (U * split) + (u * split + q), 1)]

    attention(nc, m, dict(name="L0", dv=8, tiles=range(TB), mode="bias", gate=0, clear=["L0"],
                          wq=w["L0_xattn_Wq"][:], wk=w["L0_xattn_Wk"][:], wv=w["L0_xattn_Wv"][:],
                          wo=w["L0_xattn_Wo"][:].unsqueeze(1)))
    norm_transpose(nc, m, "L0n1", m.X1, m.XN, m.col("L0_xattn_g1"), m.col("L0_xattn_be1"))
    experts(nc, m, "L0h", dict(w1=d["L0_xattn_W1"].unsqueeze(0), w2=d["L0_xattn_W2"].unsqueeze(0), act=ACT.Gelu,
                               b1=d["L0_xattn_b1"].unsqueeze(0), b2=lambda i, U, u: m.row("L0_xattn_b2"),
                               dst=m.X1, share=lambda *a: m.ones[:, 0:1]))
    norm_transpose(nc, m, "L0n2", m.X1, m.XN, turn=False)
    add_layer(nc, m, "L0a", m.XN, 0, m.wide("L0_xattn_g2"), m.wide("L0_xattn_be2"))
    if upto == 0: return
    norm_transpose(nc, m, "L0r", m.X, m.XN, router=dict(E=8, kind="L0", w=w["L0_ffn_Wr"][:], gate=4, comb=m.comb[:, :, 0:8]))
    routed_experts(nc, m, "L0f", dict(w1=d["L0_ffn_W1"], w3=d["L0_ffn_W3"], w2=d["L0_ffn_W2"], act=ACT.Silu, rows=m.XN,
                                      U=4, chunks=[3, 2], key="L0"))
    if upto == 1: return
    attention(nc, m, dict(name="L1", dv=64, tiles=range(TB), mode="mask", gate=1, clear=["L2", "L3"],
                          wq=w["L1_xattn_W_Q"][:], wk=w["L1_xattn_W_K"][:], wv=w["L1_xattn_W_V"][:],
                          wo=w["L1_xattn_W_O"][:]))
    if upto == 2: return
    norm_transpose(nc, m, "L1r", m.X, m.XN, router=dict(E=16, kind="L1", w=w["L1_ffn_router_w"][:], gate=5, comb=m.comb[:]))
    experts(nc, m, "L1s", dict(w1=d["L1_ffn_sh_gate"], w3=d["L1_ffn_sh_up"], w2=d["L1_ffn_sh_down"], act=ACT.Silu,
                               dst=m.X, share=lambda *a: m.gate(5)))
    experts(nc, m, "L1f", dict(w1=d["L1_ffn_gate_proj"], w3=d["L1_ffn_up_proj"], w2=d["L1_ffn_down_proj"], act=ACT.Silu,
                               dst=m.X, share=share(16, 2), split=2))
    if upto == 3: return
    attention(nc, m, dict(name="L2", dv=8, tiles=[2, 3], mode="causal", gate=2, clear=[],
                          wq=w["L2_xattn_Wq"][:], wk=w["L2_xattn_Wk"][:], wv=w["L2_xattn_Wv"][:],
                          wo=w["L2_xattn_Wo"][:].unsqueeze(1)))
    if upto == 4: return
    norm_transpose(nc, m, "L2r", m.X, m.XN, router=dict(E=8, kind="L2", w=w["L2_ffn_Wr"][:], gate=6, comb=m.comb[:, :, 0:8]))
    routed_experts(nc, m, "L2f", dict(w1=d["L2_ffn_W1"], w2=d["L2_ffn_W2"], act=ACT.Silu, rows=m.XN,
                                      U=UL2, chunks=[BT], blocks=NBLOCKS, key="L2"))
    if upto == 5: return
    single_head(nc, m)
    if upto == 6: return
    norm_transpose(nc, m, "L3n0", m.X, m.XN, turn=False)
    norm_transpose(nc, m, "L3n1", m.XN, m.X1, m.col("L3_ffn_ln1_w"), m.col("L3_ffn_ln1_b"))
    self_attention(nc, m, d)
    norm_transpose(nc, m, "L3r", m.XN, m.X1, m.col("L3_ffn_ln2_w"), m.col("L3_ffn_ln2_b"),
                   router=dict(E=16, kind="L3", w=w["L3_ffn_router_w"][:], gate=7, comb=m.comb[:]))
    add_layer(nc, m, "L3a", m.XN, 7)
    routed_experts(nc, m, "L3f", dict(w1=d["L3_ffn_fc1_w"], w2=d["L3_ffn_fc2_w"], b1=d["L3_ffn_fc1_b"], b2=d["L3_ffn_fc2_b"],
                                      act=ACT.Gelu, rows=m.X1, scale=m.col("L3_ffn_ln2_w"), bias=m.col("L3_ffn_ln2_b"),
                                      U=8, chunks=[2], key="L3"))


def _t(a):
    return a.T


def _dh(a):
    return a.reshape(a.shape[:-1] + (H, D // H)).swapaxes(-1, -2).reshape(a.shape)


INPUTS = {
    "x": lambda a: a.reshape(NT, P, D),
    "ctx_1024": lambda a: a.transpose(2, 0, 1),
    "fside_Bx16xSxS2_0": lambda a: a,
    "mask_1x1xSxS2_ik0": lambda a: a.reshape(S, S2),
    "g_xattn": lambda a: a.reshape(1, 4),
    "g_ffn": lambda a: a.reshape(1, 4),
    "L0_xattn_Wq": lambda a: a, "L0_xattn_Wk": _t, "L0_xattn_Wv": _t, "L0_xattn_Wo": _t,
    "L0_xattn_W1": _t, "L0_xattn_b1": lambda a: a.reshape(4, P).T, "L0_xattn_W2": lambda a: a.T.reshape(4, P, D).transpose(1, 0, 2),
    "L0_ffn_Wr": lambda a: a, "L0_ffn_W1": lambda a: a, "L0_ffn_W3": lambda a: a,
    "L0_ffn_W2": lambda a: a.reshape(8, 4, P, D).transpose(0, 2, 1, 3),
    "L1_xattn_W_Q": lambda a: a.T.reshape(8, P, D).transpose(1, 0, 2), "L1_xattn_W_K": lambda a: a,
    "L1_xattn_W_V": lambda a: a, "L1_xattn_W_O": lambda a: a.reshape(8, P, D).transpose(1, 0, 2),
    "L1_ffn_router_w": _t,
    "L1_ffn_router_bias": lambda a: a.reshape(1, 16),
    "L1_ffn_up_proj": lambda a: a.reshape(8, 2, D, 64).transpose(0, 2, 1, 3).reshape(8, D, P),
    "L1_ffn_gate_proj": lambda a: a.reshape(8, 2, D, 64).transpose(0, 2, 1, 3).reshape(8, D, P),
    "L1_ffn_down_proj": lambda a: a.reshape(8, P, 1, D),
    "L1_ffn_sh_gate": lambda a: a.T.reshape(1, D, P), "L1_ffn_sh_up": lambda a: a.T.reshape(1, D, P),
    "L1_ffn_sh_down": lambda a: a.T.reshape(1, P, 1, D),
    "L2_xattn_Wq": _t, "L2_xattn_Wk": lambda a: a, "L2_xattn_Wv": lambda a: a, "L2_xattn_Wo": lambda a: a,
    "L2_ffn_Wr": _t, "L2_ffn_W1": lambda a: a, "L2_ffn_W2": lambda a: a.reshape(8, 4, P, D).transpose(0, 2, 1, 3),
    "L3_xattn_Wk": _t, "L3_xattn_Wv": _t, "L3_xattn_Wq": lambda a: a, "L3_xattn_Wo": _t,
    "L3_ffn_q_w": _dh, "L3_ffn_k_w": _dh, "L3_ffn_v_w": lambda a: a, "L3_ffn_o_w": lambda a: a,
    "L3_ffn_router_w": lambda a: a, "L3_ffn_fc1_w": lambda a: a,
    "L3_ffn_fc1_b": lambda a: a.reshape(16, 4, P).transpose(0, 2, 1),
    "L3_ffn_fc2_w": lambda a: a.reshape(16, 4, P, D).transpose(0, 2, 1, 3),
    "L3_ffn_fc2_b": lambda a: a.reshape(16, 1, D),
}
NFIRST = 4
KEPT = ["L0_xattn_Wk", "L0_xattn_Wv", "L0_xattn_Wq", "L0_xattn_Wo", 
        "L0_ffn_Wr", "L1_xattn_W_Q", "L1_xattn_W_K", "L1_xattn_W_V", "L1_xattn_W_O", "L1_ffn_router_w",
        "L2_xattn_Wq", "L2_xattn_Wk", "L2_xattn_Wv", "L2_xattn_Wo", "L2_ffn_Wr",
        "L3_xattn_Wk", "L3_xattn_Wv", "L3_xattn_Wq", "L3_xattn_Wo",
        "L3_ffn_q_w", "L3_ffn_k_w", "L3_ffn_v_w", "L3_ffn_o_w", "L3_ffn_router_w"]


def setup(nc, ctx, m, d):
    sb = lambda s, shape: ctx.enter_context(nc.sbuf_tensor(s, shape, F32))
    m.X, m.XN = sb("X", [P, NT, D]), sb("XN", [P, NT, D])
    m.pair = sb("X1_XT", [P, 2, NT, D])
    m.X1, m.XT = m.pair[:, 0], m.pair[:, 1]
    m.XT3 = m.XT
    m.XT = m.XT.rearrange("p t d -> p (t d)")
    const = sb("const", list(CONSTS.shape))
    m.const = {}
    for name, (at, w) in CONST.items():
        m.const[name] = const[:, at:at + w]
    m.ident, m.ones, m.first, m.rest = (m.const[k] for k in ("ident", "ones", "first", "rest"))
    m.head8, m.head64 = m.const["head8"], m.const["head64"]
    m.causal = [m.const["causal%d" % i] for i in range(TB)]
    rows, cols = sb("rows", [P, len(ROWS), D]), sb("cols", [P, len(COLS)])
    m.row = lambda s: rows[0:1, ROWS.index(s), :]
    m.wide = lambda s: rows[:, ROWS.index(s), :]
    m.col = lambda s: cols[:, COLS.index(s):COLS.index(s) + 1]
    gates = sb("gates", [P, 8])
    m.gate = lambda k: gates[:, k:k + 1]
    m.ctxT = sb("ctxT", [P, B, S2])
    m.comb = sb("comb", [P, NT, 16])
    m.slot_share = sb("slot_share", [P, 2, NT])
    m.slot_to = ctx.enter_context(nc.sbuf_tensor("slot_to", [P, 2, NT], I32))
    m.block_rows = ctx.enter_context(nc.sbuf_tensor("block_rows", [P, NBLOCKS], I32))
    m.slots = {k: nc.dram_tensor("slots" + k, (n, PAY), F32).ap()
               for k, n in (("L0", 8 * CAP0), ("L2", NBLOCKS * BLOCK), ("L3", 16 * CAP3))}
    m.results = {k: nc.dram_tensor("results" + k, (2 * NT * P, D), F32).ap() for k in m.slots}
    m.scattered = ctx.enter_context(nc.semaphore("scattered"))
    m.returned = [ctx.enter_context(nc.semaphore(f"returned{g}")) for g in range(2)]
    m.fetched = [ctx.enter_context(nc.semaphore(f"fetched{u}")) for u in range(UL2)]
    m.empty = sb("empty", [P, 1, PAY])
    m.zeroed = ctx.enter_context(nc.semaphore("zeroed"))
    m.empty_ready = ctx.enter_context(nc.semaphore("empty_ready"))
    m.w = {}
    for k in KEPT:
        shape = list(d[k].shape)
        m.w[k] = sb("w_" + k, shape)
    rb = sb("router_bias", [P, 16])
    m.router_bias = rb
    loaded, gates_in = ctx.enter_context(nc.semaphore("loaded")), ctx.enter_context(nc.semaphore("gates_in"))
    m.rest_loaded = ctx.enter_context(nc.semaphore("rest_loaded"))
    tanh_done = ctx.enter_context(nc.semaphore("tanh_done"))
    with nc.Block() as block:
        @block.sync
        def _(sp):
            clear_last(m, sp)
            n = 0
            for dst, src in [(const[:], d["consts"]), (cols[:], d["cols"]), (m.ctxT[:], d["ctx_1024"]),
                             (m.X[:], d["x"].rearrange("t p d -> p t d"))]:
                sp.dma_start(dst, src).then_inc(loaded, 16)
                n += 16
            sp.dma_start(rows[:], d["rows"].unsqueeze(0).broadcast_to([P, len(ROWS), D])).then_inc(loaded, 16)
            sp.dma_start(rb[:], d["L1_ffn_router_bias"].broadcast_to([P, 16])).then_inc(loaded, 16)
            n += 32
            for k in KEPT[:NFIRST]:
                sp.dma_start(m.w[k][:], d[k]).then_inc(loaded, 16)
                n += 16
            for k in KEPT[NFIRST:]:
                sp.dma_start(m.w[k][:], d[k]).then_inc(m.rest_loaded, 16)
            sp.wait_ge(loaded, n)

        @block.vector
        def _(dve):
            nc.vector.memset(m.empty[:, :, 0:D], 0.0).then_inc(m.empty_ready, 1)
            nc.vector.memset(m.empty[:, :, D:D + 1], NOWHERE).then_inc(m.empty_ready, 1)
            nc.vector.memset(m.empty[:, :, D + 1:PAY], 0.0).then_inc(m.empty_ready, 1)

        @block.scalar
        def _(act):
            act.dma_start(gates[:, 0:4], d["g_xattn"].broadcast_to([P, 4])).then_inc(gates_in, 16)
            act.dma_start(gates[:, 4:8], d["g_ffn"].broadcast_to([P, 4])).then_inc(gates_in, 16)
            act.wait_ge(gates_in, 32)
            nc.scalar.activation(gates[:], gates[:], ACT.Tanh).then_inc(tanh_done, 1)
            act.wait_ge(tanh_done, 1)


def program(nc, d, out, upto=99):
    m = Model()
    m.mask, m.bias = d["mask_1x1xSxS2_ik0"], d["fside_Bx16xSxS2_0"]
    with ExitStack() as ctx:
        setup(nc, ctx, m, d)
        stage_list(nc, m, d, upto)
        res = m.X
        stored = ctx.enter_context(nc.semaphore("stored"))
        with nc.Block() as block:
            @block.sync
            def _(sp):
                sp.dma_start(out.rearrange("t p d -> p t d"), res[:]).then_inc(stored, 16)
                sp.wait_ge(stored, 16)


def kernel(**inputs):
    import concourse.bacc as bacc
    from concourse.bass_utils import run_bass_kernel_spmd

    nc = bacc.Bacc("TRN2", target_bir_lowering=False, num_devices=1)
    arrays, d = {}, {}
    laid = {k: np.ascontiguousarray(f(np.asarray(inputs[k]))) for k, f in INPUTS.items()}
    laid["rows"] = np.stack([np.asarray(inputs[k]) for k in ROWS])
    laid["cols"] = np.ascontiguousarray(np.stack(
        [_dh(np.asarray(inputs[k])) if k in ("L3_ffn_q_b", "L3_ffn_k_b") else np.asarray(inputs[k]) for k in COLS], 1))
    laid["consts"] = CONSTS
    for k, a in laid.items():
        arrays["in_" + k] = a
        d[k] = nc.dram_tensor("in_" + k, a.shape, mybir.dt.from_np(a.dtype), kind="ExternalInput").ap()
    out = nc.dram_tensor("out", (NT, P, D), F32, kind="ExternalOutput").ap()
    program(nc, d, out)
    r = run_bass_kernel_spmd(nc, [arrays], core_ids=[0])
    return r.results[0]["out"].reshape(B, S, D)
```
